# Optimizing a Trainium2 kernel written in Bass

```python
import numpy as np
import jax
import jax.numpy as jnp

def _softmax(x, axis=-1):
    return jax.nn.softmax(x, axis=axis)
def _gelu(x):
    return jax.nn.gelu(x, approximate=True)
def _silu(x):
    return jax.nn.silu(x)
def _sigmoid(x):
    return jax.nn.sigmoid(x)
def _layernorm(x, axis=-1, eps=1e-5):
    m = jnp.mean(x, axis=axis, keepdims=True)
    v = jnp.var(x, axis=axis, keepdims=True)
    return (x - m) / jnp.sqrt(v + eps)
def _scatter_add(tgt, idx, src, axis=0):
    return tgt.at[idx].add(src)
def _segment_sum(src, seg, n):
    return jax.ops.segment_sum(src, seg, n)

kernel_name = 'mk_conv_preact_d2_conv_nchw192_665ca9'

def setup_inputs(seed: int = 0):
    np.random.seed(seed)
    _w = jnp.asarray
    def _rec_inputs():
        import jax
        import jax.numpy as jnp
        _gk = jax.random.key(seed)
        x = -0.0005963 + 1.001 * jax.random.normal(jax.random.fold_in(_gk, 1), (16, 192, 32, 32), jnp.float32)
        return x
    x = _rec_inputs()
    def _L0_conv_setup():
        import jax, jax.numpy as jnp
        import numpy as np
        from functools import partial
        B, C, H, W = (16, 192, 32, 32)
        INNER, NH, DH, DCONV = (384, 12, 32, 4)
        S = H * W

        def _layernorm(h, w, b, eps=1e-05):
            mu = h.mean(-1, keepdims=True)
            var = h.var(-1, keepdims=True)
            return (h - mu) / jnp.sqrt(var + eps) * w + b

        def _mlstm_scan(q, k, v, i_pre, f_pre):
            qs, ks_, vs = (a.transpose(1, 0, 2, 3) for a in (q, k, v))
            iseq, fseq = (i_pre.transpose(1, 0, 2), f_pre.transpose(1, 0, 2))

            def step(carry, inp):
                Cst, nst, mst = carry
                qt, kt, vt, it, ft = inp
                log_f = jax.nn.log_sigmoid(ft)
                m_new = jnp.maximum(log_f + mst, it)
                f_s = jnp.exp(log_f + mst - m_new)[..., None]
                i_s = jnp.exp(it - m_new)[..., None]
                C_new = f_s[..., None] * Cst + i_s[..., None] * (vt[..., :, None] * kt[..., None, :])
                n_new = f_s * nst + i_s * kt
                denom = jnp.maximum(jnp.abs(jnp.einsum('bhd,bhd->bh', n_new, qt)), 1.0)[..., None]
                h = jnp.einsum('bhde,bhe->bhd', C_new, qt) / denom
                return ((C_new, n_new, m_new), h)
            bsz = q.shape[0]
            carry0 = (jnp.zeros((bsz, NH, DH, DH), q.dtype), jnp.zeros((bsz, NH, DH), q.dtype), jnp.zeros((bsz, NH), q.dtype))
            _, hs = jax.lax.scan(step, carry0, (qs, ks_, vs, iseq, fseq))
            return hs.transpose(1, 0, 2, 3)

        def _vil_block(seq, ln_w, ln_b, w_up, b_up, conv_k, conv_b, w_q, w_k, w_i, b_i, w_f, b_f, skip, mh_w, mh_b, w_down, b_down):
            bsz, s = (seq.shape[0], seq.shape[1])
            h = _layernorm(seq, ln_w, ln_b)
            x_in, z = jnp.split(h @ w_up + b_up, 2, axis=-1)
            x_pad = jnp.pad(x_in, ((0, 0), (DCONV - 1, 0), (0, 0)))
            x_conv = sum((x_pad[:, t:t + s, :] * conv_k[:, t] for t in range(DCONV))) + conv_b
            x_act = jax.nn.silu(x_conv)
            q = x_act @ w_q
            k = x_act @ w_k
            v = x_in
            gin = jnp.concatenate([q, k, v], -1)
            i_pre = gin @ w_i + b_i
            f_pre = gin @ w_f + b_f
            qh = q.reshape(bsz, s, NH, DH)
            kh = k.reshape(bsz, s, NH, DH) * DH ** (-0.5)
            vh = v.reshape(bsz, s, NH, DH)
            hs = _mlstm_scan(qh, kh, vh, i_pre, f_pre)
            mu = hs.mean(-1, keepdims=True)
            var = hs.var(-1, keepdims=True)
            hn = ((hs - mu) / jnp.sqrt(var + 1e-05)).reshape(bsz, s, INNER) * mh_w + mh_b
            h_out = (hn + skip * x_act) * jax.nn.silu(z)
            return seq + (h_out @ w_down + b_down)
        key = jax.random.key(seed)
        ks = jax.random.split(key, 12)

        def n(k, shape, s=0.02):
            return jax.random.normal(k, shape, jnp.float32) * s
        f32 = jnp.float32
        return {'x': jax.random.normal(ks[0], (B, C, H, W), f32), 'ln_w': jnp.ones((C,), f32), 'ln_b': jnp.zeros((C,), f32), 'w_up': n(ks[1], (C, 2 * INNER)), 'b_up': jnp.zeros((2 * INNER,), f32), 'conv_k': n(ks[2], (INNER, DCONV), 0.1), 'conv_b': jnp.zeros((INNER,), f32), 'w_q': n(ks[3], (INNER, INNER)), 'w_k': n(ks[4], (INNER, INNER)), 'w_i': n(ks[5], (3 * INNER, NH)), 'b_i': jnp.zeros((NH,), f32), 'w_f': n(ks[6], (3 * INNER, NH)), 'b_f': 3.0 * jnp.ones((NH,), f32), 'skip': jnp.ones((INNER,), f32), 'mh_w': jnp.ones((INNER,), f32), 'mh_b': jnp.zeros((INNER,), f32), 'w_down': n(ks[7], (INNER, C)), 'b_down': jnp.zeros((C,), f32), 'w_lin': n(ks[8], (C, C)), 'b_lin': jnp.zeros((C,), f32), 'conv2_w': n(ks[9], (C, C, 3, 3), 0.05), 'conv2_b': jnp.zeros((C,), f32), 'bn_g': jnp.ones((C,), f32), 'bn_b': jnp.zeros((C,), f32)}
    _L0_conv_all = _L0_conv_setup()
    _L0_conv_in = {k: v for k, v in _L0_conv_all.items() if k in ('ln_w', 'ln_b', 'w_up', 'b_up', 'conv_k', 'conv_b', 'w_q', 'w_k', 'w_i', 'b_i', 'w_f', 'b_f', 'skip', 'mh_w', 'mh_b', 'w_down', 'b_down', 'w_lin', 'b_lin', 'conv2_w', 'conv2_b', 'bn_g', 'bn_b', )}
    del _L0_conv_all

    def _L1_conv_setup():
        import jax, jax.numpy as jnp
        import numpy as np
        D_MODEL = 192
        D_STATE = 64
        D_CONV = 4
        EXPAND = 2
        HEADDIM = 64
        CHUNK = 256
        D_INNER = EXPAND * D_MODEL
        NHEADS = D_INNER // HEADDIM
        CONV_DIM = D_INNER + 2 * D_STATE
        D_IN_PROJ = 2 * D_INNER + 2 * D_STATE + NHEADS

        def _layernorm(x, w, b, eps=1e-05):
            mu = jnp.mean(x, -1, keepdims=True)
            var = jnp.mean((x - mu) ** 2, -1, keepdims=True)
            return (x - mu) * jax.lax.rsqrt(var + eps) * w + b

        def _segsum(a):
            T = a.shape[-1]
            cs = jnp.cumsum(a, -1)
            d = cs[..., :, None] - cs[..., None, :]
            mask = jnp.tril(jnp.ones((T, T), bool))
            return jnp.where(mask, d, -jnp.inf)

        def _ssd(x, A, Bm, Cm):
            b, l, h, p = x.shape
            c = l // CHUNK
            x = x.reshape(b, c, CHUNK, h, p)
            A = A.reshape(b, c, CHUNK, h).transpose(0, 3, 1, 2)
            Bm = Bm.reshape(b, c, CHUNK, h, D_STATE)
            Cm = Cm.reshape(b, c, CHUNK, h, D_STATE)
            A_cs = jnp.cumsum(A, -1)
            L = jnp.exp(_segsum(A))
            Y_diag = jnp.einsum('bclhn,bcshn,bhcls,bcshp->bclhp', Cm, Bm, L, x)
            decay_states = jnp.exp(A_cs[..., -1:] - A_cs)
            states = jnp.einsum('bclhn,bhcl,bclhp->bchpn', Bm, decay_states, x)
            A_last = jnp.pad(A_cs[..., -1], ((0, 0), (0, 0), (1, 0)))
            decay_chunk = jnp.exp(_segsum(A_last))
            states = jnp.concatenate([jnp.zeros_like(states[:, :1]), states], axis=1)
            new_states = jnp.einsum('bhzc,bchpn->bzhpn', decay_chunk, states)
            states = new_states[:, :-1]
            Y_off = jnp.einsum('bclhn,bchpn,bhcl->bclhp', Cm, states, jnp.exp(A_cs))
            return (Y_diag + Y_off).reshape(b, l, h, p)

        def _mamba2(u, in_proj_w, conv_w, conv_b, dt_bias, A_log, D_skip, ssm_norm_w, out_proj_w):
            b, l, _ = u.shape
            zxbcdt = u @ in_proj_w.T
            z = zxbcdt[..., :D_INNER]
            xBC = zxbcdt[..., D_INNER:D_INNER + CONV_DIM]
            dt = jax.nn.softplus(zxbcdt[..., -NHEADS:] + dt_bias)
            xBC_t = jax.lax.conv_general_dilated(xBC.transpose(0, 2, 1), conv_w[:, None, :], (1,), [(D_CONV - 1, 0)], feature_group_count=CONV_DIM, dimension_numbers=('NCH', 'OIH', 'NCH'))
            xBC = jax.nn.silu(xBC_t.transpose(0, 2, 1) + conv_b)
            xs = xBC[..., :D_INNER].reshape(b, l, NHEADS, HEADDIM)
            Bm = jnp.broadcast_to(xBC[..., D_INNER:D_INNER + D_STATE][:, :, None, :], (b, l, NHEADS, D_STATE))
            Cm = jnp.broadcast_to(xBC[..., D_INNER + D_STATE:][:, :, None, :], (b, l, NHEADS, D_STATE))
            A = -jnp.exp(A_log)
            y = _ssd(xs * dt[..., None], dt * A, Bm, Cm)
            y = y + xs * D_skip[None, None, :, None]
            y = y.reshape(b, l, D_INNER)
            g = y * jax.nn.silu(z)
            g = g * jax.lax.rsqrt(jnp.mean(g * g, -1, keepdims=True) + 1e-05) * ssm_norm_w
            return g @ out_proj_w.T
        key = jax.random.key(seed)
        ks = jax.random.split(key, 10)
        B, H, W = (8, 64, 64)
        rn = lambda k, s, sc: jax.random.normal(k, s, jnp.float32) * sc
        return {'x': rn(ks[0], (B, D_MODEL, H, W), 1.0), 'norm1_w': jnp.ones((D_MODEL,), jnp.float32), 'norm1_b': jnp.zeros((D_MODEL,), jnp.float32), 'in_proj_w': rn(ks[1], (D_IN_PROJ, D_MODEL), D_MODEL ** (-0.5)), 'conv_w': rn(ks[2], (CONV_DIM, D_CONV), D_CONV ** (-0.5)), 'conv_b': jnp.zeros((CONV_DIM,), jnp.float32), 'dt_bias': jnp.log(jnp.expm1(jax.random.uniform(ks[3], (NHEADS,), jnp.float32, 0.001, 0.1))), 'A_log': jnp.log(jax.random.uniform(ks[4], (NHEADS,), jnp.float32, 1.0, 16.0)), 'D_skip': jnp.ones((NHEADS,), jnp.float32), 'ssm_norm_w': jnp.ones((D_INNER,), jnp.float32), 'out_proj_w': rn(ks[5], (D_MODEL, D_INNER), D_INNER ** (-0.5)), 'norm2_w': jnp.ones((D_MODEL,), jnp.float32), 'norm2_b': jnp.zeros((D_MODEL,), jnp.float32), 'ffn_w1': rn(ks[6], (2 * D_MODEL, D_MODEL), D_MODEL ** (-0.5)), 'ffn_b1': jnp.zeros((2 * D_MODEL,), jnp.float32), 'ffn_w2': rn(ks[7], (D_MODEL, 2 * D_MODEL), (2 * D_MODEL) ** (-0.5)), 'ffn_b2': jnp.zeros((D_MODEL,), jnp.float32)}
    _L1_conv_all = _L1_conv_setup()
    _L1_conv_in = {k: v for k, v in _L1_conv_all.items() if k in ('norm1_w', 'norm1_b', 'in_proj_w', 'conv_w', 'conv_b', 'dt_bias', 'A_log', 'D_skip', 'ssm_norm_w', 'out_proj_w', 'norm2_w', 'norm2_b', 'ffn_w1', 'ffn_b1', 'ffn_w2', 'ffn_b2', )}
    del _L1_conv_all

    return {
        "x": x,
        "L0_conv_ln_w": _L0_conv_in["ln_w"],
        "L0_conv_ln_b": _L0_conv_in["ln_b"],
        "L0_conv_w_up": _L0_conv_in["w_up"],
        "L0_conv_b_up": _L0_conv_in["b_up"],
        "L0_conv_conv_k": _L0_conv_in["conv_k"],
        "L0_conv_conv_b": _L0_conv_in["conv_b"],
        "L0_conv_w_q": _L0_conv_in["w_q"],
        "L0_conv_w_k": _L0_conv_in["w_k"],
        "L0_conv_w_i": _L0_conv_in["w_i"],
        "L0_conv_b_i": _L0_conv_in["b_i"],
        "L0_conv_w_f": _L0_conv_in["w_f"],
        "L0_conv_b_f": _L0_conv_in["b_f"],
        "L0_conv_skip": _L0_conv_in["skip"],
        "L0_conv_mh_w": _L0_conv_in["mh_w"],
        "L0_conv_mh_b": _L0_conv_in["mh_b"],
        "L0_conv_w_down": _L0_conv_in["w_down"],
        "L0_conv_b_down": _L0_conv_in["b_down"],
        "L0_conv_w_lin": _L0_conv_in["w_lin"],
        "L0_conv_b_lin": _L0_conv_in["b_lin"],
        "L0_conv_conv2_w": _L0_conv_in["conv2_w"],
        "L0_conv_conv2_b": _L0_conv_in["conv2_b"],
        "L0_conv_bn_g": _L0_conv_in["bn_g"],
        "L0_conv_bn_b": _L0_conv_in["bn_b"],
        "L1_conv_norm1_w": _L1_conv_in["norm1_w"],
        "L1_conv_norm1_b": _L1_conv_in["norm1_b"],
        "L1_conv_in_proj_w": _L1_conv_in["in_proj_w"],
        "L1_conv_conv_w": _L1_conv_in["conv_w"],
        "L1_conv_conv_b": _L1_conv_in["conv_b"],
        "L1_conv_dt_bias": _L1_conv_in["dt_bias"],
        "L1_conv_A_log": _L1_conv_in["A_log"],
        "L1_conv_D_skip": _L1_conv_in["D_skip"],
        "L1_conv_ssm_norm_w": _L1_conv_in["ssm_norm_w"],
        "L1_conv_out_proj_w": _L1_conv_in["out_proj_w"],
        "L1_conv_norm2_w": _L1_conv_in["norm2_w"],
        "L1_conv_norm2_b": _L1_conv_in["norm2_b"],
        "L1_conv_ffn_w1": _L1_conv_in["ffn_w1"],
        "L1_conv_ffn_b1": _L1_conv_in["ffn_b1"],
        "L1_conv_ffn_w2": _L1_conv_in["ffn_w2"],
        "L1_conv_ffn_b2": _L1_conv_in["ffn_b2"],
    }

def reference(x, L0_conv_ln_w, L0_conv_ln_b, L0_conv_w_up, L0_conv_b_up, L0_conv_conv_k, L0_conv_conv_b, L0_conv_w_q, L0_conv_w_k, L0_conv_w_i, L0_conv_b_i, L0_conv_w_f, L0_conv_b_f, L0_conv_skip, L0_conv_mh_w, L0_conv_mh_b, L0_conv_w_down, L0_conv_b_down, L0_conv_w_lin, L0_conv_b_lin, L0_conv_conv2_w, L0_conv_conv2_b, L0_conv_bn_g, L0_conv_bn_b, L1_conv_norm1_w, L1_conv_norm1_b, L1_conv_in_proj_w, L1_conv_conv_w, L1_conv_conv_b, L1_conv_dt_bias, L1_conv_A_log, L1_conv_D_skip, L1_conv_ssm_norm_w, L1_conv_out_proj_w, L1_conv_norm2_w, L1_conv_norm2_b, L1_conv_ffn_w1, L1_conv_ffn_b1, L1_conv_ffn_w2, L1_conv_ffn_b2):
    import jax
    import jax.numpy as jnp
    def _L0_conv_ref(x, ln_w, ln_b, w_up, b_up, conv_k, conv_b, w_q, w_k, w_i, b_i, w_f, b_f, skip, mh_w, mh_b, w_down, b_down, w_lin, b_lin, conv2_w, conv2_b, bn_g, bn_b):
        import jax, jax.numpy as jnp
        import numpy as np
        from functools import partial
        B, C, H, W = (16, 192, 32, 32)
        INNER, NH, DH, DCONV = (384, 12, 32, 4)
        S = H * W

        def _layernorm(h, w, b, eps=1e-05):
            mu = h.mean(-1, keepdims=True)
            var = h.var(-1, keepdims=True)
            return (h - mu) / jnp.sqrt(var + eps) * w + b

        def _mlstm_scan(q, k, v, i_pre, f_pre):
            qs, ks_, vs = (a.transpose(1, 0, 2, 3) for a in (q, k, v))
            iseq, fseq = (i_pre.transpose(1, 0, 2), f_pre.transpose(1, 0, 2))

            def step(carry, inp):
                Cst, nst, mst = carry
                qt, kt, vt, it, ft = inp
                log_f = jax.nn.log_sigmoid(ft)
                m_new = jnp.maximum(log_f + mst, it)
                f_s = jnp.exp(log_f + mst - m_new)[..., None]
                i_s = jnp.exp(it - m_new)[..., None]
                C_new = f_s[..., None] * Cst + i_s[..., None] * (vt[..., :, None] * kt[..., None, :])
                n_new = f_s * nst + i_s * kt
                denom = jnp.maximum(jnp.abs(jnp.einsum('bhd,bhd->bh', n_new, qt)), 1.0)[..., None]
                h = jnp.einsum('bhde,bhe->bhd', C_new, qt) / denom
                return ((C_new, n_new, m_new), h)
            bsz = q.shape[0]
            carry0 = (jnp.zeros((bsz, NH, DH, DH), q.dtype), jnp.zeros((bsz, NH, DH), q.dtype), jnp.zeros((bsz, NH), q.dtype))
            _, hs = jax.lax.scan(step, carry0, (qs, ks_, vs, iseq, fseq))
            return hs.transpose(1, 0, 2, 3)

        def _vil_block(seq, ln_w, ln_b, w_up, b_up, conv_k, conv_b, w_q, w_k, w_i, b_i, w_f, b_f, skip, mh_w, mh_b, w_down, b_down):
            bsz, s = (seq.shape[0], seq.shape[1])
            h = _layernorm(seq, ln_w, ln_b)
            x_in, z = jnp.split(h @ w_up + b_up, 2, axis=-1)
            x_pad = jnp.pad(x_in, ((0, 0), (DCONV - 1, 0), (0, 0)))
            x_conv = sum((x_pad[:, t:t + s, :] * conv_k[:, t] for t in range(DCONV))) + conv_b
            x_act = jax.nn.silu(x_conv)
            q = x_act @ w_q
            k = x_act @ w_k
            v = x_in
            gin = jnp.concatenate([q, k, v], -1)
            i_pre = gin @ w_i + b_i
            f_pre = gin @ w_f + b_f
            qh = q.reshape(bsz, s, NH, DH)
            kh = k.reshape(bsz, s, NH, DH) * DH ** (-0.5)
            vh = v.reshape(bsz, s, NH, DH)
            hs = _mlstm_scan(qh, kh, vh, i_pre, f_pre)
            mu = hs.mean(-1, keepdims=True)
            var = hs.var(-1, keepdims=True)
            hn = ((hs - mu) / jnp.sqrt(var + 1e-05)).reshape(bsz, s, INNER) * mh_w + mh_b
            h_out = (hn + skip * x_act) * jax.nn.silu(z)
            return seq + (h_out @ w_down + b_down)
        bsz, c, hh, ww = x.shape
        seq = x.reshape(bsz, c, hh * ww).transpose(0, 2, 1)
        x1 = _vil_block(seq, ln_w, ln_b, w_up, b_up, conv_k, conv_b, w_q, w_k, w_i, b_i, w_f, b_f, skip, mh_w, mh_b, w_down, b_down)
        x1 = x1.transpose(0, 2, 1).reshape(bsz, c, hh, ww)
        x2 = jax.nn.silu(seq @ w_lin + b_lin).transpose(0, 2, 1).reshape(bsz, c, hh, ww)
        y = x1 + x2
        y = jax.lax.conv_general_dilated(y, conv2_w, (1, 1), ((1, 1), (1, 1)), dimension_numbers=('NCHW', 'OIHW', 'NCHW'))
        y = y + conv2_b[None, :, None, None]
        mu = y.mean((0, 2, 3), keepdims=True)
        var = y.var((0, 2, 3), keepdims=True)
        y = (y - mu) / jnp.sqrt(var + 1e-05) * bn_g[None, :, None, None] + bn_b[None, :, None, None]
        return jnp.where(y >= 0, y, 0.01 * y)

    def _L1_conv_ref(x, norm1_w, norm1_b, in_proj_w, conv_w, conv_b, dt_bias, A_log, D_skip, ssm_norm_w, out_proj_w, norm2_w, norm2_b, ffn_w1, ffn_b1, ffn_w2, ffn_b2):
        import jax, jax.numpy as jnp
        import numpy as np
        D_MODEL = 192
        D_STATE = 64
        D_CONV = 4
        EXPAND = 2
        HEADDIM = 64
        CHUNK = 256
        D_INNER = EXPAND * D_MODEL
        NHEADS = D_INNER // HEADDIM
        CONV_DIM = D_INNER + 2 * D_STATE
        D_IN_PROJ = 2 * D_INNER + 2 * D_STATE + NHEADS

        def _layernorm(x, w, b, eps=1e-05):
            mu = jnp.mean(x, -1, keepdims=True)
            var = jnp.mean((x - mu) ** 2, -1, keepdims=True)
            return (x - mu) * jax.lax.rsqrt(var + eps) * w + b

        def _segsum(a):
            T = a.shape[-1]
            cs = jnp.cumsum(a, -1)
            d = cs[..., :, None] - cs[..., None, :]
            mask = jnp.tril(jnp.ones((T, T), bool))
            return jnp.where(mask, d, -jnp.inf)

        def _ssd(x, A, Bm, Cm):
            b, l, h, p = x.shape
            c = l // CHUNK
            x = x.reshape(b, c, CHUNK, h, p)
            A = A.reshape(b, c, CHUNK, h).transpose(0, 3, 1, 2)
            Bm = Bm.reshape(b, c, CHUNK, h, D_STATE)
            Cm = Cm.reshape(b, c, CHUNK, h, D_STATE)
            A_cs = jnp.cumsum(A, -1)
            L = jnp.exp(_segsum(A))
            Y_diag = jnp.einsum('bclhn,bcshn,bhcls,bcshp->bclhp', Cm, Bm, L, x)
            decay_states = jnp.exp(A_cs[..., -1:] - A_cs)
            states = jnp.einsum('bclhn,bhcl,bclhp->bchpn', Bm, decay_states, x)
            A_last = jnp.pad(A_cs[..., -1], ((0, 0), (0, 0), (1, 0)))
            decay_chunk = jnp.exp(_segsum(A_last))
            states = jnp.concatenate([jnp.zeros_like(states[:, :1]), states], axis=1)
            new_states = jnp.einsum('bhzc,bchpn->bzhpn', decay_chunk, states)
            states = new_states[:, :-1]
            Y_off = jnp.einsum('bclhn,bchpn,bhcl->bclhp', Cm, states, jnp.exp(A_cs))
            return (Y_diag + Y_off).reshape(b, l, h, p)

        def _mamba2(u, in_proj_w, conv_w, conv_b, dt_bias, A_log, D_skip, ssm_norm_w, out_proj_w):
            b, l, _ = u.shape
            zxbcdt = u @ in_proj_w.T
            z = zxbcdt[..., :D_INNER]
            xBC = zxbcdt[..., D_INNER:D_INNER + CONV_DIM]
            dt = jax.nn.softplus(zxbcdt[..., -NHEADS:] + dt_bias)
            xBC_t = jax.lax.conv_general_dilated(xBC.transpose(0, 2, 1), conv_w[:, None, :], (1,), [(D_CONV - 1, 0)], feature_group_count=CONV_DIM, dimension_numbers=('NCH', 'OIH', 'NCH'))
            xBC = jax.nn.silu(xBC_t.transpose(0, 2, 1) + conv_b)
            xs = xBC[..., :D_INNER].reshape(b, l, NHEADS, HEADDIM)
            Bm = jnp.broadcast_to(xBC[..., D_INNER:D_INNER + D_STATE][:, :, None, :], (b, l, NHEADS, D_STATE))
            Cm = jnp.broadcast_to(xBC[..., D_INNER + D_STATE:][:, :, None, :], (b, l, NHEADS, D_STATE))
            A = -jnp.exp(A_log)
            y = _ssd(xs * dt[..., None], dt * A, Bm, Cm)
            y = y + xs * D_skip[None, None, :, None]
            y = y.reshape(b, l, D_INNER)
            g = y * jax.nn.silu(z)
            g = g * jax.lax.rsqrt(jnp.mean(g * g, -1, keepdims=True) + 1e-05) * ssm_norm_w
            return g @ out_proj_w.T
        B, C, H, W = x.shape
        x_flat = x.transpose(0, 2, 3, 1).reshape(B, H * W, C)
        h1 = _layernorm(x_flat, norm1_w, norm1_b)
        u = h1.reshape(B, C, H, W).reshape(B, C, H * W).transpose(0, 2, 1)
        m = _mamba2(u, in_proj_w, conv_w, conv_b, dt_bias, A_log, D_skip, ssm_norm_w, out_proj_w)
        m_flat = m.transpose(0, 2, 1).reshape(B, C, H, W).transpose(0, 2, 3, 1).reshape(B, H * W, C)
        x_flat = x_flat + m_flat
        h2 = _layernorm(x_flat, norm2_w, norm2_b)
        f = jax.nn.gelu(h2 @ ffn_w1.T + ffn_b1, approximate=False) @ ffn_w2.T + ffn_b2
        x_flat = x_flat + f
        return x_flat.reshape(B, H, W, C).transpose(0, 3, 1, 2)

    def _gn(v, G=32, eps=1e-5):
        B_, C_, H_, W_ = v.shape
        g = v.reshape(B_, G, C_ // G, H_, W_)
        m = jnp.mean(g, axis=(2, 3, 4), keepdims=True)
        s = jnp.var(g, axis=(2, 3, 4), keepdims=True)
        return ((g - m) / jnp.sqrt(s + eps)).reshape(v.shape)

    def _ln_c(v, eps=1e-6):
        m = jnp.mean(v, axis=1, keepdims=True)
        s = jnp.var(v, axis=1, keepdims=True)
        return (v - m) / jnp.sqrt(s + eps)

    def _ln_t(v, eps=1e-5):
        m = jnp.mean(v, axis=-1, keepdims=True)
        s = jnp.var(v, axis=-1, keepdims=True)
        return (v - m) / jnp.sqrt(s + eps)

    def _to_tokens(v):
        B_, C_, H_, W_ = v.shape
        return v.reshape(B_, C_, H_ * W_).transpose(0, 2, 1)
    def _from_tokens(t, like):
        B_, C_, H_, W_ = like.shape
        return t.transpose(0, 2, 1).reshape(B_, C_, H_, W_)

    x = x + _L0_conv_ref(_gn(x), L0_conv_ln_w, L0_conv_ln_b, L0_conv_w_up, L0_conv_b_up, L0_conv_conv_k, L0_conv_conv_b, L0_conv_w_q, L0_conv_w_k, L0_conv_w_i, L0_conv_b_i, L0_conv_w_f, L0_conv_b_f, L0_conv_skip, L0_conv_mh_w, L0_conv_mh_b, L0_conv_w_down, L0_conv_b_down, L0_conv_w_lin, L0_conv_b_lin, L0_conv_conv2_w, L0_conv_conv2_b, L0_conv_bn_g, L0_conv_bn_b)
    x = x + _L1_conv_ref(_gn(x), L1_conv_norm1_w, L1_conv_norm1_b, L1_conv_in_proj_w, L1_conv_conv_w, L1_conv_conv_b, L1_conv_dt_bias, L1_conv_A_log, L1_conv_D_skip, L1_conv_ssm_norm_w, L1_conv_out_proj_w, L1_conv_norm2_w, L1_conv_norm2_b, L1_conv_ffn_w1, L1_conv_ffn_b1, L1_conv_ffn_w2, L1_conv_ffn_b2)
    return x


_drawn_inputs = setup_inputs


def setup_inputs(seed=0):
    import zlib

    import numpy as np

    out = dict(_drawn_inputs(seed))
    spreads = {'L0_conv_ln_w': (1.0, 0.6),
     'L0_conv_ln_b': (0.0, 0.8),
     'L0_conv_b_up': (0.0, 0.485),
     'L0_conv_conv_b': (0.0, 0.439),
     'L0_conv_b_i': (0.0, 2.0),
     'L0_conv_b_f': (3.0, 0.6),
     'L0_conv_skip': (1.0, 0.6),
     'L0_conv_mh_w': (1.0, 0.6),
     'L0_conv_mh_b': (0.0, 0.8),
     'L0_conv_b_down': (0.0, 1.735),
     'L0_conv_b_lin': (0.0, 2.0),
     'L0_conv_conv2_b': (0.0, 2.0),
     'L0_conv_bn_g': (1.0, 0.2),
     'L0_conv_bn_b': (0.0, 0.1),
     'L1_conv_norm1_w': (1.0, 0.2),
     'L1_conv_norm1_b': (0.0, 0.1),
     'L1_conv_conv_b': (0.0, 0.1),
     'L1_conv_D_skip': (1.0, 0.2),
     'L1_conv_ssm_norm_w': (1.0, 0.2),
     'L1_conv_norm2_w': (1.0, 0.2),
     'L1_conv_norm2_b': (0.0, 0.278),
     'L1_conv_ffn_b1': (0.0, 0.296),
     'L1_conv_ffn_b2': (0.0, 0.1)}
    factors = {'L0_conv_w_up': 3.018,
     'L0_conv_conv_k': 5.571,
     'L0_conv_w_q': 3.326,
     'L0_conv_w_k': 4.23,
     'L0_conv_w_i': 8.0,
     'L0_conv_w_f': 8.0,
     'L0_conv_w_down': 2.965}
    for name, (base, spread) in spreads.items():
        noise = np.random.default_rng([zlib.crc32(name.encode()), seed]).standard_normal(out[name].shape)
        drawn = base * np.exp(spread * noise) if base else spread * noise
        out[name] = jnp.asarray(drawn.astype(out[name].dtype))
    for name, factor in factors.items():
        out[name] = (out[name] * factor).astype(out[name].dtype)
    return out
```

```python
from contextlib import ExitStack

import concourse.bass as bass
from concourse import mybir

F32 = mybir.dt.float32
BF16 = mybir.dt.bfloat16
ALU = mybir.AluOpType
ACT = mybir.ActivationFunctionType
AX = mybir.AxisListType.X

B, C, HW = 16, 192, 32
T = HW * HW
CH = C // 2
INNER = 2 * C
G3 = INNER // 128
NT = T // 512
L = 128
NCH = T // L
TAPS = 4
PAD = TAPS - 1
GN_EPS = 1e-5

NH0, DH0 = 12, 32
V0 = DH0 + 1
HG = 128 // DH0

NH1, DH1, NS = 6, 64, 64
HB = NH1 // 2

COL96 = ["ln_w", "ln_b", "b_lin", "b_down", "conv2_b", "bn_g", "bn_b",
         "norm1_w", "norm1_b", "norm2_w", "norm2_b", "ffn_b2"]
COL128 = {"b_up": 6, "conv_k": 12, "conv_b": 3, "skip": 3, "mh_w": 3, "mh_b": 3,
          "m_conv_w": 16, "m_conv_b": 4, "ssm_w": 3, "ffn_b1": 3, "D": 6}
ROWS = ["b_i", "b_f", "dt_bias", "A_log"]
CONSTS = {"ident": 128, "causal": 128, "block": 4 * V0, "group": CH, "mean": CH, "expand": 3 * 128,
          "pick1": 3 * NH1, "reset": T}
SELECT = {"a_sel0": 3 * 512, "b_sel0": NH0 * 128, "a_sel1": NH1 * L, "b_sel1": NH1 * 128}


def offsets(widths):
    at, out = 0, {}
    for name, w in widths.items():
        out[name] = (at, at + w)
        at += w
    return out, at


AT96, W96 = offsets({n: 2 for n in COL96})
AT128, W128 = offsets(COL128)
ATC, WC = offsets(CONSTS)
ATS, WS = offsets(SELECT)


class Signal:

    def __init__(self, sem, per_image, unit=1):
        self.sem, self.per_image, self.unit = sem, per_image, unit

    def at(self, image, count):
        return (image * self.per_image + count) * self.unit


def later(image):
    return not (isinstance(image, int) and image == 0)


class Own:

    def __init__(self, sem):
        self.sem, self.count, self.per_image, self.image, self.before = sem, 0, 0, 0, 0

    def start(self, image):
        if isinstance(image, int) and image == 0:
            self.before = self.count
            self.count = 0
            return
        assert self.per_image in (0, self.count)
        self.per_image = self.count
        self.image, self.count = image, 0

    def step(self):
        self.count += 1
        return 1

    def value(self):
        return self.before + self.image * self.per_image + self.count


def over_images(eng, own, body, after=None):
    for i in range(2):
        if own:
            own.start(i)
        body(i)
    with eng.Fori(2, B) as i:
        if own:
            own.start(i)
        body(i)
    if after:
        if own:
            own.start(B)
        after(B)


def layer0(nc, ctx, d, shared):
    def sb(name, shape, dt=F32):
        return ctx.enter_context(nc.sbuf_tensor(name, shape, dt))

    def signal(name, per_image, unit=1):
        return Signal(ctx.enter_context(nc.semaphore(name)), per_image, unit)

    bank = shared["bank"]
    w96, w128, rows, cst, eps = (shared[k] for k in ("w96", "w128", "rows", "cst", "eps"))
    bn = shared["bn"]
    setup_loaded = signal("setup_loaded", 0, 16)
    setup_done = shared["setup_done"]
    fold_mm = signal("fold_mm", 0)

    Wup = sb("Wup", [CH, 2, 2 * INNER])
    Wq = sb("Wq", [128, G3, INNER])
    Wk = sb("Wk", [128, G3, INNER])
    Wg = sb("Wg", [128, 3 * G3, 44])
    Wdown = sb("Wdown", [128, G3, C])
    Wlin = sb("Wlin", [CH, 2, C])
    Wc3 = sb("Wc3", [CH, 2, 9, C])
    X = sb("X", [CH, 2, T])
    XG = sb("XG", [CH, 2, T])
    gs = sb("gs", [CH, 2, 8])
    gst = sb("gst", [CH, 2, 12])
    arena = sb("arena", [128, NCH * NH0 * V0 + 2 * (NCH // 2) * INNER])
    w_num, w_dd = NCH * NH0 * V0, NCH // 2 * INNER
    SQ = arena[0:CH, 0:2 * T].rearrange("p (c t) -> p c t", c=2)
    RS = arena[0:CH, 2 * T:3 * T]
    H = arena[0:CH, w_num:w_num + 2 * T].rearrange("p (c t) -> p c t", c=2)
    XIN = arena[:, 0:G3 * (PAD + T)].rearrange("p (g t) -> p g t", g=G3)
    R = arena[0:12, 0:4 * T].rearrange("p (r t) -> p r t", r=4)
    GW = arena[0:44, 4 * T:5 * T]
    MX = arena[0:12, 5 * T:6 * T + 1]
    NUM = arena[:, 0:w_num].rearrange("p (c n) -> p c n", c=NCH)
    DD = arena[:, w_num:w_num + w_dd].rearrange("p (c n) -> p c n", c=NCH // 2)
    WT = arena[:, ATS["b_sel0"][1]:ATS["b_sel0"][1] + 2 * G3 * INNER].rearrange("p (c n) -> p c n", c=2 * G3)
    SQB = arena[:, w_num + w_dd:w_num + 2 * w_dd]
    pair = sb("pair", [128, 4, 512])
    AB = pair[0:96, :, :].rearrange("p (r x) t -> p r (x t)", r=2)
    XB, PB = pair[:, 0:2, :], pair[:, 2:4, :]
    ZS = sb("ZS", [128, G3, T])
    XA = sb("XA", [128, G3, T])
    X2 = sb("X2", [CH, 2, T])
    Q = sb("Q", [128, G3, T])
    K = sb("K", [128, G3, T])
    KT = sb("KT", [128, 2, INNER])
    VE = sb("VE", [128, NCH, NH0 * V0])
    QBD = sb("QBD", [128, 2, HG, L])
    AB3 = sb("AB3", [96, 2, T], BF16)
    GT = sb("GT", [128, NCH, 2 * NH0])
    DEC = sb("DEC", [128, G3, NCH])
    ST = sb("ST", [128, HG * V0 * G3])
    TI = sb("TI", [128, NH0 * V0])
    TC = sb("TC", [128, NH0 * V0])
    sm = sb("sm", [128, 4, NCH // 2 * NH0])
    TZ = sb("TZ", [128, 512])
    YP = sb("YP", [CH, 2, HW + 2, HW + 2])
    YC = sb("YC", [CH, 2, T])
    identb = sb("identb", [128, 128], BF16)
    maskb = sb("maskb", [128, HG, L], BF16)
    a_sel = sb("a_sel", [96, G3, HG * L], BF16)
    b_sel = sb("b_sel", [96, NH0, 128], BF16)

    ident, block, group, mean_w = (cst(n) for n in ("ident", "block", "group", "mean"))
    block_all = block.unsqueeze(1).broadcast_to([128, G3, HG * V0])
    expand = cst("expand")[0:12, :].rearrange("p (g m) -> p g m", g=G3)
    reset = cst("reset")[0:12, :]

    x_loaded = signal("x_loaded", 1, 16)
    gn_stats = signal("gn_stats", 1)
    gn_mean = signal("gn_mean", 1)
    gn_dev = signal("gn_dev", 1)
    gn_var = signal("gn_var", 1)
    gn_sum = signal("gn_sum", 1)
    gn_rstd = signal("gn_rstd", 1)
    xg_ready = signal("xg_ready", 2)
    mean_mm = signal("mean_mm", 2)
    d_ready = signal("d_ready", 2)
    sq_ready = signal("sq_ready", 2)
    var_mm = signal("var_mm", 2)
    rs_ready = signal("rs_ready", 2)
    hn_ready = signal("hn_ready", 2)
    h_ready = signal("h_ready", 4)
    up_mm = signal("up_mm", 16)
    up_evac = signal("up_evac", 16)
    vt_mm = signal("vt_mm", NCH)
    vt_evac = signal("vt_evac", NCH)
    conv_done = signal("conv_done", G3)
    xa_ready = signal("xa_ready", G3)
    qk_mm = signal("qk_mm", 12)
    q_evac = signal("q_evac", 6)
    k_evac = signal("k_evac", 6)
    u_ready = signal("u_ready", G3)
    rx_ready = signal("rx_ready", 1)
    gate_mm = signal("gate_mm", 2)
    gate_evac = signal("gate_evac", 1)
    row_i = signal("row_i", 1)
    row_ab = signal("row_ab", 2)
    row_gx = signal("row_gx", 1)
    part_cast = signal("part_cast", 3)
    part_left = signal("part_left", 2)
    gw_ready = signal("gw_ready", 2)
    gw_mm = signal("gw_mm", 3)
    gt_ready = signal("gt_ready", 3)
    kt_mm = signal("kt_mm", NCH - 1)
    kt_evac = signal("kt_evac", NCH - 1)
    kw_ready = signal("kw_ready", NCH - 1)
    qbd_ready = signal("qbd_ready", G3 * NCH)
    se_mm = signal("se_mm", G3 * NCH)
    x_exp = signal("x_exp", G3 * NCH)
    p_ready = signal("p_ready", G3 * NCH)
    o_mm = signal("o_mm", G3 * NCH)
    inter_mm = signal("inter_mm", NCH - 1)
    inter_used = signal("inter_used", NCH - 1)
    state_mm = signal("state_mm", NCH - 1)
    state_used = signal("state_used", NCH - 1)
    st_ready = signal("st_ready", NCH - 1)
    num_done = signal("num_done", NCH)
    dd_ready = signal("dd_ready", 2)
    dsq_ready = signal("dsq_ready", 2)
    arg_ready = signal("arg_ready", 2)
    rho_ready = signal("rho_ready", 2)
    hn_tok = signal("hn_tok", 2)
    hT_mm = signal("hT_mm", 6)
    hT_evac = signal("hT_evac", 6)
    ho_ready = signal("ho_ready", 6)
    down_mm = signal("down_mm", 4)
    y_done = signal("y_done", 4)
    c3_mm = signal("c3_mm", 4)
    c3_evac = signal("c3_evac", 4)
    bn_done = signal("bn_done", 4)
    yc_stored = signal("yc_stored", 2, 16)
    own_v = Own(ctx.enter_context(nc.semaphore("vector_own")))
    own_a = Own(ctx.enter_context(nc.semaphore("scalar_own")))
    own_p = Own(ctx.enter_context(nc.semaphore("pool_own")))

    block_ctx = ctx.enter_context(nc.Block())
    x_in = d["x"].rearrange("b (c p) h w -> b p c (h w)", p=CH)
    yc_out = d["yc"].rearrange("b p (c t) -> b p c t", c=2)
    span = lambda n: slice(n * 512, (n + 1) * 512)
    chunk = lambda c: slice(c * L, (c + 1) * L)
    heads = lambda ap, w: ap.rearrange("p (h v) -> p h v", v=w)

    @block_ctx.sync
    def _(sp):
        loads = [
            (Wup[:, :, :], d["w_up"].rearrange("(c p) n -> p c n", p=CH)),
            (Wlin[:, :, :], d["w_lin"].rearrange("(c p) n -> p c n", p=CH)),
            (Wq[:, :, :], d["w_q"].rearrange("(c p) n -> p c n", p=128)),
            (Wk[:, :, :], d["w_k"].rearrange("(c p) n -> p c n", p=128)),
            (Wg[:, :, :], d["w_gate"].rearrange("(c p) n -> p c n", p=128)),
            (Wdown[:, :, :], d["w_down"].rearrange("(c p) n -> p c n", p=128)),
            (Wc3[:, :, :, :], d["w_c3"].rearrange("(c p) k n -> p c k n", p=CH)),
            (shared["w96_sb"][:, :], d["col96"]), (shared["w128_sb"][:, :], d["col128"]),
            (shared["rows_sb"][:, :], d["rows"]), (shared["consts"][:, :], d["consts"]),
            (arena[:, 0:ATS["b_sel0"][1]], d["select"][:, 0:ATS["b_sel0"][1]]),
            (WT, d["w_qk_t"].rearrange("(c p) n -> p c n", p=128)),
        ]
        for dst, src in loads:
            sp.dma_start(dst, src).then_inc(setup_loaded.sem, 16)
        assert len(loads) == 13

        def store(i):
            for m in range(2):
                sp.wait_ge(c3_evac.sem, c3_evac.at(i, 2 * m + 2))
                sp.dma_start(yc_out[i][:, m, :], YC[:, m, :]).then_inc(yc_stored.sem, 16)

        def body(i):
            if later(i):
                sp.wait_ge(xg_ready.sem, xg_ready.at(i - 1, 2))
            sp.dma_start(X[:, :, :], x_in[i]).then_inc(x_loaded.sem, 16)
            if not (isinstance(i, int) and i == 0):
                store(i - 1)

        over_images(sp, None, body, lambda i: store(i - 1))
        sp.wait_ge(yc_stored.sem, yc_stored.at(B - 1, 2))

    @block_ctx.gpsimd
    def _(pool):
        for ap in (AB3[:, :, :], YP[:, :, :, :]):
            pool.memset(ap, 0.0).then_inc(setup_done.sem, 1)
        for h in range(NH0):
            pool.memset(VE[:, :, h * V0 + DH0:h * V0 + V0], 1.0).then_inc(setup_done.sem, 1)
        pool.memset(eps[:, 0:1], GN_EPS).then_inc(setup_done.sem, 1)
        pool.memset(eps[:, 1:2], -0.5).then_inc(setup_done.sem, 1)
        pool.wait_ge(setup_loaded.sem, 13 * 16)
        pool.wait_ge(setup_done.sem, shared["n_setup0"])

        rsqrt = lambda out, x: nc.gpsimd.tensor_tensor(
            out, x, eps[0:x.shape[0], 1:2].broadcast_to(list(x.shape)), ALU.pow)

        def body(i):
            pool.wait_ge(gn_sum.sem, gn_sum.at(i, 1))
            rsqrt(gs[:, :, 5], gs[:, :, 3]).then_inc(gn_rstd.sem, 1)
            pool.wait_ge(up_evac.sem, up_evac.at(i, 16))
            pool.wait_ge(qk_mm.sem, qk_mm.at(i, 12))
            nc.gpsimd.tensor_tensor(X2[:, :, :], X2[:, :, :], XG[:, :, :], ALU.add).then_inc(rx_ready.sem, 1)
            for g in range(G3):
                nc.gpsimd.tensor_scalar(XA[:, g, :], XA[:, g, :], w128("skip", g), w128("mh_b", g),
                                        ALU.mult, ALU.add).then_inc(u_ready.sem, 1)
            pool.wait_ge(q_evac.sem, q_evac.at(i, 6))
            for c in range(NCH):
                for g in range(G3):
                    j = G3 * c + g
                    if j >= 2:
                        pool.wait_ge(se_mm.sem, se_mm.at(i, j - 1))
                    else:
                        if later(i):
                            pool.wait_ge(se_mm.sem, se_mm.at(i - 1, G3 * NCH - 1 + j))
                    nc.gpsimd.tensor_tensor(
                        QBD[:, j % 2, :, :], Q[:, g, chunk(c)].unsqueeze(1).broadcast_to([128, HG, L]),
                        block[:, ::V0].unsqueeze(2).broadcast_to([128, HG, L]), ALU.mult).then_inc(qbd_ready.sem, 1)
                if c < NCH - 1:
                    pool.wait_ge(kt_evac.sem, kt_evac.at(i, c + 1))
                    pool.wait_ge(gt_ready.sem, gt_ready.at(i, 3))
                    k = heads(KT[:, c % 2, :], DH0)
                    nc.gpsimd.tensor_tensor(
                        k, k, GT[:, c, NH0:2 * NH0].unsqueeze(2).broadcast_to([128, NH0, DH0]), ALU.mult).then_inc(kw_ready.sem, 1)
                if c == 6:
                    pool.wait_ge(arg_ready.sem, arg_ready.at(i, 1))
                    rsqrt(sm[:, 3, :], sm[:, 2, :]).then_inc(rho_ready.sem, 1)
            pool.wait_ge(arg_ready.sem, arg_ready.at(i, 2))
            rsqrt(sm[:, 3, :], sm[:, 2, :]).then_inc(rho_ready.sem, 1)

        over_images(pool, own_p, body)

    @block_ctx.tensor
    def _(pe):
        mm = nc.tensor.matmul
        pe.wait_ge(setup_loaded.sem, 13 * 16)
        for c in range(G3):
            for k in range(2 * G3):
                last = mm(bank[0][:, 44 * c:44 * c + 44], WT[:, k, c * 128:(c + 1) * 128], Wg[:, k, :],
                          start=(k == 0), stop=(k == 2 * G3 - 1))
        last.then_inc(fold_mm.sem, 1)
        pe.wait_ge(setup_done.sem, shared["n_setup0"])

        def conv3(i, g, part):
            m, n = g // 2, g % 2
            if part == 0:
                if g == 0:
                    pe.wait_ge(y_done.sem, y_done.at(i, 4))
            c = part
            for k in range(9):
                rhs = YP[:, c, n * 16 + k // 3:n * 16 + k // 3 + 16, k % 3:k % 3 + HW]
                last = mm(bank[g][0:CH, :], Wc3[:, c, k, m * CH:(m + 1) * CH], rhs,
                          start=(c == 0 and k == 0), stop=(c == 1 and k == 8))
            if part == 1:
                last.then_inc(c3_mm.sem, 1)

        def body(i, conv=True, rest=True):
            has_conv = conv and not (isinstance(i, int) and i == 0)
            if has_conv:
                conv3(i - 1, 0, 0)
            if rest:
                pe.wait_ge(gn_stats.sem, gn_stats.at(i, 1))
                if later(i):
                    pe.wait_ge(hT_evac.sem, hT_evac.at(i - 1, 6))
                mm(bank[6][0:CH, 0:4], group[0:CH, :], gs[:, :, 0:2], start=True, stop=True).then_inc(gn_mean.sem, 1)
            if has_conv:
                conv3(i - 1, 0, 1)
            if rest:
                pe.wait_ge(gn_dev.sem, gn_dev.at(i, 1))
                mm(bank[6][0:CH, 8:10], group[0:CH, :], gs[:, :, 2], start=True, stop=True).then_inc(gn_var.sem, 1)
            if has_conv:
                conv3(i - 1, 1, 0)
            if rest:
                for n in range(NT):
                    pe.wait_ge(xg_ready.sem, xg_ready.at(i, 2))
                    for c in range(2):
                        last = mm(bank[4 + n][0:CH, :], mean_w[0:CH, :], XG[:, c, span(n)], start=(c == 0), stop=(c == 1))
                    last.then_inc(mean_mm.sem, 1)
            if has_conv:
                conv3(i - 1, 1, 1)
            if not rest:
                conv3(i - 1, 2, 0), conv3(i - 1, 2, 1), conv3(i - 1, 3, 0), conv3(i - 1, 3, 1)
                return
            for n in range(NT):
                pe.wait_ge(sq_ready.sem, sq_ready.at(i, n + 1))
                if n == 0:
                    pe.wait_ge(gn_rstd.sem, gn_rstd.at(i, 1))
                for c in range(2):
                    last = mm(bank[6 + n][0:CH, :], mean_w[0:CH, :], SQ[:, c, span(n)], start=(c == 0), stop=(c == 1))
                last.then_inc(var_mm.sem, 1)

            if has_conv:
                if later(i):
                    pe.wait_ge(c3_evac.sem, c3_evac.at(i - 1, 2))
            if later(i):
                pe.wait_ge(y_done.sem, y_done.at(i - 1, 4))
            pe.wait_ge(h_ready.sem, h_ready.at(i, 4))
            for u in range(16):
                m, n = u // 2, u % 2
                if u >= 4:
                    pe.wait_ge(up_evac.sem, up_evac.at(i, u - 3))
                for c in range(2):
                    if m < 6:
                        last = mm(bank[u % 4][:, :], Wup[:, c, m * 128:(m + 1) * 128], H[:, c, span(n)],
                                  start=(c == 0), stop=(c == 1))
                    else:
                        last = mm(bank[u % 4][0:CH, :], Wlin[:, c, (m - 6) * CH:(m - 5) * CH], XG[:, c, span(n)],
                                  start=(c == 0), stop=(c == 1))
                last.then_inc(up_mm.sem, 1)
            for c in range(NCH):
                if c >= 2:
                    pe.wait_ge(vt_evac.sem, vt_evac.at(i, c - 1))
                else:
                    pe.wait_ge(hn_ready.sem, hn_ready.at(i, 2))
                for g in range(G3):
                    last = nc.tensor.transpose(bank[4 + c % 2][:, 128 * g:128 * g + 128],
                                               XIN[:, g, PAD + c * L:PAD + (c + 1) * L], ident)
                last.then_inc(vt_mm.sem, 1)
            pe.wait_ge(xa_ready.sem, xa_ready.at(i, 3))
            pe.wait_ge(rs_ready.sem, rs_ready.at(i, 2))
            for n in range(NT):
                for c in range(2 * G3):
                    w, src = (c, XA[:, c, span(n)]) if c < G3 else (
                        G3 + c, XIN[:, c - G3, PAD + n * 512:PAD + (n + 1) * 512])
                    last = mm(bank[6 + n][0:44, :], Wg[:, w, :], src, start=(c == 0), stop=(c == 2 * G3 - 1))
                last.then_inc(gate_mm.sem, 1)
            for w in range(12):
                W, m, n = (Wq, w // 2, w % 2) if w < 6 else (Wk, w // 2 - 3, w % 2)
                if w < 4:
                    pe.wait_ge(up_evac.sem, up_evac.at(i, 16))
                else:
                    pe.wait_ge(q_evac.sem, q_evac.at(i, min(w - 3, 6)))
                    if w >= 10:
                        pe.wait_ge(k_evac.sem, k_evac.at(i, w - 9))
                for c in range(G3):
                    last = mm(bank[w % 4][:, :], W[:, c, m * 128:(m + 1) * 128], XA[:, c, span(n)],
                              start=(c == 0), stop=(c == 2))
                last.then_inc(qk_mm.sem, 1)
            if has_conv:
                pe.wait_ge(k_evac.sem, k_evac.at(i, 5))
                conv3(i - 1, 2, 0)
                conv3(i - 1, 2, 1)

            pe.wait_ge(gw_ready.sem, gw_ready.at(i, 2))
            pe.wait_ge(rs_ready.sem, rs_ready.at(i, 2))
            pe.wait_ge(vt_evac.sem, vt_evac.at(i, NCH))
            for k in range(2):
                p = slice(32 * k, 32 * k + NH0)
                for c in range(NCH):
                    last = mm(bank[4 + 2 * k][:, NH0 * c:NH0 * c + NH0], GW[p, chunk(c)], ident[p, p],
                              start=True, stop=True)
                last.then_inc(gw_mm.sem, 1)
            for g in range(G3):
                last = mm(bank[5][:, NCH * g:NCH * g + NCH], expand[:, g, :], GW[0:12, L - 1::L],
                          start=True, stop=True)
            last.then_inc(gw_mm.sem, 1)

            def key_tokens(c):
                if c >= 1:
                    pe.wait_ge(kt_evac.sem, kt_evac.at(i, c))
                else:
                    pe.wait_ge(rs_ready.sem, rs_ready.at(i, 2))
                    pe.wait_ge(k_evac.sem, k_evac.at(i, 6))
                for g in range(G3):
                    last = nc.tensor.transpose(bank[7][:, 128 * g:128 * g + 128], K[:, g, chunk(c)], ident)
                last.then_inc(kt_mm.sem, 1)

            def scores(j):
                c, g = divmod(j, G3)
                if j == 0:
                    pe.wait_ge(gate_evac.sem, gate_evac.at(i, 1))
                    pe.wait_ge(part_cast.sem, part_cast.at(i, 3))
                    if has_conv:
                        if later(i):
                            pe.wait_ge(c3_evac.sem, c3_evac.at(i - 1, 3))
                if j >= 2:
                    pe.wait_ge(p_ready.sem, p_ready.at(i, j - 1))
                    pe.wait_ge(x_exp.sem, x_exp.at(i, j - 1))
                pe.wait_ge(qbd_ready.sem, qbd_ready.at(i, j + 1))
                mm(bank[j % 2][:, :], K[:, g, chunk(c)], QBD[:, j % 2, :, :], start=True, stop=True)
                e = bank[2 + j % 2]
                mm(e[:, :], identb[:, :], maskb[:, :, :], start=True, stop=False)
                mm(e[:, :], AB3[:, 0, chunk(c)], a_sel[:, g, :], start=False, stop=False)
                for h in range(HG):
                    last = mm(e[:, h * L:(h + 1) * L], b_sel[:, HG * g + h, :], AB3[:, 1, chunk(c)],
                              start=False, stop=(h == HG - 1))
                last.then_inc(se_mm.sem, 1)

            def outputs(j):
                c, g = divmod(j, G3)
                pe.wait_ge(p_ready.sem, p_ready.at(i, j + 1))
                if g == 0 and c >= 1:
                    pe.wait_ge(num_done.sem, num_done.at(i, c))
                for h in range(HG):
                    o = (HG * g + h) * V0
                    last = mm(bank[6][:, o:o + V0], PB[:, j % 2, h * L:(h + 1) * L], VE[:, c, o:o + V0],
                              start=True, stop=True)
                last.then_inc(o_mm.sem, 1)

            def inter(c):
                pe.wait_ge(st_ready.sem, st_ready.at(i, c))
                if c >= 2:
                    pe.wait_ge(inter_used.sem, inter_used.at(i, c - 1))
                for g in range(G3):
                    o = g * HG * V0
                    last = mm(bank[5][:, o:o + HG * V0], Q[:, g, chunk(c)], ST[:, o:o + HG * V0], start=True, stop=True)
                last.then_inc(inter_mm.sem, 1)

            def state(c):
                pe.wait_ge(kw_ready.sem, kw_ready.at(i, c + 1))
                if c >= 1:
                    pe.wait_ge(state_used.sem, state_used.at(i, c))
                for g in range(G3):
                    o = g * HG * V0
                    last = mm(bank[4][:, o:o + HG * V0], KT[:, c % 2, 128 * g:128 * g + 128],
                              VE[:, c, o:o + HG * V0], start=True, stop=True)
                last.then_inc(state_mm.sem, 1)

            def head_outputs(half):
                pe.wait_ge(hn_tok.sem, hn_tok.at(i, half + 1))
                for g in range(G3):
                    w = half * G3 + g
                    pe.wait_ge(kt_evac.sem, kt_evac.at(i, NCH - 1))
                    if w >= 1:
                        pe.wait_ge(hT_evac.sem, hT_evac.at(i, w))
                    for cc in range(NCH // 2):
                        last = nc.tensor.transpose(bank[7][:, cc * L:(cc + 1) * L],
                                                   DD[:, cc, 128 * g:128 * g + 128], ident)
                    last.then_inc(hT_mm.sem, 1)

            pe.wait_ge(gt_ready.sem, gt_ready.at(i, 3))
            key_tokens(0)
            scores(0)
            for c in range(NCH):
                scores(3 * c + 1)
                if c < NCH - 1:
                    state(c)
                outputs(3 * c)
                if c >= 1:
                    inter(c)
                scores(3 * c + 2)
                outputs(3 * c + 1)
                if c + 1 < NCH:
                    if c + 1 < NCH - 1:
                        key_tokens(c + 1)
                    scores(3 * c + 3)
                outputs(3 * c + 2)
                if c == 6:
                    head_outputs(0)
            pe.wait_ge(x_exp.sem, x_exp.at(i, G3 * NCH))
            if has_conv:
                conv3(i - 1, 3, 0)
                conv3(i - 1, 3, 1)
                if later(i):
                    pe.wait_ge(c3_evac.sem, c3_evac.at(i - 1, 4))
            head_outputs(1)
            pe.wait_ge(ho_ready.sem, ho_ready.at(i, 6))
            for w in range(4):
                m, n = w // 2, w % 2
                for c in range(G3):
                    last = mm(bank[w][0:CH, :], Wdown[:, c, m * CH:(m + 1) * CH], ZS[:, c, span(n)],
                              start=(c == 0), stop=(c == 2))
                last.then_inc(down_mm.sem, 1)

        over_images(pe, None, body, lambda i: body(i, rest=False))

    @block_ctx.scalar
    def _(act):
        A = nc.scalar.activation
        act.wait_ge(setup_loaded.sem, 13 * 16)
        act.wait_ge(setup_done.sem, shared["n_setup0"])

        def conv_out(i, g):
            m, n = g // 2, g % 2
            act.wait_ge(c3_mm.sem, c3_mm.at(i, g + 1))
            if g == 0:
                if later(i):
                    act.wait_ge(yc_stored.sem, yc_stored.at(i - 1, 2))
                if later(i):
                    act.wait_ge(bn_done.sem, bn_done.at(i - 1, 4))
            A(YC[:, m, span(n)], bank[g][0:CH, :], ACT.Identity, bias=w96("conv2_b", m)).then_inc(c3_evac.sem, 1)

        def body(i, rest=True):
            has_conv = not (isinstance(i, int) and i == 0)
            if not rest:
                for g in range(4):
                    conv_out(i - 1, g)
                return
            for n in range(NT):
                act.wait_ge(d_ready.sem, d_ready.at(i, n + 1))
                A(SQ[:, :, span(n)], H[:, :, span(n)], ACT.Square).then_inc(sq_ready.sem, 1)
                if n == 0 and has_conv:
                    conv_out(i - 1, 0)
            for n in range(NT):
                act.wait_ge(var_mm.sem, var_mm.at(i, n + 1))
                A(RS[:, span(n)], bank[6 + n][0:CH, :], ACT.Ln, bias=eps[0:CH, 0:1]).then_inc(own_a.sem, own_a.step())
            act.wait_ge(own_a.sem, own_a.value())
            for n in range(NT):
                A(RS[:, span(n)], RS[:, span(n)], ACT.Exp, scale=-0.5).then_inc(rs_ready.sem, 1)
            if has_conv:
                conv_out(i - 1, 1)
            for n in range(NT):
                act.wait_ge(hn_ready.sem, hn_ready.at(i, n + 1))
                for c in range(2):
                    A(H[:, c, span(n)], H[:, c, span(n)], ACT.Identity,
                      bias=w96("ln_b", c), scale=w96("ln_w", c)).then_inc(h_ready.sem, 1)
            for u in range(16):
                m, n = u // 2, u % 2
                act.wait_ge(up_mm.sem, up_mm.at(i, u + 1))
                if m < 3:
                    A(XIN[:, m, PAD + n * 512:PAD + (n + 1) * 512], bank[u % 4][:, :], ACT.Identity,
                      bias=w128("b_up", m)).then_inc(up_evac.sem, 1)
                elif m < 6:
                    if u == 6:
                        if later(i):
                            act.wait_ge(down_mm.sem, down_mm.at(i - 1, 4))
                    A(ZS[:, m - 3, span(n)], bank[u % 4][:, :], ACT.Silu, bias=w128("b_up", m)).then_inc(up_evac.sem, 1)
                else:
                    if u == 12:
                        if later(i):
                            act.wait_ge(y_done.sem, y_done.at(i - 1, 4))
                    A(X2[:, m - 6, span(n)], bank[u % 4][0:CH, :], ACT.Silu, bias=w96("b_lin", m - 6)).then_inc(up_evac.sem, 1)
            for g in range(G3):
                act.wait_ge(conv_done.sem, conv_done.at(i, g + 1))
                A(XA[:, g, :], XA[:, g, :], ACT.Silu).then_inc(xa_ready.sem, 1)
            for c in range(NCH):
                act.wait_ge(vt_mm.sem, vt_mm.at(i, c + 1))
                A(heads(VE[:, c, :], V0)[:, :, 0:DH0], heads(bank[4 + c % 2][:, 0:INNER], DH0), ACT.Copy).then_inc(vt_evac.sem, 1)
            act.wait_ge(gate_mm.sem, gate_mm.at(i, 2))
            for n in range(NT):
                A(R[:, 0, span(n)], bank[6 + n][32:44, :], ACT.Identity, bias=rows("b_f")).then_inc(own_a.sem, own_a.step())
                ins = A(R[:, 1, span(n)], bank[6 + n][0:12, :], ACT.Identity, bias=rows("b_i"))
                if n:
                    ins.then_inc(gate_evac.sem, 1)
                else:
                    ins.then_inc(own_a.sem, own_a.step())
            act.wait_ge(own_a.sem, own_a.value())
            A(R[:, 2, :], R[:, 0, :], ACT.Abs).then_inc(own_a.sem, own_a.step())
            act.wait_ge(own_a.sem, own_a.value())
            A(R[:, 2, :], R[:, 2, :], ACT.Exp, scale=-1.0).then_inc(own_a.sem, own_a.step())
            act.wait_ge(own_a.sem, own_a.value())
            A(R[:, 2, :], R[:, 2, :], ACT.Ln, bias=1.0).then_inc(row_i.sem, 1)

            def queries(w):
                act.wait_ge(qk_mm.sem, qk_mm.at(i, w + 1))
                A(Q[:, w // 2, span(w % 2)], bank[w % 4][:, :], ACT.Copy).then_inc(q_evac.sem, 1)

            for w in range(4):
                queries(w)
            for part in range(3):
                p = slice(32 * part, 32 * part + NH0)
                if part:
                    act.wait_ge(part_left.sem, part_left.at(i, part))
                else:
                    act.wait_ge(row_ab.sem, row_ab.at(i, 2))
                A(AB3[p, :, :], AB[p, :, :], ACT.Copy).then_inc(part_cast.sem, 1)
                if part < 2:
                    queries(4 + part)
            act.wait_ge(row_gx.sem, row_gx.at(i, 1))
            A(GW[0:12, :], R[:, 0, :], ACT.Exp).then_inc(gw_ready.sem, 1)
            A(GW[32:44, :], R[:, 3, :], ACT.Exp).then_inc(gw_ready.sem, 1)
            if has_conv:
                conv_out(i - 1, 2)

            def keys(c):
                act.wait_ge(kt_mm.sem, kt_mm.at(i, c + 1))
                if c >= 2:
                    act.wait_ge(state_mm.sem, state_mm.at(i, c - 1))
                A(KT[:, c % 2, :], bank[7][:, 0:INNER], ACT.Copy).then_inc(kt_evac.sem, 1)

            def exps(j):
                act.wait_ge(se_mm.sem, se_mm.at(i, j + 1))
                if j >= 2:
                    act.wait_ge(p_ready.sem, p_ready.at(i, j - 1))
                A(XB[:, j % 2, :], bank[2 + j % 2][:, :], ACT.Exp).then_inc(x_exp.sem, 1)

            def deviations(half):
                act.wait_ge(dd_ready.sem, dd_ready.at(i, half + 1))
                A(SQB[:, :], DD[:, :, :].rearrange("p c n -> p (c n)"), ACT.Square).then_inc(dsq_ready.sem, 1)

            keys(0)
            exps(0)
            for c in range(NCH):
                exps(3 * c + 1)
                exps(3 * c + 2)
                if c + 1 < NCH - 1:
                    keys(c + 1)
                if c + 1 < NCH:
                    exps(3 * c + 3)
                if c == 4:
                    deviations(0)
            if has_conv:
                conv_out(i - 1, 3)
            deviations(1)

        over_images(act, own_a, body, lambda i: body(i, rest=False))

    @block_ctx.vector
    def _(dve):
        V = nc.vector
        dve.wait_ge(setup_loaded.sem, 13 * 16)
        V.tensor_copy(identb[:, :], ident).then_inc(setup_done.sem, 1)
        V.tensor_copy(maskb[:, :, :], cst("causal").unsqueeze(1).broadcast_to([128, HG, L])).then_inc(setup_done.sem, 1)
        V.tensor_copy(a_sel[:, :, :], arena[0:96, 0:G3 * HG * L].rearrange("p (g n) -> p g n", g=G3)).then_inc(setup_done.sem, 1)
        V.tensor_copy(b_sel[:, :, :], arena[0:96, ATS["b_sel0"][0]:ATS["b_sel0"][1]].rearrange("p (g n) -> p g n", g=NH0)).then_inc(setup_done.sem, 1)
        dve.wait_ge(fold_mm.sem, 1)
        V.tensor_copy(Wg[:, 0:G3, :], bank[0][:, 0:G3 * 44].rearrange("p (c n) -> p c n", c=G3)).then_inc(setup_done.sem, 1)
        dve.wait_ge(setup_done.sem, shared["n_setup0"])

        def batch_stats(i, g):
            m, n = g // 2, g % 2
            dve.wait_ge(c3_evac.sem, c3_evac.at(i, g + 1))
            V.bn_stats(bn[:, m, bass.ds(i * 12 + n * 6, 6)], YC[:, m, span(n)]).then_inc(bn_done.sem, 1)

        def body(i, rest=True):
            has_conv = not (isinstance(i, int) and i == 0)
            if not rest:
                for g in range(4):
                    batch_stats(i - 1, g)
                return
            dve.wait_ge(x_loaded.sem, x_loaded.at(i, 1))
            for c in range(2):
                for n in range(NT):
                    V.bn_stats(gst[:, c, 6 * n:6 * n + 6], X[:, c, span(n)]).then_inc(own_v.sem, own_v.step())
            dve.wait_ge(own_v.sem, own_v.value())
            V.memset(gs[:, 0, 3:4], 0.0).then_inc(own_v.sem, own_v.step())
            V.bn_aggr(gs[:, 0, 0:2], gst[:, 0, :]).then_inc(own_v.sem, own_v.step())
            V.bn_aggr(gs[:, 1, 0:2], gst[:, 1, :]).then_inc(gn_stats.sem, 1)
            dve.wait_ge(gn_mean.sem, gn_mean.at(i, 1))
            V.tensor_copy(gs[:, :, 6:8], bank[6][0:CH, 0:4].rearrange("p (c s) -> p c s", c=2)).then_inc(own_v.sem, own_v.step())
            dve.wait_ge(own_v.sem, own_v.value())
            V.tensor_tensor(gs[:, :, 2], gs[:, :, 0], gs[:, :, 6], ALU.subtract).then_inc(own_v.sem, own_v.step())
            dve.wait_ge(own_v.sem, own_v.value())
            V.tensor_tensor(gs[:, :, 2], gs[:, :, 2], gs[:, :, 2], ALU.mult).then_inc(gn_dev.sem, 1)
            dve.wait_ge(gn_var.sem, gn_var.at(i, 1))
            V.scalar_tensor_tensor(gs[:, :, 3], bank[6][0:CH, 8:10], GN_EPS, gs[:, :, 7],
                                   ALU.add, ALU.add).then_inc(gn_sum.sem, 1)
            dve.wait_ge(gn_rstd.sem, gn_rstd.at(i, 1))
            if later(i):
                dve.wait_ge(rx_ready.sem, rx_ready.at(i - 1, 1))
            for c in range(2):
                V.tensor_scalar(XG[:, c, :], X[:, c, :], gs[:, c, 6:7], gs[:, c, 5:6],
                                ALU.subtract, ALU.mult).then_inc(xg_ready.sem, 1)
            if later(i):
                dve.wait_ge(up_mm.sem, up_mm.at(i - 1, 12))
            for n in range(NT):
                dve.wait_ge(mean_mm.sem, mean_mm.at(i, n + 1))
                V.tensor_tensor(H[:, :, span(n)], XG[:, :, span(n)],
                                bank[4 + n][0:CH, :].unsqueeze(1).broadcast_to([CH, 2, 512]), ALU.subtract).then_inc(d_ready.sem, 1)
            if has_conv:
                batch_stats(i - 1, 0)
            for n in range(NT):
                dve.wait_ge(rs_ready.sem, rs_ready.at(i, n + 1))
                V.tensor_tensor(H[:, :, span(n)], H[:, :, span(n)],
                                RS[:, span(n)].unsqueeze(1).broadcast_to([CH, 2, 512]), ALU.mult).then_inc(hn_ready.sem, 1)
            if has_conv:
                batch_stats(i - 1, 1)
            dve.wait_ge(hn_ready.sem, hn_ready.at(i, 2))
            V.memset(XIN[:, :, 0:PAD], 0.0).then_inc(own_v.sem, own_v.step())
            dve.wait_ge(own_v.sem, own_v.value())
            if later(i):
                dve.wait_ge(hT_evac.sem, hT_evac.at(i - 1, 6))
            for g in range(G3):
                dve.wait_ge(up_evac.sem, up_evac.at(i, 2 * g + 2))
                if g == 0:
                    if later(i):
                        dve.wait_ge(ho_ready.sem, ho_ready.at(i - 1, 6))
                V.tensor_scalar(XA[:, g, :], XIN[:, g, 0:T], w128("conv_k", 4 * g), w128("conv_b", g),
                                ALU.mult, ALU.add).then_inc(own_v.sem, own_v.step())
                for t in range(1, TAPS):
                    dve.wait_ge(own_v.sem, own_v.value())
                    ins = V.scalar_tensor_tensor(
                        XA[:, g, :], XIN[:, g, t:t + T], w128("conv_k", 4 * g + t), XA[:, g, :], ALU.mult, ALU.add)
                    if t == TAPS - 1:
                        ins.then_inc(conv_done.sem, 1)
                    else:
                        ins.then_inc(own_v.sem, own_v.step())
            dve.wait_ge(row_i.sem, row_i.at(i, 1))
            dve.wait_ge(gate_evac.sem, gate_evac.at(i, 1))
            V.scalar_tensor_tensor(R[:, 3, :], R[:, 0, :], 0.0, R[:, 2, :], ALU.min, ALU.subtract).then_inc(own_v.sem, own_v.step())
            dve.wait_ge(own_v.sem, own_v.value())
            V.tensor_tensor_scan(R[:, 2, :], reset, R[:, 3, :], 0.0, ALU.mult, ALU.add).then_inc(own_v.sem, own_v.step())
            V.memset(MX[:, 0:1], 0.0).then_inc(own_v.sem, own_v.step())
            V.tensor_tensor_scan(MX[:, 1:1 + T], R[:, 3, :], R[:, 1, :], 0.0, ALU.add, ALU.max).then_inc(own_v.sem, own_v.step())
            dve.wait_ge(own_v.sem, own_v.value())
            V.tensor_tensor(AB[0:12, 0, :], R[:, 1, :], R[:, 2, :], ALU.subtract).then_inc(row_ab.sem, 1)
            V.tensor_tensor(AB[0:12, 1, :], R[:, 2, :], MX[:, 1:1 + T], ALU.subtract).then_inc(row_ab.sem, 1)
            dve.wait_ge(row_ab.sem, row_ab.at(i, 2))
            by_chunk = lambda ap: ap.rearrange("p (c l) -> p c l", l=L)
            spread = lambda ap: ap.unsqueeze(2).broadcast_to([12, NCH, L])
            V.tensor_tensor(by_chunk(R[:, 0, :]), by_chunk(AB[0:12, 1, :]), spread(MX[:, 0:T:L]), ALU.add).then_inc(own_v.sem, own_v.step())
            V.tensor_tensor(by_chunk(R[:, 3, :]), by_chunk(AB[0:12, 0, :]),
                            spread(AB[0:12, 1, L - 1::L]), ALU.add).then_inc(row_gx.sem, 1)
            for part in range(2):
                p, q = slice(32 * part, 32 * part + NH0), slice(32 * part + 32, 32 * part + 32 + NH0)
                dve.wait_ge(part_cast.sem, part_cast.at(i, part + 1))
                V.tensor_tensor(AB[q, :, :], AB[p, :, :], AB3[p, :, :], ALU.subtract).then_inc(part_left.sem, 1)
            for w in range(6):
                dve.wait_ge(qk_mm.sem, qk_mm.at(i, 7 + w))
                V.tensor_scalar(K[:, w // 2, span(w % 2)], bank[(6 + w) % 4][:, :], float(DH0) ** -0.5,
                                None, ALU.mult).then_inc(k_evac.sem, 1)
            if has_conv:
                batch_stats(i - 1, 2)
            dve.wait_ge(gw_mm.sem, gw_mm.at(i, 3))
            for k in range(2):
                V.tensor_copy(GT[:, :, NH0 * k:NH0 * k + NH0], bank[4 + 2 * k][:, 0:NH0 * NCH]
                              .rearrange("p (c n) -> p c n", c=NCH)).then_inc(gt_ready.sem, 1)
            V.tensor_copy(DEC[:, :, :], bank[5][:, 0:G3 * NCH].rearrange("p (g c) -> p g c", g=G3)).then_inc(gt_ready.sem, 1)

            def weigh(j):
                dve.wait_ge(x_exp.sem, x_exp.at(i, j + 1))
                if j >= 2:
                    dve.wait_ge(o_mm.sem, o_mm.at(i, j - 1))
                V.tensor_tensor(PB[:, j % 2, :], bank[j % 2][:, :], XB[:, j % 2, :], ALU.mult).then_inc(p_ready.sem, 1)

            def state(c):
                dve.wait_ge(state_mm.sem, state_mm.at(i, c + 1))
                new = bank[4][:, 0:NH0 * V0].rearrange("p (g n) -> p g n", g=G3)
                V.tensor_tensor(TC[:, :].rearrange("p (g n) -> p g n", g=G3), new, block_all, ALU.mult).then_inc(state_used.sem, 1)
                dve.wait_ge(state_used.sem, state_used.at(i, c + 1))
                if c == 0:
                    if later(i):
                        dve.wait_ge(inter_mm.sem, inter_mm.at(i - 1, NCH - 1))
                    V.tensor_copy(ST[:, :], TC[:, :]).then_inc(st_ready.sem, 1)
                    return
                dve.wait_ge(inter_mm.sem, inter_mm.at(i, c))
                dve.wait_ge(st_ready.sem, st_ready.at(i, c))
                for g in range(G3):
                    o = slice(g * HG * V0, (g + 1) * HG * V0)
                    ins = V.scalar_tensor_tensor(ST[:, o], ST[:, o], DEC[:, g, c:c + 1], TC[:, o], ALU.mult, ALU.add)
                    if g == G3 - 1:
                        ins.then_inc(st_ready.sem, 1)
                    else:
                        ins.then_inc(own_v.sem, own_v.step())

            def reach(c):
                dve.wait_ge(inter_mm.sem, inter_mm.at(i, c))
                V.tensor_tensor(heads(TI[:, :], V0), heads(bank[5][:, 0:NH0 * V0], V0),
                                GT[:, c, 0:NH0].unsqueeze(2).broadcast_to([128, NH0, V0]), ALU.mult).then_inc(inter_used.sem, 1)

            def total(c):
                dve.wait_ge(o_mm.sem, o_mm.at(i, G3 * (c + 1)))
                out = NUM[:, c, :]
                if c == 0:
                    V.tensor_copy(out, bank[6][:, 0:NH0 * V0]).then_inc(num_done.sem, 1)
                else:
                    dve.wait_ge(inter_used.sem, inter_used.at(i, c))
                    V.tensor_tensor(out, bank[6][:, 0:NH0 * V0], TI[:, :], ALU.add).then_inc(num_done.sem, 1)

            half_n = NCH // 2 * NH0
            dd = DD[:, :, :].rearrange("p c (h v) -> p (c h) v", v=DH0)

            def center(half):
                dve.wait_ge(num_done.sem, num_done.at(i, 4 * half + 4))
                num = NUM[:, 4 * half:4 * half + 4, :].rearrange("p c (h v) -> p (c h) v", v=V0)
                V.tensor_tensor(sm[:, 0, :], num[:, :, DH0], num[:, :, DH0], ALU.mult).then_inc(own_v.sem, own_v.step())
                V.reduce_sum(sm[:, 1, :], num[:, :, 0:DH0], AX).then_inc(own_v.sem, own_v.step())
                dve.wait_ge(own_v.sem, own_v.value())
                V.tensor_scalar(sm[:, 0, :], sm[:, 0, :], 1.0, GN_EPS, ALU.max, ALU.mult).then_inc(own_v.sem, own_v.step())
                if half:
                    dve.wait_ge(hT_mm.sem, hT_mm.at(i, 3))
                V.scalar_tensor_tensor(dd, sm[:, 1, :].unsqueeze(2).broadcast_to([128, half_n, DH0]),
                                       -1.0 / DH0, num[:, :, 0:DH0], ALU.mult, ALU.add).then_inc(dd_ready.sem, 1)

            def spread_of(half):
                dve.wait_ge(dsq_ready.sem, dsq_ready.at(i, half + 1))
                V.reduce_sum(sm[:, 1, :], SQB[:, :].rearrange("p (h v) -> p h v", v=DH0), AX).then_inc(own_v.sem, own_v.step())
                dve.wait_ge(own_v.sem, own_v.value())
                V.scalar_tensor_tensor(sm[:, 2, :], sm[:, 1, :], 1.0 / DH0, sm[:, 0, :],
                                       ALU.mult, ALU.add).then_inc(arg_ready.sem, 1)

            def normalise(half):
                dve.wait_ge(rho_ready.sem, rho_ready.at(i, half + 1))
                V.tensor_tensor(dd, dd, sm[:, 3, :].unsqueeze(2).broadcast_to([128, half_n, DH0]),
                                ALU.mult).then_inc(hn_tok.sem, 1)

            def gate(half):
                dve.wait_ge(u_ready.sem, u_ready.at(i, 3))
                for g in range(G3):
                    dve.wait_ge(hT_mm.sem, hT_mm.at(i, half * G3 + g + 1))
                    if later(i) or half * G3 + g:
                        dve.wait_ge(ho_ready.sem, ho_ready.at(i, half * G3 + g))
                    V.scalar_tensor_tensor(TZ[:, :], bank[7][:, :], w128("mh_w", g),
                                           XA[:, g, span(half)], ALU.mult, ALU.add).then_inc(hT_evac.sem, 1)
                    dve.wait_ge(hT_evac.sem, hT_evac.at(i, half * G3 + g + 1))
                    V.tensor_tensor(ZS[:, g, span(half)], TZ[:, :], ZS[:, g, span(half)], ALU.mult).then_inc(ho_ready.sem, 1)

            weigh(0)
            for c in range(NCH):
                weigh(3 * c + 1)
                if c == 0:
                    state(c)
                else:
                    reach(c)
                weigh(3 * c + 2)
                if 1 <= c < NCH - 1:
                    state(c)
                if c + 1 < NCH:
                    weigh(3 * c + 3)
                total(c)
                if c == 4:
                    center(0)
                if c == 5:
                    spread_of(0)
                if c == 6:
                    normalise(0)
                    gate(0)
            center(1)
            if has_conv:
                batch_stats(i - 1, 3)
            spread_of(1)
            normalise(1)
            gate(1)
            dve.wait_ge(rx_ready.sem, rx_ready.at(i, 1))
            if later(i):
                dve.wait_ge(c3_mm.sem, c3_mm.at(i - 1, 4))
            for w in range(4):
                m, n = w // 2, w % 2
                dve.wait_ge(down_mm.sem, down_mm.at(i, w + 1))
                V.scalar_tensor_tensor(
                    YP[:, m, 1 + 16 * n:17 + 16 * n, 1:1 + HW], bank[w][0:CH, :].rearrange("p (r s) -> p r s", s=HW),
                    w96("b_down", m), X2[:, m, span(n)].rearrange("p (r s) -> p r s", s=HW), ALU.add, ALU.add).then_inc(y_done.sem, 1)

        over_images(dve, own_v, body, lambda i: body(i, rest=False))


def layer1(nc, ctx, d, shared, out):
    def sb(name, shape, dt=F32):
        return ctx.enter_context(nc.sbuf_tensor(name, shape, dt))

    def signal(name, per_image, unit=1):
        return Signal(ctx.enter_context(nc.semaphore(name)), per_image, unit)

    bank = shared["bank"]
    w96, w128, rows, cst, eps = (shared[k] for k in ("w96", "w128", "rows", "cst", "eps"))
    bn = shared["bn"]
    XBC_T = 4
    KX = INNER + NS

    Win = sb("Win", [CH, 2, 2 * INNER + 2 * NS + NH1])
    Wout = sb("Wout", [128, G3, C])
    Wf1 = sb("Wf1", [CH, 2, INNER])
    Wf2 = sb("Wf2", [128, G3, C])
    identb = sb("m_identb", [128, 128], BF16)
    maskb = sb("m_maskb", [128, HB, L], BF16)
    a_sel = sb("m_a_sel", [96, 2, HB * L], BF16)
    b_sel = sb("m_b_sel", [96, NH1, 128], BF16)
    ones = sb("m_ones", [NH1, NS])
    X1 = sb("X1", [CH, 2, T])
    Y0 = sb("Y0", [CH, 2, T])
    XG = sb("m_XG", [CH, 2, T])
    hst = sb("hst", [128, NCH, 6])
    hmv = sb("hmv", [128, NCH, 4])
    n1 = sb("n1", [128, 2, C])
    U = sb("U", [CH, 2, T])
    gs = sb("m_gs", [CH, 2, 8])
    gst = sb("m_gst", [CH, 2, 12])
    bns = sb("bns", [CH, 2, 6])
    XBC = sb("XBC", [128, XBC_T, PAD + T])
    CV = sb("CV", [128, XBC_T, T])
    BS = sb("BS", [NS, T])
    CS = sb("CS", [NS, T])
    ZT = sb("ZT", [128, NCH, INNER])
    XT = sb("XT", [128, NCH, KX])
    XD = sb("XD", [128, 2, INNER])
    XW = sb("XW", [128, 2, INNER])
    R = sb("m_R", [NH1, 2, T])
    CU = sb("CU", [96, T])
    CU3 = sb("CU3", [96, T], BF16)
    GWD = sb("GWD", [64 + NH1, T])
    GT = sb("m_GT", [128, NCH, 3 * NH1])
    DG = sb("DG", [NH1, NCH, NH1])
    DEC = sb("m_DEC", [NS, NCH, NH1])
    XB = sb("m_XB", [128, 2, HB * L])
    PB = sb("m_PB", [128, 4, HB * L])
    ST = sb("m_ST", [NS, INNER])
    TI = sb("m_TI", [128, INNER])
    YT = sb("YT", [128, NCH, INNER])
    JK = sb("JK", [128, INNER])
    SS = sb("SS", [128, NCH])
    RR = sb("RR", [128, NCH])
    GC = sb("GC", [128, G3, T])
    XX = sb("XX", [CH, 2, T])
    OUT = sb("OUT", [CH, 2, T])
    halves = lambda ap: ap.rearrange("p (c t) -> p c t", c=2)
    HT = ZT[:, 0:NCH // 2, :].rearrange("p c n -> p (c n)").rearrange("p (c n) -> p c n", n=C)
    yt = YT[:, :, :].rearrange("p c n -> p (c n)")
    H2, RS2, SQ2 = halves(yt[0:CH, 0:2 * T]), yt[0:CH, 2 * T:3 * T], OUT
    XF = CV[0:CH, 0:2, :]
    F = GC
    sel = yt[0:96, 0:NH1 * (L + 128)]

    ident, group, mean_w = (cst(n) for n in ("ident", "group", "mean"))
    pick = cst("pick1")[0:64 + NH1, :]
    reset = cst("reset")[0:NH1, :]

    loaded = signal("m_loaded", 0, 16)
    setup = signal("m_setup", 0)
    n_setup = 11
    y_loaded = signal("y_loaded", 1, 16)
    x_loaded = signal("m_x_loaded", 1, 16)
    y_scaled = signal("y_scaled", 2)
    x1_ready = signal("x1_ready", 1)
    gn_stats = signal("m_gn_stats", 1)
    gn_mean = signal("m_gn_mean", 1)
    gn_dev = signal("m_gn_dev", 1)
    gn_var = signal("m_gn_var", 1)
    gn_sum = signal("m_gn_sum", 1)
    gn_rstd = signal("m_gn_rstd", 1)
    xg_ready = signal("m_xg_ready", 2)
    ln2 = {n: signal(f"ln2_{n}", c) for n, c in
           [("mean", 2), ("d", 2), ("sq", 2), ("var", 2), ("ln", 2), ("rs", 2), ("hn", 2), ("h", 4)]}
    ht_mm = signal("ht_mm", 4)
    ht_evac = signal("ht_evac", 4)
    hv_ready = signal("hv_ready", 1)
    hr_ready = signal("hr_ready", 1)
    ht_ready = signal("ht_ready", NCH)
    u_stored = signal("u_stored", 1, 16)
    u_loaded = signal("u_loaded", 1, 16)
    in_mm = signal("in_mm", 18)
    in_evac = signal("in_evac", 18)
    conv_done = signal("m_conv_done", XBC_T)
    xs_ready = signal("xs_ready", 5)
    row_sp = signal("row_sp", 1)
    cu_ready = signal("cu_ready", 1)
    part_cast = signal("m_part_cast", 3)
    part_left = signal("m_part_left", 2)
    row_w = signal("row_w", 1)
    row_we = signal("row_we", 1)
    g_ready = signal("g_ready", 2)
    w_ready = signal("w_ready", 1)
    dg_ready = signal("dg_ready", 1)
    gw_mm = signal("m_gw_mm", 2)
    gt_ready = signal("m_gt_ready", 2)
    xt_mm = signal("xt_mm", NCH)
    xt_evac = signal("xt_evac", NCH)
    xd_ready = signal("xd_ready", NCH)
    xw_ready = signal("xw_ready", NCH)
    xu_ready = signal("xu_ready", NCH)
    s_mm = signal("s_mm", NCH)
    e_mm = signal("e_mm", 2 * NCH)
    x_exp = signal("m_x_exp", 2 * NCH)
    p_ready = signal("m_p_ready", 2 * NCH)
    state_mm = signal("m_state_mm", NCH - 1)
    st_ready = signal("m_st_ready", NCH - 1)
    o_mm = signal("m_o_mm", NCH)
    inter_mm = signal("m_inter_mm", NCH - 1)
    inter_used = signal("m_inter_used", NCH - 1)
    o_used = signal("o_used", NCH)
    y_gated = signal("y_gated", NCH)
    ss_ready = signal("ss_ready", NCH)
    ms_ready = signal("ms_ready", 2)
    rr_ready = signal("rr_ready", 2)
    yn_ready = signal("yn_ready", NCH)
    gT_mm = signal("gT_mm", 6)
    gT_evac = signal("gT_evac", 6)
    out_mm = signal("out_mm", 4)
    xf_ready = signal("xf_ready", 4)
    xx_ready = signal("xx_ready", 1)
    f1_mm = signal("f1_mm", 6)
    f1_evac = signal("f1_evac", 6)
    f2_mm = signal("f2_mm", 4)
    out_ready = signal("out_ready", 4)
    stored = signal("stored", 1, 16)
    own_v = Own(ctx.enter_context(nc.semaphore("m_vector_own")))
    own_a = Own(ctx.enter_context(nc.semaphore("m_scalar_own")))
    own_p = Own(ctx.enter_context(nc.semaphore("m_pool_own")))

    block_ctx = ctx.enter_context(nc.Block())
    x_in = d["x"].rearrange("b (c p) h w -> b p c (h w)", p=CH)
    x_out = out.rearrange("b (c p) h w -> b p c (h w)", p=CH)
    u_by_token = d["u"].rearrange("b (c p n) -> b p c n", p=128, n=C)
    u_by_channel = d["u"].rearrange("b (c p t) -> b p c t", c=2, t=T)
    y_in = d["yc"].rearrange("b p (c t) -> b p c t", c=2)
    span = lambda n: slice(n * 512, (n + 1) * 512)
    chunk = lambda c: slice(c * L, (c + 1) * L)
    heads = lambda ap: ap.rearrange("p (h v) -> p h v", v=DH1)
    is_first = lambda i: isinstance(i, int) and i == 0

    def tile_rows(w):
        return (slice(INNER + (w // 2) * 128, INNER + (w // 2 + 1) * 128) if w < 8
                else slice(2 * INNER + 2 * NS, 2 * INNER + 2 * NS + NH1))

    @block_ctx.sync
    def _(sp):
        loads = [
            (Win[:, :, :], d["w_in"].rearrange("(c p) n -> p c n", p=CH)),
            (Wout[:, :, :], d["w_out"].rearrange("(c p) n -> p c n", p=128)),
            (Wf1[:, :, :], d["w_f1"].rearrange("(c p) n -> p c n", p=CH)),
            (Wf2[:, :, :], d["w_f2"].rearrange("(c p) n -> p c n", p=128)),
            (n1[:, :, :], d["norm1"].rearrange("p (k n) -> p k n", k=2)),
            (sel[:, :], d["select"][0:96, ATS["a_sel1"][0]:ATS["b_sel1"][1]]),
        ]
        for dst, src in loads:
            sp.dma_start(dst, src).then_inc(loaded.sem, 16)
        assert len(loads) == 6

        def store(i):
            sp.wait_ge(out_ready.sem, out_ready.at(i, 4))
            sp.dma_start(x_out[i], OUT[:, :, :]).then_inc(stored.sem, 16)

        def body(i):
            if later(i):
                sp.wait_ge(x1_ready.sem, x1_ready.at(i - 1, 1))
            sp.dma_start(Y0[:, :, :], y_in[i]).then_inc(y_loaded.sem, 16)
            if later(i):
                sp.wait_ge(xx_ready.sem, xx_ready.at(i - 1, 1))
            sp.dma_start(X1[:, :, :], x_in[i]).then_inc(x_loaded.sem, 16)
            sp.wait_ge(ht_ready.sem, ht_ready.at(i, NCH))
            sp.dma_start(u_by_token[i], HT[:, :, :]).then_inc(u_stored.sem, 16)
            sp.wait_ge(u_stored.sem, u_stored.at(i, 1))
            if later(i):
                sp.wait_ge(in_mm.sem, in_mm.at(i - 1, 18))
            sp.dma_start(U[:, :, :], u_by_channel[i]).then_inc(u_loaded.sem, 16)
            if not is_first(i):
                store(i - 1)

        over_images(sp, None, body, lambda i: store(i - 1))
        sp.wait_ge(stored.sem, stored.at(B - 1, 1))

    @block_ctx.gpsimd
    def _(pool):
        pool.memset(CU3[:, :], 0.0).then_inc(setup.sem, 1)
        pool.memset(GWD[:, :], 0.0).then_inc(setup.sem, 1)
        pool.memset(XBC[:, :, 0:PAD], 0.0).then_inc(setup.sem, 1)
        pool.memset(ones[:, :], 1.0).then_inc(setup.sem, 1)
        rsqrt = lambda o, x: nc.gpsimd.tensor_tensor(
            o, x, eps[0:x.shape[0], 1:2].broadcast_to(list(x.shape)), ALU.pow)
        pool.wait_ge(setup.sem, n_setup - 2)
        rsqrt(bns[:, :, 3], bns[:, :, 2]).then_inc(setup.sem, 1)
        pool.wait_ge(setup.sem, n_setup)

        def body(i):
            pool.wait_ge(gn_sum.sem, gn_sum.at(i, 1))
            rsqrt(gs[:, :, 5], gs[:, :, 3]).then_inc(gn_rstd.sem, 1)
            pool.wait_ge(hv_ready.sem, hv_ready.at(i, 1))
            rsqrt(hmv[:, :, 3], hmv[:, :, 2]).then_inc(hr_ready.sem, 1)
            for c in range(NCH):
                pool.wait_ge(xt_evac.sem, xt_evac.at(i, c + 1))
                if c == 0:
                    pool.wait_ge(gt_ready.sem, gt_ready.at(i, 1))
                x = heads(XT[:, c, 0:INNER])
                by_head = lambda ap: ap.unsqueeze(2).broadcast_to([128, NH1, DH1])
                if c >= 2:
                    pool.wait_ge(o_mm.sem, o_mm.at(i, c - 1))
                    pool.wait_ge(state_mm.sem, state_mm.at(i, c - 1))
                nc.gpsimd.tensor_tensor(heads(XD[:, c % 2, :]), x, by_head(GT[:, c, 12:18]), ALU.mult).then_inc(xd_ready.sem, 1)
                nc.gpsimd.tensor_tensor(heads(XW[:, c % 2, :]), x, by_head(GT[:, c, 6:12]), ALU.mult).then_inc(xw_ready.sem, 1)
                pool.wait_ge(xw_ready.sem, xw_ready.at(i, c + 1))
                nc.gpsimd.tensor_tensor(x, x, by_head(w128("D", 0, NH1)), ALU.mult).then_inc(xu_ready.sem, 1)
                if c in (5, 7):
                    pool.wait_ge(ms_ready.sem, ms_ready.at(i, (c - 3) // 2))
                    h = slice(4 * ((c - 5) // 2), 4 * ((c - 5) // 2) + 4)
                    rsqrt(RR[:, h], SS[:, h]).then_inc(rr_ready.sem, 1)
            pool.wait_ge(xf_ready.sem, xf_ready.at(i, 4))
            nc.gpsimd.tensor_tensor(XX[:, :, :], XF[:, :, :], X1[:, :, :], ALU.add).then_inc(xx_ready.sem, 1)

        over_images(pool, own_p, body)

    @block_ctx.tensor
    def _(pe):
        mm = nc.tensor.matmul
        pe.wait_ge(loaded.sem, 6 * 16)
        pe.wait_ge(setup.sem, n_setup)

        def average(i, kind, src, ready, count):
            b = 4 if kind == "mean" else 6
            for n in range(NT):
                pe.wait_ge(ready.sem, ready.at(i, count if kind == "mean" else n + 1))
                for c in range(2):
                    last = mm(bank[b + n][0:CH, :], mean_w[0:CH, :], src[:, c, span(n)], start=(c == 0), stop=(c == 1))
                last.then_inc(ln2[kind].sem, 1)

        def ffn1(i):
            pe.wait_ge(ln2["h"].sem, ln2["h"].at(i, 4))
            pe.wait_ge(xf_ready.sem, xf_ready.at(i, 4))
            for w in range(6):
                m, n = w // 2, w % 2
                if w >= 4:
                    pe.wait_ge(f1_evac.sem, f1_evac.at(i, w - 3))
                for c in range(2):
                    last = mm(bank[w % 4][:, :], Wf1[:, c, m * 128:(m + 1) * 128], H2[:, c, span(n)],
                              start=(c == 0), stop=(c == 1))
                last.then_inc(f1_mm.sem, 1)

        def ffn2(i):
            pe.wait_ge(f1_evac.sem, f1_evac.at(i, 6))
            for w in range(4):
                m, n = w // 2, w % 2
                for c in range(G3):
                    last = mm(bank[(6 + w) % 4][0:CH, :], Wf2[:, c, m * CH:(m + 1) * CH], F[:, c, span(n)],
                              start=(c == 0), stop=(c == 2))
                last.then_inc(f2_mm.sem, 1)

        def body(i, rest=True):
            back = not is_first(i)
            if back:
                average(i - 1, "mean", XF, xf_ready, 4)
                if rest:
                    if later(i):
                        pe.wait_ge(gT_evac.sem, gT_evac.at(i - 1, 6))
            if rest:
                pe.wait_ge(gn_stats.sem, gn_stats.at(i, 1))
                mm(bank[7][0:CH, 0:4], group[0:CH, :], gs[:, :, 0:2], start=True, stop=True).then_inc(gn_mean.sem, 1)
                pe.wait_ge(gn_dev.sem, gn_dev.at(i, 1))
                mm(bank[7][0:CH, 8:10], group[0:CH, :], gs[:, :, 2], start=True, stop=True).then_inc(gn_var.sem, 1)
                pe.wait_ge(gn_rstd.sem, gn_rstd.at(i, 1))
            if back:
                average(i - 1, "var", SQ2, ln2["sq"], 0)
                if later(i):
                    pe.wait_ge(ln2["d"].sem, ln2["d"].at(i - 1, 2))
            if rest:
                pe.wait_ge(xg_ready.sem, xg_ready.at(i, 2))
                for q in range(4):
                    if q >= 2:
                        pe.wait_ge(ht_evac.sem, ht_evac.at(i, q - 1))
                    for k in range(4):
                        c, half = 2 * q + k // 2, k % 2
                        last = nc.tensor.transpose(bank[4 + q % 2][:, CH * k:CH * k + CH], XG[:, half, chunk(c)],
                                                   ident[0:CH, 0:CH])
                    last.then_inc(ht_mm.sem, 1)
            if back:
                ffn1(i - 1)
            if back:
                ffn2(i - 1)
            if not rest:
                return
            pe.wait_ge(u_loaded.sem, u_loaded.at(i, 1))
            if back:
                if later(i):
                    pe.wait_ge(out_ready.sem, out_ready.at(i - 1, 4))
            for w in range(18):
                if w >= 4:
                    pe.wait_ge(in_evac.sem, in_evac.at(i, w - 3))
                b = bank[w % 4]
                for c in range(2):
                    flags = dict(start=(c == 0), stop=(c == 1))
                    if w < 10:
                        r = tile_rows(w)
                        last = mm(b[0:r.stop - r.start, :], Win[:, c, r], U[:, c, span(w % 2)], **flags)
                    else:
                        last = mm(b[:, 0:INNER], U[:, c, chunk(w - 10)], Win[:, c, 0:INNER], **flags)
                last.then_inc(in_mm.sem, 1)
            pe.wait_ge(ht_evac.sem, ht_evac.at(i, 4))
            pe.wait_ge(xs_ready.sem, xs_ready.at(i, 5))
            for c in range(NCH):
                if c >= 2:
                    pe.wait_ge(xt_evac.sem, xt_evac.at(i, c - 1))
                b = bank[4 + c % 2]
                for g in range(G3):
                    nc.tensor.transpose(b[:, 128 * g:128 * g + 128], CV[:, g, chunk(c)], ident)
                nc.tensor.transpose(b[:, INNER:KX], BS[:, chunk(c)], ident[0:NS, 0:NS]).then_inc(xt_mm.sem, 1)
            if later(i):
                pe.wait_ge(ln2["rs"].sem, ln2["rs"].at(i - 1, 2))
            pe.wait_ge(g_ready.sem, g_ready.at(i, 2))
            pe.wait_ge(w_ready.sem, w_ready.at(i, 1))
            for c in range(NCH):
                last = mm(bank[6][:, 18 * c:18 * c + 18], GWD[:, chunk(c)], pick, start=True, stop=True)
            last.then_inc(gw_mm.sem, 1)
            pe.wait_ge(dg_ready.sem, dg_ready.at(i, 1))
            mm(bank[7][0:NS, 0:NCH * NH1], ones[:, :], DG[:, :, :], start=True, stop=True).then_inc(gw_mm.sem, 1)

            def scores(c):
                if c == 0:
                    pe.wait_ge(in_evac.sem, in_evac.at(i, 18))
                    pe.wait_ge(part_cast.sem, part_cast.at(i, 3))
                if c >= 2:
                    pe.wait_ge(p_ready.sem, p_ready.at(i, 2 * (c - 1)))
                mm(bank[c % 2][:, 0:L], BS[:, chunk(c)], CS[:, chunk(c)], start=True, stop=True).then_inc(s_mm.sem, 1)
                for k in range(2):
                    if c >= 1:
                        pe.wait_ge(x_exp.sem, x_exp.at(i, 2 * c - 1 + k))
                    e = bank[2 + k][:, 0:HB * L]
                    mm(e, identb[:, :], maskb[:, :, :], start=True, stop=False)
                    mm(e, CU3[:, chunk(c)], a_sel[:, k, :], start=False, stop=False)
                    for h in range(HB):
                        last = mm(bank[2 + k][:, h * L:(h + 1) * L], b_sel[:, HB * k + h, :], CU3[:, chunk(c)],
                                  start=False, stop=(h == HB - 1))
                    last.then_inc(e_mm.sem, 1)

            def state(c):
                pe.wait_ge(xw_ready.sem, xw_ready.at(i, c + 1))
                if c == 0:
                    pe.wait_ge(gt_ready.sem, gt_ready.at(i, 2))
                else:
                    pe.wait_ge(st_ready.sem, st_ready.at(i, c))
                mm(bank[6][0:NS, 0:INNER], XT[:, c, INNER:KX], XW[:, c % 2, :], start=True, stop=True).then_inc(state_mm.sem, 1)

            def outputs(c):
                pe.wait_ge(xd_ready.sem, xd_ready.at(i, c + 1))
                if c == 0:
                    pe.wait_ge(xt_evac.sem, xt_evac.at(i, NCH))
                else:
                    pe.wait_ge(o_used.sem, o_used.at(i, c))
                for h in range(NH1):
                    if h % HB == 0:
                        pe.wait_ge(p_ready.sem, p_ready.at(i, 2 * c + 1 + h // HB))
                    last = mm(bank[4][:, DH1 * h:DH1 * h + DH1],
                              PB[:, (2 * c + h // HB) % 4, (h % HB) * L:(h % HB + 1) * L],
                              XD[:, c % 2, DH1 * h:DH1 * h + DH1], start=True, stop=True)
                last.then_inc(o_mm.sem, 1)

            def inter(c):
                pe.wait_ge(st_ready.sem, st_ready.at(i, c))
                if c >= 2:
                    pe.wait_ge(inter_used.sem, inter_used.at(i, c - 1))
                mm(bank[5][:, 0:INNER], CS[:, chunk(c)], ST[:, :], start=True, stop=True).then_inc(inter_mm.sem, 1)

            def by_channel(half):
                for g in range(G3):
                    w = half * G3 + g
                    pe.wait_ge(yn_ready.sem, yn_ready.at(i, 4 * half + 4))
                    if w == 0:
                        pe.wait_ge(gt_ready.sem, gt_ready.at(i, 2))
                    else:
                        pe.wait_ge(gT_evac.sem, gT_evac.at(i, w))
                    for cc in range(4):
                        last = nc.tensor.transpose(bank[7][:, cc * L:(cc + 1) * L],
                                                   YT[:, 4 * half + cc, 128 * g:128 * g + 128], ident)
                    last.then_inc(gT_mm.sem, 1)

            scores(0)
            for c in range(NCH):
                if c + 1 < NCH:
                    scores(c + 1)
                if c >= 1:
                    inter(c)
                if c < NCH - 1:
                    state(c)
                outputs(c)
                if c == 6:
                    by_channel(0)
            by_channel(1)
            pe.wait_ge(gT_evac.sem, gT_evac.at(i, 6))
            pe.wait_ge(p_ready.sem, p_ready.at(i, 2 * NCH))
            pe.wait_ge(x_exp.sem, x_exp.at(i, 2 * NCH))
            for w in range(4):
                m, n = w // 2, w % 2
                for c in range(G3):
                    last = mm(bank[w][0:CH, :], Wout[:, c, m * CH:(m + 1) * CH], GC[:, c, span(n)],
                              start=(c == 0), stop=(c == 2))
                last.then_inc(out_mm.sem, 1)

        over_images(pe, None, body, lambda i: body(i, rest=False))

    @block_ctx.scalar
    def _(act):
        A = nc.scalar.activation
        A(R[:, 0, 0:1], rows("A_log")[0:NH1, :], ACT.Exp).then_inc(setup.sem, 1)
        act.wait_ge(setup.sem, n_setup)

        def squares(i, src, dst):
            for n in range(NT):
                act.wait_ge(ln2["d"].sem, ln2["d"].at(i, n + 1))
                if n == 0:
                    if later(i):
                        act.wait_ge(stored.sem, stored.at(i - 1, 1))
                A(dst[:, :, span(n)], src[:, :, span(n)], ACT.Square).then_inc(ln2["sq"].sem, 1)

        def deviations(i, dst):
            for n in range(NT):
                act.wait_ge(ln2["var"].sem, ln2["var"].at(i, n + 1))
                A(dst[:, span(n)], bank[6 + n][0:CH, :], ACT.Ln, bias=eps[0:CH, 0:1]).then_inc(ln2["ln"].sem, 1)
            for n in range(NT):
                act.wait_ge(ln2["ln"].sem, ln2["ln"].at(i, n + 1))
                A(dst[:, span(n)], dst[:, span(n)], ACT.Exp, scale=-0.5).then_inc(ln2["rs"].sem, 1)

        def affine(i, buf, w, b):
            for n in range(NT):
                act.wait_ge(ln2["hn"].sem, ln2["hn"].at(i, n + 1))
                for c in range(2):
                    A(buf[:, c, span(n)], buf[:, c, span(n)], ACT.Identity,
                        bias=w96(b, c), scale=w96(w, c)).then_inc(ln2["h"].sem, 1)

        def body(i, rest=True):
            back = not is_first(i)
            if rest:
                act.wait_ge(y_loaded.sem, y_loaded.at(i, 1))
                for c in range(2):
                    A(Y0[:, c, :], Y0[:, c, :], ACT.Identity, bias=bns[:, c, 5:6], scale=bns[:, c, 4:5]).then_inc(y_scaled.sem, 1)
            if back:
                squares(i - 1, H2, SQ2)
                deviations(i - 1, RS2)
            if rest:
                for q in range(4):
                    act.wait_ge(ht_mm.sem, ht_mm.at(i, q + 1))
                    if q == 0:
                        if later(i):
                            act.wait_ge(u_stored.sem, u_stored.at(i - 1, 1))
                    A(HT[:, 2 * q:2 * q + 2, :], bank[4 + q % 2][:, 0:2 * C]
                      .rearrange("p (c n) -> p c n", c=2), ACT.Copy).then_inc(ht_evac.sem, 1)
            if back:
                affine(i - 1, H2, "norm2_w", "norm2_b")
                for w in range(6):
                    m, n = w // 2, w % 2
                    if later(i):
                        act.wait_ge(f1_mm.sem, f1_mm.at(i - 1, w + 1))
                    A(F[:, m, span(n)], bank[w % 4][:, :], ACT.Gelu, bias=w128("ffn_b1", m)).then_inc(f1_evac.sem, 1)
            if not rest:
                return
            for w in range(18):
                act.wait_ge(in_mm.sem, in_mm.at(i, w + 1))
                b = bank[w % 4]
                if w < 8:
                    A(XBC[:, w // 2, PAD + (w % 2) * 512:PAD + (w % 2 + 1) * 512], b[:, :], ACT.Copy).then_inc(in_evac.sem, 1)
                elif w < 10:
                    A(R[:, 0, span(w % 2)], b[0:NH1, :], ACT.Identity, bias=rows("dt_bias")[0:NH1, :]).then_inc(in_evac.sem, 1)
                else:
                    A(ZT[:, w - 10, :], b[:, 0:INNER], ACT.Silu).then_inc(in_evac.sem, 1)
            act.wait_ge(in_evac.sem, in_evac.at(i, 10))
            A(R[:, 1, :], R[:, 0, :], ACT.Abs).then_inc(own_a.sem, own_a.step())
            for g in (3, 0, 1, 2):
                act.wait_ge(conv_done.sem, conv_done.at(i, (3, 0, 1, 2).index(g) + 1))
                if g < 3:
                    A(CV[:, g, :], CV[:, g, :], ACT.Silu).then_inc(xs_ready.sem, 1)
                else:
                    A(BS[:, :], CV[0:NS, g, :], ACT.Silu).then_inc(xs_ready.sem, 1)
                    A(CS[:, :], CV[NS:2 * NS, g, :], ACT.Silu).then_inc(xs_ready.sem, 1)
            act.wait_ge(own_a.sem, own_a.value())
            A(R[:, 1, :], R[:, 1, :], ACT.Exp, scale=-1.0).then_inc(own_a.sem, own_a.step())
            act.wait_ge(own_a.sem, own_a.value())
            A(R[:, 1, :], R[:, 1, :], ACT.Ln, bias=1.0).then_inc(row_sp.sem, 1)
            for part in range(3):
                p = slice(32 * part, 32 * part + NH1)
                if part:
                    act.wait_ge(part_left.sem, part_left.at(i, part))
                else:
                    act.wait_ge(cu_ready.sem, cu_ready.at(i, 1))
                A(CU3[p, :], CU[p, :], ACT.Copy).then_inc(part_cast.sem, 1)
            A(GWD[64:64 + NH1, :], R[:, 0, :], ACT.Copy).then_inc(g_ready.sem, 1)
            A(GWD[0:NH1, :], CU[0:NH1, :], ACT.Exp).then_inc(g_ready.sem, 1)
            act.wait_ge(row_w.sem, row_w.at(i, 1))
            A(R[:, 1, :], R[:, 1, :], ACT.Exp).then_inc(row_we.sem, 1)
            for c in range(NCH):
                act.wait_ge(xt_mm.sem, xt_mm.at(i, c + 1))
                A(XT[:, c, :], bank[4 + c % 2][:, 0:KX], ACT.Copy).then_inc(xt_evac.sem, 1)

            def exps(c):
                for k in range(2):
                    j = 2 * c + k
                    act.wait_ge(e_mm.sem, e_mm.at(i, j + 1))
                    if j >= 2:
                        act.wait_ge(p_ready.sem, p_ready.at(i, j - 1))
                    A(XB[:, k, :], bank[2 + k][:, 0:HB * L], ACT.Exp).then_inc(x_exp.sem, 1)

            def square_sum(c):
                act.wait_ge(y_gated.sem, y_gated.at(i, c + 1))
                if c:
                    act.wait_ge(ss_ready.sem, ss_ready.at(i, c))
                A(JK[:, :], YT[:, c, :], ACT.Square, accum_out=SS[:, c:c + 1]).then_inc(ss_ready.sem, 1)

            def channels(half):
                for g in range(G3):
                    w = half * G3 + g
                    act.wait_ge(gT_mm.sem, gT_mm.at(i, w + 1))
                    A(GC[:, g, span(half)], bank[7][:, :], ACT.Copy).then_inc(gT_evac.sem, 1)

            exps(0)
            for c in range(NCH):
                if c + 1 < NCH:
                    exps(c + 1)
                if c >= 1:
                    square_sum(c - 1)
                if c == 6:
                    channels(0)
            square_sum(NCH - 1)
            channels(1)

        over_images(act, own_a, body, lambda i: body(i, rest=False))

    @block_ctx.vector
    def _(dve):
        V = nc.vector
        dve.wait_ge(loaded.sem, 6 * 16)
        for c in range(2):
            V.bn_aggr(bns[:, c, 0:2], bn[:, c, :]).then_inc(own_v.sem, own_v.step())
        dve.wait_ge(own_v.sem, own_v.value())
        V.tensor_scalar(bns[:, :, 2], bns[:, :, 1], GN_EPS, None, ALU.add).then_inc(own_v.sem, own_v.step())
        dve.wait_ge(own_v.sem, own_v.value())
        for g in range(G3):
            ins = V.tensor_scalar(Wout[:, g, :], Wout[:, g, :], w128("ssm_w", g), None, ALU.mult)
            ins.then_inc(*((own_v.sem, own_v.step()) if g else (setup.sem, 1)))
        V.tensor_copy(identb[:, :], ident).then_inc(setup.sem, 1)
        V.tensor_copy(maskb[:, :, :], cst("causal").unsqueeze(1).broadcast_to([128, HB, L])).then_inc(setup.sem, 1)
        V.tensor_copy(a_sel[:, :, :], sel[:, 0:NH1 * L].rearrange("p (g n) -> p g n", g=2)).then_inc(setup.sem, 1)
        dve.wait_ge(setup.sem, n_setup - 2)
        dve.wait_ge(setup.sem, n_setup - 1)
        V.tensor_copy(b_sel[:, :, :], sel[:, NH1 * L:].rearrange("p (g n) -> p g n", g=NH1)).then_inc(own_v.sem, own_v.step())
        V.tensor_scalar(rows("A_log")[0:NH1, :], R[:, 0, 0:1], -1.0, None, ALU.mult).then_inc(own_v.sem, own_v.step())
        V.tensor_tensor(bns[:, :, 4], bns[:, :, 3], shared["w96_pair"]("bn_g"), ALU.mult).then_inc(own_v.sem, own_v.step())
        dve.wait_ge(own_v.sem, own_v.value())
        V.tensor_tensor(bns[:, :, 3], bns[:, :, 0], bns[:, :, 4], ALU.mult).then_inc(own_v.sem, own_v.step())
        dve.wait_ge(own_v.sem, own_v.value())
        V.tensor_tensor(bns[:, :, 5], shared["w96_pair"]("bn_b"), bns[:, :, 3], ALU.subtract).then_inc(setup.sem, 1)
        dve.wait_ge(setup.sem, n_setup)

        def deviate(i, src, dst):
            for n in range(NT):
                dve.wait_ge(ln2["mean"].sem, ln2["mean"].at(i, n + 1))
                V.tensor_tensor(dst[:, :, span(n)], src[:, :, span(n)],
                                  bank[4 + n][0:CH, :].unsqueeze(1).broadcast_to([CH, 2, 512]),
                                  ALU.subtract).then_inc(ln2["d"].sem, 1)

        def scale(i, buf, rs):
            for n in range(NT):
                dve.wait_ge(ln2["rs"].sem, ln2["rs"].at(i, n + 1))
                V.tensor_tensor(buf[:, :, span(n)], buf[:, :, span(n)],
                                  rs[:, span(n)].unsqueeze(1).broadcast_to([CH, 2, 512]), ALU.mult).then_inc(ln2["hn"].sem, 1)

        def body(i, rest=True):
            back = not is_first(i)
            if back:
                deviate(i - 1, XF, H2)
            if rest:
                dve.wait_ge(y_scaled.sem, y_scaled.at(i, 2))
                V.scalar_tensor_tensor(Y0[:, :, :], Y0[:, :, :], 0.01, Y0[:, :, :], ALU.mult, ALU.max).then_inc(own_v.sem, own_v.step())
                dve.wait_ge(own_v.sem, own_v.value())
                dve.wait_ge(x_loaded.sem, x_loaded.at(i, 1))
                V.tensor_tensor(X1[:, :, :], Y0[:, :, :], X1[:, :, :], ALU.add).then_inc(x1_ready.sem, 1)
                dve.wait_ge(x1_ready.sem, x1_ready.at(i, 1))
                for c in range(2):
                    for n in range(NT):
                        V.bn_stats(gst[:, c, 6 * n:6 * n + 6], X1[:, c, span(n)]).then_inc(own_v.sem, own_v.step())
                dve.wait_ge(own_v.sem, own_v.value())
                V.memset(gs[:, 0, 3:4], 0.0).then_inc(own_v.sem, own_v.step())
                V.bn_aggr(gs[:, 0, 0:2], gst[:, 0, :]).then_inc(own_v.sem, own_v.step())
                V.bn_aggr(gs[:, 1, 0:2], gst[:, 1, :]).then_inc(gn_stats.sem, 1)
                dve.wait_ge(gn_mean.sem, gn_mean.at(i, 1))
                V.tensor_copy(gs[:, :, 6:8], bank[7][0:CH, 0:4].rearrange("p (c s) -> p c s", c=2)).then_inc(own_v.sem, own_v.step())
                dve.wait_ge(own_v.sem, own_v.value())
                V.tensor_tensor(gs[:, :, 2], gs[:, :, 0], gs[:, :, 6], ALU.subtract).then_inc(own_v.sem, own_v.step())
                dve.wait_ge(own_v.sem, own_v.value())
                V.tensor_tensor(gs[:, :, 2], gs[:, :, 2], gs[:, :, 2], ALU.mult).then_inc(gn_dev.sem, 1)
                dve.wait_ge(gn_var.sem, gn_var.at(i, 1))
                V.scalar_tensor_tensor(gs[:, :, 3], bank[7][0:CH, 8:10], GN_EPS, gs[:, :, 7],
                                       ALU.add, ALU.add).then_inc(gn_sum.sem, 1)
                dve.wait_ge(gn_rstd.sem, gn_rstd.at(i, 1))
                for c in range(2):
                    V.tensor_scalar(XG[:, c, :], X1[:, c, :], gs[:, c, 6:7], gs[:, c, 5:6],
                                    ALU.subtract, ALU.mult).then_inc(xg_ready.sem, 1)
            if back:
                scale(i - 1, H2, RS2)
            if rest:
                for c in range(NCH):
                    dve.wait_ge(ht_evac.sem, ht_evac.at(i, c // 2 + 1))
                    V.bn_stats(hst[:, c, :], HT[:, c, :]).then_inc(own_v.sem, own_v.step())
                dve.wait_ge(own_v.sem, own_v.value())
                V.memset(hmv[:, 0, 3:4], 0.0).then_inc(own_v.sem, own_v.step())
                for c in range(NCH):
                    V.bn_aggr(hmv[:, c, 0:2], hst[:, c, :]).then_inc(own_v.sem, own_v.step())
                dve.wait_ge(own_v.sem, own_v.value())
                V.tensor_scalar(hmv[:, :, 2], hmv[:, :, 1], GN_EPS, None, ALU.add).then_inc(hv_ready.sem, 1)
                for c in range(NCH):
                    V.scalar_tensor_tensor(HT[:, c, :], HT[:, c, :], hmv[:, c, 0:1], n1[:, 0, :],
                                           ALU.subtract, ALU.mult).then_inc(own_v.sem, own_v.step())
                dve.wait_ge(own_v.sem, own_v.value())
                dve.wait_ge(hr_ready.sem, hr_ready.at(i, 1))
                for c in range(NCH):
                    V.scalar_tensor_tensor(HT[:, c, :], HT[:, c, :], hmv[:, c, 3:4], n1[:, 1, :],
                                           ALU.mult, ALU.add).then_inc(ht_ready.sem, 1)
            if back:
                if later(i):
                    dve.wait_ge(xx_ready.sem, xx_ready.at(i - 1, 1))
                for w in range(4):
                    m, n = w // 2, w % 2
                    if later(i):
                        dve.wait_ge(f2_mm.sem, f2_mm.at(i - 1, w + 1))
                    if w == 0:
                        if later(i):
                            dve.wait_ge(ln2["var"].sem, ln2["var"].at(i - 1, 2))
                    V.scalar_tensor_tensor(OUT[:, m, span(n)], bank[(6 + w) % 4][0:CH, :],
                                           w96("ffn_b2", m), XX[:, m, span(n)], ALU.add, ALU.add).then_inc(out_ready.sem, 1)
            if not rest:
                return
            for k, g in enumerate((3, 0, 1, 2)):
                dve.wait_ge(in_evac.sem, in_evac.at(i, 2 * g + 2))
                if k == 0:
                    if later(i):
                        dve.wait_ge(xt_mm.sem, xt_mm.at(i - 1, NCH))
                V.tensor_scalar(CV[:, g, :], XBC[:, g, 0:T], w128("m_conv_w", 4 * g), w128("m_conv_b", g),
                                ALU.mult, ALU.add).then_inc(own_v.sem, own_v.step())
                for t in range(1, TAPS):
                    dve.wait_ge(own_v.sem, own_v.value())
                    ins = V.scalar_tensor_tensor(
                        CV[:, g, :], XBC[:, g, t:t + T], w128("m_conv_w", 4 * g + t), CV[:, g, :], ALU.mult, ALU.add)
                    if t == TAPS - 1:
                        ins.then_inc(conv_done.sem, 1)
                    else:
                        ins.then_inc(own_v.sem, own_v.step())
            dve.wait_ge(row_sp.sem, row_sp.at(i, 1))
            V.scalar_tensor_tensor(R[:, 0, :], R[:, 0, :], 0.0, R[:, 1, :], ALU.max, ALU.add).then_inc(own_v.sem, own_v.step())
            dve.wait_ge(own_v.sem, own_v.value())
            V.tensor_scalar(R[:, 1, :], R[:, 0, :], rows("A_log")[0:NH1, :], None, ALU.mult).then_inc(own_v.sem, own_v.step())
            dve.wait_ge(own_v.sem, own_v.value())
            V.tensor_tensor_scan(CU[0:NH1, :], reset, R[:, 1, :], 0.0, ALU.mult, ALU.add).then_inc(cu_ready.sem, 1)
            dve.wait_ge(cu_ready.sem, cu_ready.at(i, 1))
            by_chunk = lambda ap: ap.rearrange("p (c l) -> p c l", l=L)
            V.scalar_tensor_tensor(by_chunk(R[:, 1, :]), by_chunk(CU[0:NH1, :]), -1.0,
                                   CU[0:NH1, L - 1::L].unsqueeze(2).broadcast_to([NH1, NCH, L]),
                                   ALU.mult, ALU.add).then_inc(row_w.sem, 1)
            for part in range(2):
                p, q = slice(32 * part, 32 * part + NH1), slice(32 * part + 32, 32 * part + 32 + NH1)
                dve.wait_ge(part_cast.sem, part_cast.at(i, part + 1))
                V.tensor_tensor(CU[q, :], CU[p, :], CU3[p, :], ALU.subtract).then_inc(part_left.sem, 1)
            dve.wait_ge(g_ready.sem, g_ready.at(i, 2))
            V.tensor_tensor(DG[:, :, :], GWD[0:NH1, L - 1::L].unsqueeze(2).broadcast_to([NH1, NCH, NH1]),
                            ident[0:NH1, 0:NH1].unsqueeze(1).broadcast_to([NH1, NCH, NH1]), ALU.mult).then_inc(dg_ready.sem, 1)
            dve.wait_ge(row_we.sem, row_we.at(i, 1))
            V.tensor_tensor(GWD[32:32 + NH1, :], R[:, 1, :], R[:, 0, :], ALU.mult).then_inc(w_ready.sem, 1)
            dve.wait_ge(gw_mm.sem, gw_mm.at(i, 2))
            V.tensor_copy(GT[:, :, :], bank[6][:, 0:18 * NCH].rearrange("p (c n) -> p c n", c=NCH)).then_inc(gt_ready.sem, 1)
            V.tensor_copy(DEC[:, :, :], bank[7][0:NS, 0:NH1 * NCH].rearrange("p (c n) -> p c n", c=NCH)).then_inc(gt_ready.sem, 1)

            def weigh(c):
                for k in range(2):
                    j = 2 * c + k
                    dve.wait_ge(x_exp.sem, x_exp.at(i, j + 1))
                    if j >= 4:
                        dve.wait_ge(o_mm.sem, o_mm.at(i, c - 1))
                    V.tensor_tensor(PB[:, j % 4, :].rearrange("p (h t) -> p h t", t=L),
                                    XB[:, k, :].rearrange("p (h t) -> p h t", t=L),
                                    bank[c % 2][:, 0:L].unsqueeze(1).broadcast_to([128, HB, L]), ALU.mult).then_inc(p_ready.sem, 1)

            def state(c):
                dve.wait_ge(state_mm.sem, state_mm.at(i, c + 1))
                if c == 0:
                    if later(i):
                        dve.wait_ge(inter_mm.sem, inter_mm.at(i - 1, NCH - 1))
                    V.tensor_copy(ST[:, :], bank[6][0:NS, 0:INNER]).then_inc(st_ready.sem, 1)
                    return
                dve.wait_ge(inter_mm.sem, inter_mm.at(i, c))
                dve.wait_ge(st_ready.sem, st_ready.at(i, c))
                V.tensor_tensor(heads(ST[:, :]), heads(ST[:, :]),
                                DEC[:, c, :].unsqueeze(2).broadcast_to([NS, NH1, DH1]), ALU.mult).then_inc(own_v.sem, own_v.step())
                dve.wait_ge(own_v.sem, own_v.value())
                V.tensor_tensor(ST[:, :], ST[:, :], bank[6][0:NS, 0:INNER], ALU.add).then_inc(st_ready.sem, 1)

            def total(c):
                if c:
                    dve.wait_ge(inter_mm.sem, inter_mm.at(i, c))
                    V.tensor_tensor(heads(TI[:, :]), heads(bank[5][:, 0:INNER]),
                                    GT[:, c, 0:6].unsqueeze(2).broadcast_to([128, NH1, DH1]), ALU.mult).then_inc(inter_used.sem, 1)
                dve.wait_ge(o_mm.sem, o_mm.at(i, c + 1))
                if c == 0:
                    dve.wait_ge(xu_ready.sem, xu_ready.at(i, 1))
                    V.tensor_tensor(YT[:, c, :], bank[4][:, 0:INNER], XT[:, c, 0:INNER], ALU.add).then_inc(o_used.sem, 1)
                    dve.wait_ge(o_used.sem, o_used.at(i, 1))
                else:
                    dve.wait_ge(inter_used.sem, inter_used.at(i, c))
                    V.tensor_tensor(YT[:, c, :], bank[4][:, 0:INNER], TI[:, :], ALU.add).then_inc(o_used.sem, 1)
                    dve.wait_ge(o_used.sem, o_used.at(i, c + 1))
                    dve.wait_ge(xu_ready.sem, xu_ready.at(i, c + 1))
                    V.tensor_tensor(YT[:, c, :], YT[:, c, :], XT[:, c, 0:INNER], ALU.add).then_inc(own_v.sem, own_v.step())
                    dve.wait_ge(own_v.sem, own_v.value())
                V.tensor_tensor(YT[:, c, :], YT[:, c, :], ZT[:, c, :], ALU.mult).then_inc(y_gated.sem, 1)

            def mean_square(half):
                dve.wait_ge(ss_ready.sem, ss_ready.at(i, 4 * half + 4))
                h = slice(4 * half, 4 * half + 4)
                V.tensor_scalar(SS[:, h], SS[:, h], 1.0 / INNER, 1e-5, ALU.mult, ALU.add).then_inc(ms_ready.sem, 1)

            def normalise(half):
                dve.wait_ge(rr_ready.sem, rr_ready.at(i, half + 1))
                for c in range(4 * half, 4 * half + 4):
                    V.tensor_scalar(YT[:, c, :], YT[:, c, :], RR[:, c:c + 1], None, ALU.mult).then_inc(yn_ready.sem, 1)

            weigh(0)
            for c in range(NCH):
                if c < NCH - 1:
                    state(c)
                if c + 1 < NCH:
                    weigh(c + 1)
                total(c)
                if c == 4:
                    mean_square(0)
                if c == 6:
                    normalise(0)
            mean_square(1)
            normalise(1)
            if later(i):
                dve.wait_ge(ln2["mean"].sem, ln2["mean"].at(i - 1, 2))
            for w in range(4):
                m, n = w // 2, w % 2
                dve.wait_ge(out_mm.sem, out_mm.at(i, w + 1))
                V.tensor_tensor(XF[:, m, span(n)], bank[w][0:CH, :], XG[:, m, span(n)], ALU.add).then_inc(xf_ready.sem, 1)

        over_images(dve, own_v, body, lambda i: body(i, rest=False))


def program(nc, d, out):
    with ExitStack() as ctx:
        def sb(name, shape, dt=F32):
            return ctx.enter_context(nc.sbuf_tensor(name, shape, dt))

        bank = [ctx.enter_context(nc.psum_tensor(f"bank{n}", [128, 512], F32)) for n in range(8)]
        w96, w128, rows, consts = (sb("col96", [CH, W96]), sb("col128", [128, W128]), sb("rows_sb", [12, 4]),
                                   sb("consts_sb", [128, WC]))
        shared = {
            "bank": bank, "consts": consts, "eps": sb("eps", [128, 2]), "bn": sb("bn", [CH, 2, B * 12]),
            "w96_sb": w96, "w128_sb": w128, "rows_sb": rows, "n_setup0": 21,
            "setup_done": Signal(ctx.enter_context(nc.semaphore("setup_done")), 0),
            "w96": lambda n, c: w96[:, AT96[n][0] + c:AT96[n][0] + c + 1],
            "w96_pair": lambda n: w96[:, AT96[n][0]:AT96[n][1]],
            "w128": lambda n, c, k=1: w128[:, AT128[n][0] + c:AT128[n][0] + c + k],
            "rows": lambda n: rows[:, ROWS.index(n):ROWS.index(n) + 1],
            "cst": lambda n: consts[:, ATC[n][0]:ATC[n][1]],
        }
        d["yc"] = nc.dram_tensor("yc", (B, CH, 2 * T), F32, kind=d.get("yc_kind", "Internal")).ap()
        d["u"] = nc.dram_tensor("u", (B, C * T), F32, kind="Internal").ap()
        with ExitStack() as ctx0:
            layer0(nc, ctx0, d, shared)
        if "yc_kind" not in d:
            with ExitStack() as ctx1:
                layer1(nc, ctx1, d, shared, out)


def constants():
    import numpy as np

    c = {n: np.zeros((128, w), np.float32) for n, w in (CONSTS | SELECT).items()}
    c["ident"][:] = np.eye(128)
    s, t = np.arange(128)[:, None], np.arange(L)[None, :]
    c["causal"][:] = np.where(s <= t, 0.0, -1e30)
    v = c["block"].reshape(128, HG, V0)
    for h in range(HG):
        v[DH0 * h:DH0 * h + DH0, h] = 1.0
    size = C // 32
    for p in range(CH):
        c["group"][p, p // size * size:p // size * size + size] = 1.0 / size
    c["mean"][:CH] = 1.0 / C
    e = c["expand"].reshape(128, G3, 128)
    a0, b0 = c["a_sel0"].reshape(128, G3, HG, L), c["b_sel0"].reshape(128, NH0, 128)
    for h in range(NH0):
        e[h, h // HG, DH0 * (h % HG):DH0 * (h % HG) + DH0] = 1.0
        for part in range(3):
            a0[32 * part + h, h // HG, h % HG] = 1.0
            b0[32 * part + h, h] = 1.0
    a1, b1 = c["a_sel1"].reshape(128, NH1, L), c["b_sel1"].reshape(128, NH1, 128)
    for h in range(NH1):
        for part in range(3):
            c["pick1"][32 * part + h, NH1 * part + h] = 1.0
            a1[32 * part + h, h] = -1.0
            b1[32 * part + h, h] = 1.0
    c["reset"][:] = 1.0
    c["reset"][:, ::L] = 0.0
    return np.concatenate([c[n] for n in CONSTS], 1), np.concatenate([c[n] for n in SELECT], 1)


def laid_out(q):
    import numpy as np

    a = {k: np.asarray(v) for k, v in q.items()}
    f = np.float32
    L0, L1 = (lambda n: a["L0_conv_" + n]), (lambda n: a["L1_conv_" + n])
    col = lambda v, p: v.reshape(-1, p).T
    src96 = {"ln_w": L0("ln_w"), "ln_b": L0("ln_b"), "b_lin": L0("b_lin"), "b_down": L0("b_down"),
             "conv2_b": L0("conv2_b"), "bn_g": L0("bn_g"), "bn_b": L0("bn_b"), "norm1_w": L1("norm1_w"),
             "norm1_b": L1("norm1_b"), "norm2_w": L1("norm2_w"), "norm2_b": L1("norm2_b"), "ffn_b2": L1("ffn_b2")}
    taps = lambda v: v.reshape(-1, 128, TAPS).transpose(1, 0, 2).reshape(128, -1)
    src128 = {"b_up": col(L0("b_up"), 128), "conv_k": taps(L0("conv_k")), "conv_b": col(L0("conv_b"), 128),
              "skip": col(L0("skip"), 128), "mh_w": col(L0("mh_w"), 128), "mh_b": col(L0("mh_b"), 128),
              "m_conv_w": taps(L1("conv_w")), "m_conv_b": col(L1("conv_b"), 128), "ssm_w": col(L1("ssm_norm_w"), 128),
              "ffn_b1": col(L1("ffn_b1"), 128), "D": np.broadcast_to(L1("D_skip")[None, :], (128, NH1))}
    rows = np.zeros((12, 4), f)
    rows[:, 0], rows[:, 1] = L0("b_i"), L0("b_f")
    rows[:NH1, 2], rows[:NH1, 3] = L1("dt_bias"), L1("A_log")
    gate = np.zeros((3 * INNER, 44), f)
    gate[:, 0:12], gate[:, 32:44] = L0("w_i"), L0("w_f")
    return {
        "x": a["x"], "w_up": L0("w_up"), "w_q": L0("w_q"), "w_k": L0("w_k"),
        "w_qk_t": np.concatenate([L0("w_q").T, L0("w_k").T]), "w_gate": gate, "w_down": L0("w_down"),
        "w_lin": L0("w_lin"), "w_c3": L0("conv2_w").transpose(1, 2, 3, 0).reshape(C, 9, C),
        "w_in": L1("in_proj_w").T, "w_out": L1("out_proj_w").T, "w_f1": L1("ffn_w1").T, "w_f2": L1("ffn_w2").T,
        "col96": np.concatenate([col(src96[n], CH) for n in COL96], 1),
        "col128": np.concatenate([src128[n] for n in COL128], 1), "rows": rows,
        "norm1": np.broadcast_to(np.concatenate([L1("norm1_w"), L1("norm1_b")])[None, :], (128, 2 * C)),
        "consts": constants()[0], "select": constants()[1],
    }


def kernel(**inputs):
    import concourse.bacc as _bacc
    import numpy as _np
    from concourse import mybir as _mybir
    from concourse.bass_utils import run_bass_kernel_spmd as _run

    nc = _bacc.Bacc("TRN2", target_bir_lowering=False, num_devices=1)
    arrays, d = {}, {}
    for name, a in laid_out(inputs).items():
        a = _np.ascontiguousarray(a)
        arrays[f"in_{name}"] = a
        d[name] = nc.dram_tensor(f"in_{name}", a.shape, _mybir.dt.from_np(a.dtype), kind="ExternalInput").ap()
    out = nc.dram_tensor("out_0", inputs["x"].shape, _mybir.dt.float32, kind="ExternalOutput").ap()
    program(nc, d, out)
    r = _run(nc, [arrays], core_ids=[0])
    return r.results[0]["out_0"]
```

```python
from contextlib import ExitStack

import concourse.bass as bass
from concourse import mybir

F32 = mybir.dt.float32
BF16 = mybir.dt.bfloat16
ALU = mybir.AluOpType
ACT = mybir.ActivationFunctionType
AX = mybir.AxisListType.X

B, C, HW = 16, 192, 32
T = HW * HW
CH = C // 2
INNER = 2 * C
G3 = INNER // 128
NT = T // 512
L = 128
NCH = T // L
TAPS = 4
PAD = TAPS - 1
GN_EPS = 1e-5

NH0, DH0 = 12, 32
V0 = DH0 + 1
HG = 128 // DH0

NORM = [(0, 1), (1, 2), (2, 3), (3, 4), (4, 6), (6, 8)]

NH1, DH1, NS = 6, 64, 64
HB = NH1 // 2

COL96 = ["ln_w", "ln_b", "b_lin", "b_down", "conv2_b", "bn_g", "bn_b",
         "norm1_w", "norm1_b", "norm2_w", "norm2_b", "ffn_b2"]
COL128 = {"b_up": 6, "conv_k": 12, "conv_b": 3, "skip": 3, "mh_w": 3, "mh_b": 3,
          "m_conv_w": 16, "m_conv_b": 4, "ssm_w": 3, "ffn_b1": 3, "D": 6}
ROWS = ["b_i", "b_f", "dt_bias", "A_log"]
CONSTS = {"ident": 128, "causal": 128, "block": 4 * V0, "group": CH, "mean": CH, "expand": 3 * 128,
          "pick1": 3 * NH1, "reset": T}
SELECT = {"a_sel0": 3 * 512, "b_sel0": NH0 * 128, "a_sel1": NH1 * L, "b_sel1": NH1 * 128}


def offsets(widths):
    at, out = 0, {}
    for name, w in widths.items():
        out[name] = (at, at + w)
        at += w
    return out, at


AT96, W96 = offsets({n: 2 for n in COL96})
AT128, W128 = offsets(COL128)
ATC, WC = offsets(CONSTS)
ATS, WS = offsets(SELECT)


class Signal:

    def __init__(self, sem, per_image, unit=1):
        self.sem, self.per_image, self.unit = sem, per_image, unit

    def at(self, image, count):
        return (image * self.per_image + count) * self.unit


def later(image):
    return not (isinstance(image, int) and image == 0)


class Own:

    def __init__(self, sem):
        self.sem, self.count, self.per_image, self.image, self.before = sem, 0, 0, 0, 0

    def start(self, image):
        if isinstance(image, int) and image == 0:
            self.before = self.count
            self.count = 0
            return
        assert self.per_image in (0, self.count)
        self.per_image = self.count
        self.image, self.count = image, 0

    def step(self):
        self.count += 1
        return 1

    def value(self):
        return self.before + self.image * self.per_image + self.count


def over_images(eng, own, body, after=None, first=2):
    for i in range(first):
        if own:
            own.start(i)
        body(i)
    with eng.Fori(first, B) as i:
        if own:
            own.start(i)
        body(i)
    if after:
        if own:
            own.start(B)
        after(B)


def layer0(nc, ctx, d, shared):
    def sb(name, shape, dt=F32):
        return ctx.enter_context(nc.sbuf_tensor(name, shape, dt))

    def signal(name, per_image, unit=1):
        return Signal(ctx.enter_context(nc.semaphore(name)), per_image, unit)

    bank = shared["bank"]
    w96, w128, rows, cst, eps = (shared[k] for k in ("w96", "w128", "rows", "cst", "eps"))
    bn = shared["bn"]
    setup_loaded = signal("setup_loaded", 0, 16)
    setup_done = shared["setup_done"]
    fold_mm = signal("fold_mm", 0)

    Wup = sb("Wup", [CH, 2, 2 * INNER])
    Wq = sb("Wq", [128, G3, INNER])
    Wk = sb("Wk", [128, G3, INNER])
    Wg = sb("Wg", [128, 3 * G3, 44])
    Wdown = sb("Wdown", [128, G3, C])
    Wlin = sb("Wlin", [CH, 2, C])
    Wc3 = sb("Wc3", [128, 9 + 6, C])
    X = sb("X", [CH, 2, T])
    XG = sb("XG", [CH, 2, T])
    gs = sb("gs", [CH, 2, 8])
    gst = sb("gst", [CH, 2, 12])
    arena = sb("arena", [128, NCH * NH0 * V0 + 2 * (NCH // 2) * INNER])
    w_num, w_dd = NCH * NH0 * V0, NCH // 2 * INNER
    SQ = arena[0:CH, 0:2 * T].rearrange("p (c t) -> p c t", c=2)
    RS = arena[0:CH, 2 * T:3 * T]
    H = arena[0:CH, w_num:w_num + 2 * T].rearrange("p (c t) -> p c t", c=2)
    XIN = arena[:, 0:G3 * (PAD + T)].rearrange("p (g t) -> p g t", g=G3)
    R = arena[0:12, 0:4 * T].rearrange("p (r t) -> p r t", r=4)
    GW = arena[0:44, 4 * T:5 * T]
    MX = arena[0:12, 5 * T:6 * T + 1]
    NUM = arena[:, 0:w_num].rearrange("p (c n) -> p c n", c=NCH)
    DD = arena[:, w_num:w_num + w_dd].rearrange("p (c n) -> p c n", c=NCH // 2)
    WT = arena[:, ATS["b_sel0"][1]:ATS["b_sel0"][1] + 2 * G3 * INNER].rearrange("p (c n) -> p c n", c=2 * G3)
    SQB = arena[:, w_num + w_dd:w_num + 2 * w_dd]
    pair = sb("pair", [128, 4, 512])
    AB = pair[0:96, :, :].rearrange("p (r x) t -> p r (x t)", r=2)
    XB, PB = pair[:, 0:2, :], pair[:, 2:4, :]
    ZS = sb("ZS", [128, G3, T])
    XA = sb("XA", [128, G3, T])
    X2 = sb("X2", [CH, 2, T])
    Q = sb("Q", [128, G3, T])
    K = sb("K", [128, G3, T])
    KT = sb("KT", [128, 2, INNER])
    VE = sb("VE", [128, NCH, NH0 * V0])
    QBD = sb("QBD", [128, 2, HG, L])
    AB3 = sb("AB3", [96, 2, T], BF16)
    GT = sb("GT", [128, NCH, 2 * NH0])
    DEC = sb("DEC", [128, G3, NCH])
    ST = sb("ST", [128, HG * V0 * G3])
    TI = sb("TI", [128, NH0 * V0])
    TC = sb("TC", [128, NH0 * V0])
    sm = sb("sm", [128, 4, NCH * NH0])
    TZ = sb("TZ", [128, 512])
    YP = sb("YP", [128, 2, HW + 2, HW + 2])
    YC = sb("YC", [CH, 2, T])
    identb = sb("identb", [128, 128], BF16)
    maskb = sb("maskb", [128, HG, L], BF16)
    a_sel = sb("a_sel", [96, G3, HG * L], BF16)
    b_sel = sb("b_sel", [96, NH0, 128], BF16)

    ident, block, group, mean_w = (cst(n) for n in ("ident", "block", "group", "mean"))
    block_all = block.unsqueeze(1).broadcast_to([128, G3, HG * V0])
    expand = cst("expand")[0:12, :].rearrange("p (g m) -> p g m", g=G3)
    reset = cst("reset")[0:12, :]

    x_loaded = signal("x_loaded", 1, 16)
    gn_stats = signal("gn_stats", 1)
    gn_mean = signal("gn_mean", 1)
    gn_dev = signal("gn_dev", 1)
    gn_var = signal("gn_var", 1)
    gn_sum = signal("gn_sum", 1)
    gn_rstd = signal("gn_rstd", 1)
    xg_ready = signal("xg_ready", 2)
    xsum_ready = signal("xsum_ready", 2)
    mean_mm = signal("mean_mm", 2)
    d_ready = signal("d_ready", 2)
    sq_ready = signal("sq_ready", 2)
    sqsum_ready = signal("sqsum_ready", 2)
    var_mm = signal("var_mm", 2)
    rs_ready = signal("rs_ready", 2)
    hn_ready = signal("hn_ready", 2)
    h_ready = signal("h_ready", 4)
    up_mm = signal("up_mm", 16)
    up_evac = signal("up_evac", 16)
    vt_mm = signal("vt_mm", NCH)
    vt_evac = signal("vt_evac", NCH)
    conv_done = signal("conv_done", G3)
    xa_ready = signal("xa_ready", G3)
    qk_mm = signal("qk_mm", 12)
    q_evac = signal("q_evac", 6)
    k_evac = signal("k_evac", 6)
    u_ready = signal("u_ready", G3)
    rx_ready = signal("rx_ready", 1)
    gate_mm = signal("gate_mm", 2)
    gate_evac = signal("gate_evac", 1)
    row_i = signal("row_i", 1)
    row_ab = signal("row_ab", 2)
    row_gx = signal("row_gx", 1)
    part_cast = signal("part_cast", 3)
    part_left = signal("part_left", 2)
    gw_ready = signal("gw_ready", 2)
    gw_mm = signal("gw_mm", 3)
    gt_ready = signal("gt_ready", 3)
    kt_mm = signal("kt_mm", NCH - 1)
    kt_evac = signal("kt_evac", NCH - 1)
    kw_ready = signal("kw_ready", NCH - 1)
    qbd_ready = signal("qbd_ready", G3 * NCH)
    se_mm = signal("se_mm", G3 * NCH)
    x_exp = signal("x_exp", G3 * NCH)
    p_ready = signal("p_ready", G3 * NCH)
    o_mm = signal("o_mm", G3 * NCH)
    inter_mm = signal("inter_mm", NCH - 1)
    inter_used = signal("inter_used", NCH - 1)
    state_mm = signal("state_mm", NCH - 1)
    state_used = signal("state_used", NCH - 1)
    st_ready = signal("st_ready", NCH - 1)
    num_done = signal("num_done", NCH)
    dd_ready = signal("dd_ready", len(NORM))
    dsq_ready = signal("dsq_ready", len(NORM))
    arg_ready = signal("arg_ready", len(NORM))
    rho_ready = signal("rho_ready", len(NORM))
    hn_tok = signal("hn_tok", len(NORM))
    hT_mm = signal("hT_mm", 6)
    hT_evac = signal("hT_evac", 6)
    ho_ready = signal("ho_ready", 6)
    down_mm = signal("down_mm", 4)
    y_done = signal("y_done", 6)
    y_shifted = signal("y_shifted", 2)
    c3_mm = signal("c3_mm", 4)
    c3_evac = signal("c3_evac", 4)
    bn_done = signal("bn_done", 4)
    yc_stored = signal("yc_stored", 2, 16)
    own_v = Own(ctx.enter_context(nc.semaphore("vector_own")))
    own_a = Own(ctx.enter_context(nc.semaphore("scalar_own")))

    block_ctx = ctx.enter_context(nc.Block())
    x_in = d["x"].rearrange("b (c p) h w -> b p c (h w)", p=CH)
    yc_out = d["yc"].rearrange("b p (c t) -> b p c t", c=2)
    span = lambda n: slice(n * 512, (n + 1) * 512)
    chunk = lambda c: slice(c * L, (c + 1) * L)
    heads = lambda ap, w: ap.rearrange("p (h v) -> p h v", v=w)

    in_half = lambda k: slice(NORM[k][0] % 4 * INNER, (NORM[k][1] - NORM[k][0] // 4 * 4) * INNER)
    hT_bank = (7, 7, 7, 7, 4, 5)

    @block_ctx.sync
    def _(sp):
        loads = [
            (Wup[:, :, :], d["w_up"].rearrange("(c p) n -> p c n", p=CH)),
            (Wlin[:, :, :], d["w_lin"].rearrange("(c p) n -> p c n", p=CH)),
            (Wq[:, :, :], d["w_q"].rearrange("(c p) n -> p c n", p=128)),
            (Wk[:, :, :], d["w_k"].rearrange("(c p) n -> p c n", p=128)),
            (Wg[:, :, :], d["w_gate"].rearrange("(c p) n -> p c n", p=128)),
            (Wdown[:, :, :], d["w_down"].rearrange("(c p) n -> p c n", p=128)),
            (Wc3[:, :, :], d["w_c3"]),
            (shared["w96_sb"][:, :], d["col96"]), (shared["w128_sb"][:, :], d["col128"]),
            (shared["rows_sb"][:, :], d["rows"]), (shared["consts"][:, :], d["consts"]),
            (arena[:, 0:ATS["b_sel0"][1]], d["select"][:, 0:ATS["b_sel0"][1]]),
            (WT, d["w_qk_t"].rearrange("(c p) n -> p c n", p=128)),
        ]
        for dst, src in loads:
            sp.dma_start(dst, src).then_inc(setup_loaded.sem, 16)
        assert len(loads) == 13

        def store(i):
            for m in range(2):
                sp.wait_ge(c3_evac.sem, c3_evac.at(i, 2 * m + 2))
                sp.dma_start(yc_out[i][:, m, :], YC[:, m, :]).then_inc(yc_stored.sem, 16)

        def body(i):
            if later(i):
                sp.wait_ge(xg_ready.sem, xg_ready.at(i - 1, 2))
            sp.dma_start(X[:, :, :], x_in[i]).then_inc(x_loaded.sem, 16)
            if not (isinstance(i, int) and i == 0):
                store(i - 1)

        over_images(sp, None, body, lambda i: store(i - 1))
        sp.wait_ge(yc_stored.sem, yc_stored.at(B - 1, 2))

    @block_ctx.gpsimd
    def _(pool):
        for ap in (AB3[:, :, :], YP[:, :, :, :]):
            pool.memset(ap, 0.0).then_inc(setup_done.sem, 1)
        for h in range(NH0):
            pool.memset(VE[:, :, h * V0 + DH0:h * V0 + V0], 1.0).then_inc(setup_done.sem, 1)
        pool.memset(eps[:, 0:1], GN_EPS).then_inc(setup_done.sem, 1)
        pool.memset(eps[:, 1:2], -0.5).then_inc(setup_done.sem, 1)
        pool.wait_ge(setup_loaded.sem, 13 * 16)
        pool.wait_ge(setup_done.sem, shared["n_setup0"])

        rsqrt = lambda out, x: nc.gpsimd.tensor_tensor(
            out, x, eps[0:x.shape[0], 1:2].broadcast_to(list(x.shape)), ALU.pow)

        def body(i):
            pool.wait_ge(gn_sum.sem, gn_sum.at(i, 1))
            rsqrt(gs[:, :, 5], gs[:, :, 3]).then_inc(gn_rstd.sem, 1)
            pool.wait_ge(up_evac.sem, up_evac.at(i, 16))
            nc.gpsimd.tensor_tensor(X2[:, :, :], X2[:, :, :], XG[:, :, :], ALU.add).then_inc(rx_ready.sem, 1)

            def reciprocal(k):
                pool.wait_ge(arg_ready.sem, arg_ready.at(i, k + 1))
                rsqrt(sm[:, 3, NORM[k][0] * NH0:NORM[k][1] * NH0],
                      sm[:, 2, NORM[k][0] * NH0:NORM[k][1] * NH0]).then_inc(rho_ready.sem, 1)

            pool.wait_ge(q_evac.sem, q_evac.at(i, 6))
            for c in range(NCH):
                for g in range(G3):
                    j = G3 * c + g
                    if j >= 2:
                        pool.wait_ge(se_mm.sem, se_mm.at(i, j - 1))
                    else:
                        if later(i):
                            pool.wait_ge(se_mm.sem, se_mm.at(i - 1, G3 * NCH - 1 + j))
                    nc.gpsimd.tensor_tensor(
                        QBD[:, j % 2, :, :], Q[:, g, chunk(c)].unsqueeze(1).broadcast_to([128, HG, L]),
                        block[:, ::V0].unsqueeze(2).broadcast_to([128, HG, L]), ALU.mult).then_inc(qbd_ready.sem, 1)
                if c < NCH - 1:
                    pool.wait_ge(kt_evac.sem, kt_evac.at(i, c + 1))
                    pool.wait_ge(gt_ready.sem, gt_ready.at(i, 3))
                    k = heads(KT[:, c % 2, :], DH0)
                    nc.gpsimd.tensor_tensor(
                        k, k, GT[:, c, NH0:2 * NH0].unsqueeze(2).broadcast_to([128, NH0, DH0]), ALU.mult).then_inc(kw_ready.sem, 1)
                if c < G3:
                    nc.gpsimd.tensor_scalar(XA[:, c, :], XA[:, c, :], w128("skip", c), w128("mh_b", c),
                                            ALU.mult, ALU.add).then_inc(u_ready.sem, 1)
                if 2 <= c <= 5:
                    reciprocal(c - 2)
            reciprocal(4)
            reciprocal(5)

        over_images(pool, None, body)

    @block_ctx.tensor
    def _(pe):
        mm = nc.tensor.matmul
        pe.wait_ge(setup_loaded.sem, 13 * 16)
        for c in range(G3):
            for k in range(2 * G3):
                last = mm(bank[0][:, 44 * c:44 * c + 44], WT[:, k, c * 128:(c + 1) * 128], Wg[:, k, :],
                          start=(k == 0), stop=(k == 2 * G3 - 1))
        last.then_inc(fold_mm.sem, 1)
        pe.wait_ge(setup_done.sem, shared["n_setup0"])

        def conv3(i, g, part):
            m, n = g // 2, g % 2
            if g == 0 and part == 0:
                pe.wait_ge(y_done.sem, y_done.at(i, 6))
            if g == 0 and part == 1:
                pe.wait_ge(y_shifted.sem, y_shifted.at(i, 2))
            view = lambda rows, c, k: YP[0:rows, c, n * 16 + k // 3:n * 16 + k // 3 + 16, k % 3:k % 3 + HW]
            if part == 0:
                for k in range(9):
                    mm(bank[g][0:CH, :], Wc3[:, k, m * CH:(m + 1) * CH], view(128, 0, k), start=(k == 0), stop=False)
            else:
                for r in range(3):
                    mm(bank[g][0:CH, :], Wc3[:, 9 + 2 * r, m * CH:(m + 1) * CH], view(128, 1, 3 * r), start=False, stop=False)
                    last = mm(bank[g][0:CH, :], Wc3[0:64, 10 + 2 * r, m * CH:(m + 1) * CH], view(64, 1, 3 * r + 2),
                              start=False, stop=(r == 2))
            if part == 1:
                last.then_inc(c3_mm.sem, 1)

        def body(i, conv=True, rest=True):
            has_conv = conv and not (isinstance(i, int) and i == 0)
            if has_conv:
                conv3(i - 1, 0, 0)
            if rest:
                pe.wait_ge(gn_stats.sem, gn_stats.at(i, 1))
                if later(i):
                    pe.wait_ge(hT_evac.sem, hT_evac.at(i - 1, 6))
                mm(bank[6][0:CH, 0:4], group[0:CH, :], gs[:, :, 0:2], start=True, stop=True).then_inc(gn_mean.sem, 1)
            if has_conv:
                conv3(i - 1, 0, 1)
            if rest:
                pe.wait_ge(gn_dev.sem, gn_dev.at(i, 1))
                mm(bank[6][0:CH, 8:10], group[0:CH, :], gs[:, :, 2], start=True, stop=True).then_inc(gn_var.sem, 1)
            if has_conv:
                conv3(i - 1, 1, 0)
            if rest:
                for n in range(NT):
                    pe.wait_ge(xsum_ready.sem, xsum_ready.at(i, n + 1))
                    mm(bank[4 + n][0:CH, :], mean_w[0:CH, :], RS[:, span(n)], start=True, stop=True).then_inc(mean_mm.sem, 1)
            if has_conv:
                conv3(i - 1, 1, 1)
            if not rest:
                conv3(i - 1, 2, 0), conv3(i - 1, 2, 1), conv3(i - 1, 3, 0), conv3(i - 1, 3, 1)
                return
            for n in range(NT):
                pe.wait_ge(sqsum_ready.sem, sqsum_ready.at(i, n + 1))
                if n == 0:
                    pe.wait_ge(gn_rstd.sem, gn_rstd.at(i, 1))
                mm(bank[6 + n][0:CH, :], mean_w[0:CH, :], SQ[:, 0, span(n)], start=True, stop=True).then_inc(var_mm.sem, 1)
            if has_conv:
                conv3(i - 1, 2, 0)
                conv3(i - 1, 2, 1)

            if has_conv:
                if later(i):
                    pe.wait_ge(c3_evac.sem, c3_evac.at(i - 1, 2))
            if later(i):
                pe.wait_ge(y_done.sem, y_done.at(i - 1, 6))
            pe.wait_ge(h_ready.sem, h_ready.at(i, 4))
            for u in range(16):
                m, n = u // 2, u % 2
                if has_conv and u == 2:
                    pe.wait_ge(c3_evac.sem, c3_evac.at(i - 1, 3))
                if u >= 4:
                    pe.wait_ge(up_evac.sem, up_evac.at(i, u - 3))
                for c in range(2):
                    if m < 6:
                        last = mm(bank[u % 4][:, :], Wup[:, c, m * 128:(m + 1) * 128], H[:, c, span(n)],
                                  start=(c == 0), stop=(c == 1))
                    else:
                        last = mm(bank[u % 4][0:CH, :], Wlin[:, c, (m - 6) * CH:(m - 5) * CH], XG[:, c, span(n)],
                                  start=(c == 0), stop=(c == 1))
                last.then_inc(up_mm.sem, 1)
            for c in range(NCH):
                if c >= 4:
                    pe.wait_ge(vt_evac.sem, vt_evac.at(i, c - 3))
                else:
                    pe.wait_ge(hn_ready.sem, hn_ready.at(i, 2))
                for g in range(G3):
                    last = nc.tensor.transpose(bank[4 + c % 4][:, 128 * g:128 * g + 128],
                                               XIN[:, g, PAD + c * L:PAD + (c + 1) * L], ident)
                last.then_inc(vt_mm.sem, 1)
            pe.wait_ge(xa_ready.sem, xa_ready.at(i, 3))
            pe.wait_ge(up_evac.sem, up_evac.at(i, 16))
            for n in range(NT):
                for c in range(2 * G3):
                    w, src = (c, XA[:, c, span(n)]) if c < G3 else (
                        G3 + c, XIN[:, c - G3, PAD + n * 512:PAD + (n + 1) * 512])
                    last = mm(bank[n][0:44, :], Wg[:, w, :], src, start=(c == 0), stop=(c == 2 * G3 - 1))
                last.then_inc(gate_mm.sem, 1)
            for w in range(12):
                W, m, n = (Wq, w // 2, w % 2) if w < 6 else (Wk, w // 2 - 3, w % 2)
                if w in (2, 3):
                    pe.wait_ge(gate_evac.sem, gate_evac.at(i, 1))
                elif w >= 4:
                    pe.wait_ge(q_evac.sem, q_evac.at(i, min(w - 3, 6)))
                    if w >= 10:
                        pe.wait_ge(k_evac.sem, k_evac.at(i, w - 9))
                for c in range(G3):
                    last = mm(bank[(w + 2) % 4][:, :], W[:, c, m * 128:(m + 1) * 128], XA[:, c, span(n)],
                              start=(c == 0), stop=(c == 2))
                last.then_inc(qk_mm.sem, 1)
            pe.wait_ge(gw_ready.sem, gw_ready.at(i, 2))
            pe.wait_ge(rs_ready.sem, rs_ready.at(i, 2))
            pe.wait_ge(vt_evac.sem, vt_evac.at(i, NCH))
            for k in range(2):
                p = slice(32 * k, 32 * k + NH0)
                for c in range(NCH):
                    last = mm(bank[4 + 2 * k][:, NH0 * c:NH0 * c + NH0], GW[p, chunk(c)], ident[p, p],
                              start=True, stop=True)
                last.then_inc(gw_mm.sem, 1)
            for g in range(G3):
                last = mm(bank[5][:, NCH * g:NCH * g + NCH], expand[:, g, :], GW[0:12, L - 1::L],
                          start=True, stop=True)
            last.then_inc(gw_mm.sem, 1)

            def key_tokens(c):
                if c >= 1:
                    pe.wait_ge(kt_evac.sem, kt_evac.at(i, c))
                else:
                    pe.wait_ge(rs_ready.sem, rs_ready.at(i, 2))
                    pe.wait_ge(k_evac.sem, k_evac.at(i, 6))
                for g in range(G3):
                    last = nc.tensor.transpose(bank[7][:, 128 * g:128 * g + 128], K[:, g, chunk(c)], ident)
                last.then_inc(kt_mm.sem, 1)

            def scores(j):
                c, g = divmod(j, G3)
                if j == 0:
                    pe.wait_ge(gate_evac.sem, gate_evac.at(i, 1))
                    pe.wait_ge(part_cast.sem, part_cast.at(i, 3))
                if j >= 2:
                    pe.wait_ge(p_ready.sem, p_ready.at(i, j - 1))
                    pe.wait_ge(x_exp.sem, x_exp.at(i, j - 1))
                pe.wait_ge(qbd_ready.sem, qbd_ready.at(i, j + 1))
                mm(bank[j % 2][:, :], K[:, g, chunk(c)], QBD[:, j % 2, :, :], start=True, stop=True)
                e = bank[2 + j % 2]
                mm(e[:, :], identb[:, :], maskb[:, :, :], start=True, stop=False)
                mm(e[:, :], AB3[:, 0, chunk(c)], a_sel[:, g, :], start=False, stop=False)
                for h in range(HG):
                    last = mm(e[:, h * L:(h + 1) * L], b_sel[:, HG * g + h, :], AB3[:, 1, chunk(c)],
                              start=False, stop=(h == HG - 1))
                last.then_inc(se_mm.sem, 1)

            def outputs(j):
                c, g = divmod(j, G3)
                pe.wait_ge(p_ready.sem, p_ready.at(i, j + 1))
                if g == 0 and c >= 1:
                    pe.wait_ge(num_done.sem, num_done.at(i, c))
                for h in range(HG):
                    o = (HG * g + h) * V0
                    last = mm(bank[6][:, o:o + V0], PB[:, j % 2, h * L:(h + 1) * L], VE[:, c, o:o + V0],
                              start=True, stop=True)
                last.then_inc(o_mm.sem, 1)

            def inter(c):
                pe.wait_ge(st_ready.sem, st_ready.at(i, c))
                if c >= 2:
                    pe.wait_ge(inter_used.sem, inter_used.at(i, c - 1))
                for g in range(G3):
                    o = g * HG * V0
                    last = mm(bank[5][:, o:o + HG * V0], Q[:, g, chunk(c)], ST[:, o:o + HG * V0], start=True, stop=True)
                last.then_inc(inter_mm.sem, 1)

            def state(c):
                pe.wait_ge(kw_ready.sem, kw_ready.at(i, c + 1))
                if c >= 1:
                    pe.wait_ge(state_used.sem, state_used.at(i, c))
                for g in range(G3):
                    o = g * HG * V0
                    last = mm(bank[4][:, o:o + HG * V0], KT[:, c % 2, 128 * g:128 * g + 128],
                              VE[:, c, o:o + HG * V0], start=True, stop=True)
                last.then_inc(state_mm.sem, 1)

            def head_outputs(half, tiles=range(G3)):
                pe.wait_ge(hn_tok.sem, hn_tok.at(i, (4, len(NORM))[half]))
                for g in tiles:
                    w = half * G3 + g
                    if w == 0:
                        pe.wait_ge(kt_evac.sem, kt_evac.at(i, NCH - 1))
                    elif w <= 3:
                        pe.wait_ge(hT_evac.sem, hT_evac.at(i, w))
                    if w == 4:
                        pe.wait_ge(state_used.sem, state_used.at(i, NCH - 1))
                    if w == 5:
                        pe.wait_ge(inter_used.sem, inter_used.at(i, NCH - 1))
                    for cc in range(NCH // 2):
                        last = nc.tensor.transpose(bank[hT_bank[w]][:, cc * L:(cc + 1) * L],
                                                   DD[:, cc, 128 * g:128 * g + 128], ident)
                    last.then_inc(hT_mm.sem, 1)

            pe.wait_ge(gt_ready.sem, gt_ready.at(i, 3))
            key_tokens(0)
            scores(0)
            for c in range(NCH):
                scores(3 * c + 1)
                if c < NCH - 1:
                    state(c)
                outputs(3 * c)
                if c >= 1:
                    inter(c)
                if c == 6:
                    head_outputs(0, (0,))
                scores(3 * c + 2)
                outputs(3 * c + 1)
                if c == 6:
                    head_outputs(0, (1,))
                if c + 1 < NCH:
                    if c + 1 < NCH - 1:
                        key_tokens(c + 1)
                    scores(3 * c + 3)
                outputs(3 * c + 2)
                if c == 6:
                    head_outputs(0, (2,))
            pe.wait_ge(x_exp.sem, x_exp.at(i, G3 * NCH))
            if has_conv:
                conv3(i - 1, 3, 0)
                conv3(i - 1, 3, 1)
            head_outputs(1)
            for w in range(4):
                n, m = w // 2, 1 - w % 2
                pe.wait_ge(ho_ready.sem, ho_ready.at(i, 3 * n + 3))
                if has_conv and w == 3:
                    pe.wait_ge(c3_evac.sem, c3_evac.at(i - 1, 4))
                for c in range(G3):
                    last = mm(bank[w][0:CH, :], Wdown[:, c, m * CH:(m + 1) * CH], ZS[:, c, span(n)],
                              start=(c == 0), stop=(c == 2))
                last.then_inc(down_mm.sem, 1)

        over_images(pe, None, body, lambda i: body(i, rest=False))

    @block_ctx.scalar
    def _(act):
        A = nc.scalar.activation
        act.wait_ge(setup_loaded.sem, 13 * 16)
        act.wait_ge(setup_done.sem, shared["n_setup0"])

        def conv_out(i, g):
            m, n = g // 2, g % 2
            act.wait_ge(c3_mm.sem, c3_mm.at(i, g + 1))
            if g == 0:
                if later(i):
                    act.wait_ge(yc_stored.sem, yc_stored.at(i - 1, 2))
                if later(i):
                    act.wait_ge(bn_done.sem, bn_done.at(i - 1, 4))
            A(YC[:, m, span(n)], bank[g][0:CH, :], ACT.Identity, bias=w96("conv2_b", m)).then_inc(c3_evac.sem, 1)

        def body(i, rest=True):
            has_conv = not (isinstance(i, int) and i == 0)
            if not rest:
                for g in range(4):
                    conv_out(i - 1, g)
                return
            for n in range(NT):
                act.wait_ge(d_ready.sem, d_ready.at(i, n + 1))
                A(SQ[:, :, span(n)], H[:, :, span(n)], ACT.Square).then_inc(sq_ready.sem, 1)
                if n == 0 and has_conv:
                    conv_out(i - 1, 0)
            for n in range(NT):
                act.wait_ge(var_mm.sem, var_mm.at(i, n + 1))
                A(RS[:, span(n)], bank[6 + n][0:CH, :], ACT.Ln, bias=eps[0:CH, 0:1]).then_inc(own_a.sem, own_a.step())
            act.wait_ge(own_a.sem, own_a.value())
            for n in range(NT):
                A(RS[:, span(n)], RS[:, span(n)], ACT.Exp, scale=-0.5).then_inc(rs_ready.sem, 1)
            if has_conv:
                conv_out(i - 1, 1)
            for n in range(NT):
                act.wait_ge(hn_ready.sem, hn_ready.at(i, n + 1))
                for c in range(2):
                    A(H[:, c, span(n)], H[:, c, span(n)], ACT.Identity,
                      bias=w96("ln_b", c), scale=w96("ln_w", c)).then_inc(h_ready.sem, 1)
            if has_conv:
                conv_out(i - 1, 2)
            for u in range(16):
                m, n = u // 2, u % 2
                act.wait_ge(up_mm.sem, up_mm.at(i, u + 1))
                if m < 3:
                    A(XIN[:, m, PAD + n * 512:PAD + (n + 1) * 512], bank[u % 4][:, :], ACT.Identity,
                      bias=w128("b_up", m)).then_inc(up_evac.sem, 1)
                elif m < 6:
                    if u == 6:
                        if later(i):
                            act.wait_ge(down_mm.sem, down_mm.at(i - 1, 4))
                    A(ZS[:, m - 3, span(n)], bank[u % 4][:, :], ACT.Silu, bias=w128("b_up", m)).then_inc(up_evac.sem, 1)
                else:
                    if u == 12:
                        if later(i):
                            act.wait_ge(y_done.sem, y_done.at(i - 1, 6))
                    A(X2[:, m - 6, span(n)], bank[u % 4][0:CH, :], ACT.Silu, bias=w96("b_lin", m - 6)).then_inc(up_evac.sem, 1)
                if u in (9, 12, 15):
                    g = (u - 9) // 3
                    act.wait_ge(conv_done.sem, conv_done.at(i, g + 1))
                    A(XA[:, g, :], XA[:, g, :], ACT.Silu).then_inc(xa_ready.sem, 1)
            for c in range(NCH):
                act.wait_ge(vt_mm.sem, vt_mm.at(i, c + 1))
                A(heads(VE[:, c, :], V0)[:, :, 0:DH0], heads(bank[4 + c % 4][:, 0:INNER], DH0), ACT.Copy).then_inc(vt_evac.sem, 1)
            act.wait_ge(gate_mm.sem, gate_mm.at(i, 2))
            for n in range(NT):
                A(R[:, 0, span(n)], bank[n][32:44, :], ACT.Identity, bias=rows("b_f")).then_inc(own_a.sem, own_a.step())
                ins = A(R[:, 1, span(n)], bank[n][0:12, :], ACT.Identity, bias=rows("b_i"))
                if n:
                    ins.then_inc(gate_evac.sem, 1)
                else:
                    ins.then_inc(own_a.sem, own_a.step())
            act.wait_ge(own_a.sem, own_a.value())
            A(R[:, 2, :], R[:, 0, :], ACT.Abs).then_inc(own_a.sem, own_a.step())
            act.wait_ge(own_a.sem, own_a.value())
            A(R[:, 2, :], R[:, 2, :], ACT.Exp, scale=-1.0).then_inc(own_a.sem, own_a.step())
            act.wait_ge(own_a.sem, own_a.value())
            A(R[:, 2, :], R[:, 2, :], ACT.Ln, bias=1.0).then_inc(row_i.sem, 1)

            def queries(w):
                act.wait_ge(qk_mm.sem, qk_mm.at(i, w + 1))
                A(Q[:, w // 2, span(w % 2)], bank[(w + 2) % 4][:, :], ACT.Copy).then_inc(q_evac.sem, 1)

            for w in range(4):
                queries(w)
            for part in range(3):
                p = slice(32 * part, 32 * part + NH0)
                if part:
                    act.wait_ge(part_left.sem, part_left.at(i, part))
                else:
                    act.wait_ge(row_ab.sem, row_ab.at(i, 2))
                A(AB3[p, :, :], AB[p, :, :], ACT.Copy).then_inc(part_cast.sem, 1)
                if part < 2:
                    queries(4 + part)
            act.wait_ge(row_gx.sem, row_gx.at(i, 1))
            A(GW[0:12, :], R[:, 0, :], ACT.Exp).then_inc(gw_ready.sem, 1)
            A(GW[32:44, :], R[:, 3, :], ACT.Exp).then_inc(gw_ready.sem, 1)

            def keys(c):
                act.wait_ge(kt_mm.sem, kt_mm.at(i, c + 1))
                if c >= 2:
                    act.wait_ge(state_mm.sem, state_mm.at(i, c - 1))
                A(KT[:, c % 2, :], bank[7][:, 0:INNER], ACT.Copy).then_inc(kt_evac.sem, 1)

            def exps(j):
                act.wait_ge(se_mm.sem, se_mm.at(i, j + 1))
                if j >= 2:
                    act.wait_ge(p_ready.sem, p_ready.at(i, j - 1))
                A(XB[:, j % 2, :], bank[2 + j % 2][:, :], ACT.Exp).then_inc(x_exp.sem, 1)

            def deviations(k):
                act.wait_ge(dd_ready.sem, dd_ready.at(i, k + 1))
                A(SQB[:, in_half(k)], DD[:, :, :].rearrange("p c n -> p (c n)")[:, in_half(k)],
                  ACT.Square).then_inc(dsq_ready.sem, 1)

            keys(0)
            exps(0)
            for c in range(NCH):
                exps(3 * c + 1)
                if 1 <= c <= 4:
                    deviations(c - 1)
                if c == 7:
                    deviations(4)
                exps(3 * c + 2)
                if c + 1 < NCH - 1:
                    keys(c + 1)
                if c + 1 < NCH:
                    exps(3 * c + 3)
            deviations(5)
            if has_conv:
                conv_out(i - 1, 3)
            for n in range(NT):
                act.wait_ge(y_done.sem, y_done.at(i, 3 * n + 1))
                at = slice(1 + 16 * n, 17 + 16 * n)
                A(YP[64:128, 1, at, 0:HW], YP[0:64, 1, at, 1:1 + HW], ACT.Copy).then_inc(y_shifted.sem, 1)

        over_images(act, own_a, body, lambda i: body(i, rest=False))

    @block_ctx.vector
    def _(dve):
        V = nc.vector
        dve.wait_ge(setup_loaded.sem, 13 * 16)
        V.tensor_copy(identb[:, :], ident).then_inc(setup_done.sem, 1)
        V.tensor_copy(maskb[:, :, :], cst("causal").unsqueeze(1).broadcast_to([128, HG, L])).then_inc(setup_done.sem, 1)
        V.tensor_copy(a_sel[:, :, :], arena[0:96, 0:G3 * HG * L].rearrange("p (g n) -> p g n", g=G3)).then_inc(setup_done.sem, 1)
        V.tensor_copy(b_sel[:, :, :], arena[0:96, ATS["b_sel0"][0]:ATS["b_sel0"][1]].rearrange("p (g n) -> p g n", g=NH0)).then_inc(setup_done.sem, 1)
        dve.wait_ge(fold_mm.sem, 1)
        V.tensor_copy(Wg[:, 0:G3, :], bank[0][:, 0:G3 * 44].rearrange("p (c n) -> p c n", c=G3)).then_inc(setup_done.sem, 1)
        dve.wait_ge(setup_done.sem, shared["n_setup0"])

        def batch_stats(i, g):
            m, n = g // 2, g % 2
            dve.wait_ge(c3_evac.sem, c3_evac.at(i, g + 1))
            V.bn_stats(bn[:, m, bass.ds(i * 12 + n * 6, 6)], YC[:, m, span(n)]).then_inc(bn_done.sem, 1)

        def body(i, rest=True):
            has_conv = not (isinstance(i, int) and i == 0)
            if not rest:
                for g in range(4):
                    batch_stats(i - 1, g)
                return
            dve.wait_ge(x_loaded.sem, x_loaded.at(i, 1))
            for c in range(2):
                for n in range(NT):
                    V.bn_stats(gst[:, c, 6 * n:6 * n + 6], X[:, c, span(n)]).then_inc(own_v.sem, own_v.step())
            dve.wait_ge(own_v.sem, own_v.value())
            V.memset(gs[:, 0, 3:4], 0.0).then_inc(own_v.sem, own_v.step())
            V.bn_aggr(gs[:, 0, 0:2], gst[:, 0, :]).then_inc(own_v.sem, own_v.step())
            V.bn_aggr(gs[:, 1, 0:2], gst[:, 1, :]).then_inc(gn_stats.sem, 1)
            dve.wait_ge(gn_mean.sem, gn_mean.at(i, 1))
            V.tensor_copy(gs[:, :, 6:8], bank[6][0:CH, 0:4].rearrange("p (c s) -> p c s", c=2)).then_inc(own_v.sem, own_v.step())
            dve.wait_ge(own_v.sem, own_v.value())
            V.tensor_tensor(gs[:, :, 2], gs[:, :, 0], gs[:, :, 6], ALU.subtract).then_inc(own_v.sem, own_v.step())
            dve.wait_ge(own_v.sem, own_v.value())
            V.tensor_tensor(gs[:, :, 2], gs[:, :, 2], gs[:, :, 2], ALU.mult).then_inc(gn_dev.sem, 1)
            dve.wait_ge(gn_var.sem, gn_var.at(i, 1))
            V.scalar_tensor_tensor(gs[:, :, 3], bank[6][0:CH, 8:10], GN_EPS, gs[:, :, 7],
                                   ALU.add, ALU.add).then_inc(gn_sum.sem, 1)
            dve.wait_ge(gn_rstd.sem, gn_rstd.at(i, 1))
            if later(i):
                dve.wait_ge(rx_ready.sem, rx_ready.at(i - 1, 1))
            for c in range(2):
                V.tensor_scalar(XG[:, c, :], X[:, c, :], gs[:, c, 6:7], gs[:, c, 5:6],
                                ALU.subtract, ALU.mult).then_inc(xg_ready.sem, 1)
            dve.wait_ge(xg_ready.sem, xg_ready.at(i, 2))
            for n in range(NT):
                V.tensor_tensor(RS[:, span(n)], XG[:, 0, span(n)], XG[:, 1, span(n)], ALU.add).then_inc(xsum_ready.sem, 1)
            if later(i):
                dve.wait_ge(up_mm.sem, up_mm.at(i - 1, 12))
            for n in range(NT):
                dve.wait_ge(mean_mm.sem, mean_mm.at(i, n + 1))
                V.tensor_tensor(H[:, :, span(n)], XG[:, :, span(n)],
                                bank[4 + n][0:CH, :].unsqueeze(1).broadcast_to([CH, 2, 512]), ALU.subtract).then_inc(d_ready.sem, 1)
            for n in range(NT):
                dve.wait_ge(sq_ready.sem, sq_ready.at(i, n + 1))
                V.tensor_tensor(SQ[:, 0, span(n)], SQ[:, 0, span(n)], SQ[:, 1, span(n)], ALU.add).then_inc(sqsum_ready.sem, 1)
            if has_conv:
                batch_stats(i - 1, 0)
            for n in range(NT):
                dve.wait_ge(rs_ready.sem, rs_ready.at(i, n + 1))
                V.tensor_tensor(H[:, :, span(n)], H[:, :, span(n)],
                                RS[:, span(n)].unsqueeze(1).broadcast_to([CH, 2, 512]), ALU.mult).then_inc(hn_ready.sem, 1)
            if has_conv:
                batch_stats(i - 1, 1)
                batch_stats(i - 1, 2)
            dve.wait_ge(hn_ready.sem, hn_ready.at(i, 2))
            V.memset(XIN[:, :, 0:PAD], 0.0).then_inc(own_v.sem, own_v.step())
            dve.wait_ge(own_v.sem, own_v.value())
            if later(i):
                dve.wait_ge(hT_evac.sem, hT_evac.at(i - 1, 6))
            for g in range(G3):
                dve.wait_ge(up_evac.sem, up_evac.at(i, 2 * g + 2))
                if g == 0:
                    if later(i):
                        dve.wait_ge(ho_ready.sem, ho_ready.at(i - 1, 6))
                V.tensor_scalar(XA[:, g, :], XIN[:, g, 0:T], w128("conv_k", 4 * g), w128("conv_b", g),
                                ALU.mult, ALU.add).then_inc(own_v.sem, own_v.step())
                for t in range(1, TAPS):
                    dve.wait_ge(own_v.sem, own_v.value())
                    ins = V.scalar_tensor_tensor(
                        XA[:, g, :], XIN[:, g, t:t + T], w128("conv_k", 4 * g + t), XA[:, g, :], ALU.mult, ALU.add)
                    if t == TAPS - 1:
                        ins.then_inc(conv_done.sem, 1)
                    else:
                        ins.then_inc(own_v.sem, own_v.step())
            dve.wait_ge(row_i.sem, row_i.at(i, 1))
            dve.wait_ge(gate_evac.sem, gate_evac.at(i, 1))
            V.scalar_tensor_tensor(R[:, 3, :], R[:, 0, :], 0.0, R[:, 2, :], ALU.min, ALU.subtract).then_inc(own_v.sem, own_v.step())
            dve.wait_ge(own_v.sem, own_v.value())
            V.tensor_tensor_scan(R[:, 2, :], reset, R[:, 3, :], 0.0, ALU.mult, ALU.add).then_inc(own_v.sem, own_v.step())
            V.memset(MX[:, 0:1], 0.0).then_inc(own_v.sem, own_v.step())
            V.tensor_tensor_scan(MX[:, 1:1 + T], R[:, 3, :], R[:, 1, :], 0.0, ALU.add, ALU.max).then_inc(own_v.sem, own_v.step())
            dve.wait_ge(own_v.sem, own_v.value())
            V.tensor_tensor(AB[0:12, 0, :], R[:, 1, :], R[:, 2, :], ALU.subtract).then_inc(row_ab.sem, 1)
            V.tensor_tensor(AB[0:12, 1, :], R[:, 2, :], MX[:, 1:1 + T], ALU.subtract).then_inc(row_ab.sem, 1)
            dve.wait_ge(row_ab.sem, row_ab.at(i, 2))
            by_chunk = lambda ap: ap.rearrange("p (c l) -> p c l", l=L)
            spread = lambda ap: ap.unsqueeze(2).broadcast_to([12, NCH, L])
            V.tensor_tensor(by_chunk(R[:, 0, :]), by_chunk(AB[0:12, 1, :]), spread(MX[:, 0:T:L]), ALU.add).then_inc(own_v.sem, own_v.step())
            V.tensor_tensor(by_chunk(R[:, 3, :]), by_chunk(AB[0:12, 0, :]),
                            spread(AB[0:12, 1, L - 1::L]), ALU.add).then_inc(row_gx.sem, 1)
            for part in range(2):
                p, q = slice(32 * part, 32 * part + NH0), slice(32 * part + 32, 32 * part + 32 + NH0)
                dve.wait_ge(part_cast.sem, part_cast.at(i, part + 1))
                V.tensor_tensor(AB[q, :, :], AB[p, :, :], AB3[p, :, :], ALU.subtract).then_inc(part_left.sem, 1)
            for w in range(6):
                dve.wait_ge(qk_mm.sem, qk_mm.at(i, 7 + w))
                V.tensor_scalar(K[:, w // 2, span(w % 2)], bank[w % 4][:, :], float(DH0) ** -0.5,
                                None, ALU.mult).then_inc(k_evac.sem, 1)
            dve.wait_ge(gw_mm.sem, gw_mm.at(i, 3))
            for k in range(2):
                V.tensor_copy(GT[:, :, NH0 * k:NH0 * k + NH0], bank[4 + 2 * k][:, 0:NH0 * NCH]
                              .rearrange("p (c n) -> p c n", c=NCH)).then_inc(gt_ready.sem, 1)
            V.tensor_copy(DEC[:, :, :], bank[5][:, 0:G3 * NCH].rearrange("p (g c) -> p g c", g=G3)).then_inc(gt_ready.sem, 1)

            def weigh(j):
                dve.wait_ge(x_exp.sem, x_exp.at(i, j + 1))
                if j >= 2:
                    dve.wait_ge(o_mm.sem, o_mm.at(i, j - 1))
                V.tensor_tensor(PB[:, j % 2, :], bank[j % 2][:, :], XB[:, j % 2, :], ALU.mult).then_inc(p_ready.sem, 1)

            def state(c):
                dve.wait_ge(state_mm.sem, state_mm.at(i, c + 1))
                new = bank[4][:, 0:NH0 * V0].rearrange("p (g n) -> p g n", g=G3)
                V.tensor_tensor(TC[:, :].rearrange("p (g n) -> p g n", g=G3), new, block_all, ALU.mult).then_inc(state_used.sem, 1)
                dve.wait_ge(state_used.sem, state_used.at(i, c + 1))
                if c == 0:
                    if later(i):
                        dve.wait_ge(inter_mm.sem, inter_mm.at(i - 1, NCH - 1))
                    V.tensor_copy(ST[:, :], TC[:, :]).then_inc(st_ready.sem, 1)
                    return
                dve.wait_ge(inter_mm.sem, inter_mm.at(i, c))
                dve.wait_ge(st_ready.sem, st_ready.at(i, c))
                for g in range(G3):
                    o = slice(g * HG * V0, (g + 1) * HG * V0)
                    ins = V.scalar_tensor_tensor(ST[:, o], ST[:, o], DEC[:, g, c:c + 1], TC[:, o], ALU.mult, ALU.add)
                    if g == G3 - 1:
                        ins.then_inc(st_ready.sem, 1)
                    else:
                        ins.then_inc(own_v.sem, own_v.step())

            def reach(c):
                dve.wait_ge(inter_mm.sem, inter_mm.at(i, c))
                V.tensor_tensor(heads(TI[:, :], V0), heads(bank[5][:, 0:NH0 * V0], V0),
                                GT[:, c, 0:NH0].unsqueeze(2).broadcast_to([128, NH0, V0]), ALU.mult).then_inc(inter_used.sem, 1)

            def total(c):
                dve.wait_ge(o_mm.sem, o_mm.at(i, G3 * (c + 1)))
                out = NUM[:, c, :]
                if c == 0:
                    V.tensor_copy(out, bank[6][:, 0:NH0 * V0]).then_inc(num_done.sem, 1)
                else:
                    dve.wait_ge(inter_used.sem, inter_used.at(i, c))
                    V.tensor_tensor(out, bank[6][:, 0:NH0 * V0], TI[:, :], ALU.add).then_inc(num_done.sem, 1)

            def views(k):
                lo, hi = NORM[k]
                by_head = lambda ap: ap[:, in_half(k)].rearrange("p (h v) -> p h v", v=DH0)
                return (slice(lo * NH0, hi * NH0), (hi - lo) * NH0,
                        NUM[:, lo:hi, :].rearrange("p c (h v) -> p (c h) v", v=V0),
                        by_head(DD[:, :, :].rearrange("p c n -> p (c n)")), by_head(SQB[:, :]))

            def center(k):
                dve.wait_ge(num_done.sem, num_done.at(i, NORM[k][1]))
                at, n, num, dd, _ = views(k)
                V.tensor_tensor(sm[:, 0, at], num[:, :, DH0], num[:, :, DH0], ALU.mult).then_inc(own_v.sem, own_v.step())
                V.reduce_sum(sm[:, 1, at], num[:, :, 0:DH0], AX).then_inc(own_v.sem, own_v.step())
                dve.wait_ge(own_v.sem, own_v.value())
                V.tensor_scalar(sm[:, 0, at], sm[:, 0, at], 1.0, GN_EPS, ALU.max, ALU.mult).then_inc(own_v.sem, own_v.step())
                if k >= 4:
                    dve.wait_ge(hT_mm.sem, hT_mm.at(i, 3))
                V.scalar_tensor_tensor(dd, sm[:, 1, at].unsqueeze(2).broadcast_to([128, n, DH0]),
                                       -1.0 / DH0, num[:, :, 0:DH0], ALU.mult, ALU.add).then_inc(dd_ready.sem, 1)

            def spread_of(k):
                dve.wait_ge(dsq_ready.sem, dsq_ready.at(i, k + 1))
                at, n, num, dd, squares = views(k)
                V.reduce_sum(sm[:, 1, at], squares, AX).then_inc(own_v.sem, own_v.step())
                dve.wait_ge(own_v.sem, own_v.value())
                V.scalar_tensor_tensor(sm[:, 2, at], sm[:, 1, at], 1.0 / DH0, sm[:, 0, at],
                                       ALU.mult, ALU.add).then_inc(arg_ready.sem, 1)

            def normalise(k):
                dve.wait_ge(rho_ready.sem, rho_ready.at(i, k + 1))
                at, n, num, dd, _ = views(k)
                V.tensor_tensor(dd, dd, sm[:, 3, at].unsqueeze(2).broadcast_to([128, n, DH0]),
                                ALU.mult).then_inc(hn_tok.sem, 1)

            def gate(half, tiles=range(G3)):
                dve.wait_ge(u_ready.sem, u_ready.at(i, 3))
                for g in tiles:
                    dve.wait_ge(hT_mm.sem, hT_mm.at(i, half * G3 + g + 1))
                    if later(i) or half * G3 + g:
                        dve.wait_ge(ho_ready.sem, ho_ready.at(i, half * G3 + g))
                    V.scalar_tensor_tensor(TZ[:, :], bank[hT_bank[half * G3 + g]][:, :], w128("mh_w", g),
                                           XA[:, g, span(half)], ALU.mult, ALU.add).then_inc(hT_evac.sem, 1)
                    dve.wait_ge(hT_evac.sem, hT_evac.at(i, half * G3 + g + 1))
                    V.tensor_tensor(ZS[:, g, span(half)], TZ[:, :], ZS[:, g, span(half)], ALU.mult).then_inc(ho_ready.sem, 1)

            weigh(0)
            for c in range(NCH):
                weigh(3 * c + 1)
                if c == 0:
                    state(c)
                else:
                    reach(c)
                if c == 6:
                    gate(0, (0,))
                weigh(3 * c + 2)
                if 1 <= c < NCH - 1:
                    state(c)
                if c == 6:
                    gate(0, (1,))
                if c + 1 < NCH:
                    weigh(3 * c + 3)
                if c == 7:
                    spread_of(4)
                total(c)
                if c <= 3:
                    center(c)
                if 1 <= c <= 4:
                    spread_of(c - 1)
                if 2 <= c <= 5:
                    normalise(c - 2)
                if c == 6:
                    gate(0, (2,))
                    center(4)
            center(5)
            normalise(4)
            spread_of(5)
            normalise(5)
            gate(1)
            if has_conv:
                batch_stats(i - 1, 3)
            dve.wait_ge(rx_ready.sem, rx_ready.at(i, 1))
            if later(i):
                dve.wait_ge(c3_mm.sem, c3_mm.at(i - 1, 4))
            for w in range(4):
                n, m = w // 2, 1 - w % 2
                dve.wait_ge(down_mm.sem, down_mm.at(i, w + 1))
                rows_of = lambda ap: ap.rearrange("p (r s) -> p r s", s=HW)
                at = slice(1 + 16 * n, 17 + 16 * n)
                for src, dst in (((slice(0, CH), YP[0:CH, 0, at, 1:1 + HW]),) if m == 0 else
                                 ((slice(0, 64), YP[0:64, 1, at, 1:1 + HW]), (slice(64, CH), YP[96:128, 0, at, 1:1 + HW]))):
                    V.scalar_tensor_tensor(dst, rows_of(bank[w][src, :]), w96("b_down", m)[src],
                                           rows_of(X2[src, m, span(n)]), ALU.add, ALU.add).then_inc(y_done.sem, 1)


        over_images(dve, own_v, body, lambda i: body(i, rest=False))


def layer1(nc, ctx, d, shared, out):
    def sb(name, shape, dt=F32):
        return ctx.enter_context(nc.sbuf_tensor(name, shape, dt))

    def signal(name, per_image, unit=1):
        return Signal(ctx.enter_context(nc.semaphore(name)), per_image, unit)

    bank = shared["bank"]
    w96, w128, rows, cst, eps = (shared[k] for k in ("w96", "w128", "rows", "cst", "eps"))
    bn = shared["bn"]
    XBC_T = 4
    KX = INNER + NS

    Win = sb("Win", [CH, 2, 2 * INNER + 2 * NS + NH1])
    Wout = sb("Wout", [128, G3, C])
    Wf1 = sb("Wf1", [CH, 2, INNER])
    Wf2 = sb("Wf2", [128, G3, C])
    identb = sb("m_identb", [128, 128], BF16)
    maskb = sb("m_maskb", [128, HB, L], BF16)
    a_sel = sb("m_a_sel", [96, 2, HB * L], BF16)
    b_sel = sb("m_b_sel", [96, NH1, 128], BF16)
    ones = sb("m_ones", [NH1, NS])
    X1 = sb("X1", [CH, 2, T])
    Y0 = sb("Y0", [CH, 2, T])
    XG = sb("m_XG", [CH, 2, T])
    hst = sb("hst", [128, NCH, 6])
    hmv = sb("hmv", [128, NCH, 4])
    n1 = sb("n1", [128, 2, C])
    XF = sb("XF", [CH, 2, T])
    U = sb("U", [CH, 2, T])
    gs = sb("m_gs", [CH, 2, 8])
    gst = sb("m_gst", [CH, 2, 12])
    bns = sb("bns", [CH, 2, 6])
    XBC = sb("XBC", [128, XBC_T, PAD + T])
    CV = sb("CV", [128, XBC_T, T])
    BS = sb("BS", [NS, T])
    CS = sb("CS", [NS, T])
    ZT = sb("ZT", [128, NCH, INNER])
    XT = sb("XT", [128, NCH, KX])
    XD = sb("XD", [128, 2, INNER])
    XW = sb("XW", [128, 2, INNER])
    CU = sb("CU", [96, T])
    CU3 = sb("CU3", [96, T], BF16)
    GWD = sb("GWD", [64 + NH1, T])
    GT = sb("m_GT", [128, NCH, 3 * NH1])
    DG = sb("DG", [NH1, NCH, NH1])
    DEC = sb("m_DEC", [NS, NCH, NH1])
    XPB = sb("m_XPB", [128, 6, HB * L])
    XB, PB = XPB[:, 0:2, :], XPB[:, 2:6, :]
    R = XPB[:, :, :].rearrange("p j n -> p (j n)")[0:NH1, 0:2 * T].rearrange("p (r t) -> p r t", r=2)
    ST = sb("m_ST", [NS, INNER])
    TI = sb("m_TI", [128, INNER])
    YT = sb("YT", [128, NCH, INNER])
    JK = sb("JK", [128, INNER])
    SS = sb("SS", [128, NCH])
    RR = sb("RR", [128, NCH])
    GC = sb("GC", [128, G3, T])
    XX = sb("XX", [CH, 2, T])
    OUT = sb("OUT", [CH, 2, T])
    halves = lambda ap: ap.rearrange("p (c t) -> p c t", c=2)
    HT = XBC[:, 0:2, PAD:PAD + (NCH // 2) * C].rearrange("p g (c n) -> p g c n", n=C)
    ht = lambda c: HT[:, c // (NCH // 2), c % (NCH // 2), :]
    XL = XBC[0:CH, 2:4, PAD:PAD + T]
    yt = YT[:, :, :].rearrange("p c n -> p (c n)")
    H2, RS2, SQ2 = halves(yt[0:CH, 0:2 * T]), yt[0:CH, 2 * T:3 * T], OUT
    F = GC
    sel = yt[0:96, 0:NH1 * (L + 128)]

    ident, group, mean_w = (cst(n) for n in ("ident", "group", "mean"))
    pick = cst("pick1")[0:64 + NH1, :]
    reset = cst("reset")[0:NH1, :]

    loaded = signal("m_loaded", 0, 16)
    setup = signal("m_setup", 0)
    n_setup = 12
    n1_loaded = signal("n1_loaded", 0, 16)
    bn_step = signal("bn_step", 0)
    y_loaded = signal("y_loaded", 1, 16)
    x_loaded = signal("m_x_loaded", 1, 16)
    y_scaled = signal("y_scaled", 2)
    y_leaky = signal("y_leaky", 1)
    x1_ready = signal("x1_ready", 1)
    gn_stats = signal("m_gn_stats", 1)
    gn_mean = signal("m_gn_mean", 1)
    gn_dev = signal("m_gn_dev", 1)
    gn_var = signal("m_gn_var", 1)
    gn_sum = signal("m_gn_sum", 1)
    gn_rstd = signal("m_gn_rstd", 1)
    xg_ready = signal("m_xg_ready", 2)
    ln2 = {n: signal(f"ln2_{n}", c) for n, c in
           [("sum", 2), ("mean", 2), ("d", 2), ("sq", 2), ("sqsum", 2), ("var", 2), ("ln", 2), ("rs", 2), ("hn", 2), ("h", 4)]}
    ht_mm = signal("ht_mm", 4)
    ht_evac = signal("ht_evac", 4)
    hv_ready = signal("hv_ready", 1)
    hr_ready = signal("hr_ready", 1)
    ht_ready = signal("ht_ready", NCH)
    u_stored = signal("u_stored", 2, 16)
    u_loaded = signal("u_loaded", 1, 16)
    in_mm = signal("in_mm", 18)
    in_evac = signal("in_evac", 18)
    conv_done = signal("m_conv_done", XBC_T)
    xs_ready = signal("xs_ready", 5)
    row_sp = signal("row_sp", 1)
    cu_ready = signal("cu_ready", 1)
    part_cast = signal("m_part_cast", 3)
    part_left = signal("m_part_left", 2)
    row_w = signal("row_w", 1)
    row_we = signal("row_we", 1)
    g_ready = signal("g_ready", 2)
    w_ready = signal("w_ready", 1)
    dg_ready = signal("dg_ready", 1)
    gw_mm = signal("m_gw_mm", 2)
    gt_ready = signal("m_gt_ready", 2)
    xt_mm = signal("xt_mm", NCH)
    xt_evac = signal("xt_evac", NCH)
    xd_ready = signal("xd_ready", NCH)
    xw_ready = signal("xw_ready", NCH)
    xu_ready = signal("xu_ready", NCH)
    e_mm = signal("e_mm", 2 * NCH)
    x_exp = signal("m_x_exp", 2 * NCH)
    p_ready = signal("m_p_ready", 2 * NCH)
    state_mm = signal("m_state_mm", NCH - 1)
    st_ready = signal("m_st_ready", NCH - 1)
    o_mm = signal("m_o_mm", NCH)
    inter_mm = signal("m_inter_mm", NCH - 1)
    inter_used = signal("m_inter_used", NCH - 1)
    o_used = signal("o_used", NCH)
    y_summed = signal("y_summed", NCH - 2)
    y_gated = signal("y_gated", NCH)
    ss_ready = signal("ss_ready", NCH)
    ms_ready = signal("ms_ready", NCH)
    rr_ready = signal("rr_ready", NCH)
    yn_ready = signal("yn_ready", NCH)
    gT_mm = signal("gT_mm", NCH)
    gT_evac = signal("gT_evac", NCH)
    out_mm = signal("out_mm", 4)
    xf_ready = signal("xf_ready", 4)
    xf_copied = signal("xf_copied", 2)
    xs_added = signal("xs_added", 1)
    xx_ready = signal("xx_ready", 4)
    xx_moved = signal("xx_moved", 1)
    f1_mm = signal("f1_mm", 6)
    f1_evac = signal("f1_evac", 6)
    f2_mm = signal("f2_mm", 4)
    out_ready = signal("out_ready", 4)
    stored = signal("stored", 1, 16)
    own_v = Own(ctx.enter_context(nc.semaphore("m_vector_own")))
    own_f = Own(ctx.enter_context(nc.semaphore("m_vector_front_own")))
    own_a = Own(ctx.enter_context(nc.semaphore("m_scalar_own")))

    block_ctx = ctx.enter_context(nc.Block())
    x_in = d["x"].rearrange("b (c p) h w -> b p c (h w)", p=CH)
    x_out = out.rearrange("b (c p) h w -> b p c (h w)", p=CH)
    u_by_token = d["u"].rearrange("b (g c p n) -> b g p c n", g=2, p=128, n=C)
    u_by_channel = d["u"].rearrange("b (c p t) -> b p c t", c=2, t=T)
    y_in = d["yc"].rearrange("b p (c t) -> b p c t", c=2)
    span = lambda n: slice(n * 512, (n + 1) * 512)
    chunk = lambda c: slice(c * L, (c + 1) * L)
    heads = lambda ap: ap.rearrange("p (h v) -> p h v", v=DH1)

    has_main = lambda k: not (isinstance(k, int) and k < 1)
    has_back = lambda k: not (isinstance(k, int) and k < 2)
    in_order = (8, 9, 6, 7, 0, 1, 2, 3, 4, 5) + tuple(range(10, 18))

    in_bank = tuple(n % 4 for n in range(10)) + (4, 5, 2, 3, 0, 1, 4, 5)

    def tile_rows(w):
        return (slice(INNER + (w // 2) * 128, INNER + (w // 2 + 1) * 128) if w < 8
                else slice(2 * INNER + 2 * NS, 2 * INNER + 2 * NS + NH1))

    @block_ctx.sync
    def _(sp):
        loads = [
            (Win[:, :, :], d["w_in"].rearrange("(c p) n -> p c n", p=CH)),
            (Wout[:, :, :], d["w_out"].rearrange("(c p) n -> p c n", p=128)),
            (Wf1[:, :, :], d["w_f1"].rearrange("(c p) n -> p c n", p=CH)),
            (Wf2[:, :, :], d["w_f2"].rearrange("(c p) n -> p c n", p=128)),
            (sel[:, :], d["select"][0:96, ATS["a_sel1"][0]:ATS["b_sel1"][1]]),
        ]
        assert len(loads) == 5

        def store(i):
            sp.wait_ge(out_ready.sem, out_ready.at(i, 4))
            sp.dma_start(x_out[i], OUT[:, :, :]).then_inc(stored.sem, 16)

        def body(k, front=True):
            if front:
                if later(k):
                    sp.wait_ge(x1_ready.sem, x1_ready.at(k - 1, 1))
                sp.dma_start(Y0[:, :, :], y_in[k]).then_inc(y_loaded.sem, 16)
                if later(k):
                    sp.wait_ge(conv_done.sem, conv_done.at(k - 1, XBC_T))
                sp.dma_start(XL, x_in[k]).then_inc(x_loaded.sem, 16)
            if not has_main(k):
                sp.dma_start(n1[:, :, :], d["norm1"].rearrange("p (k n) -> p k n", k=2)).then_inc(n1_loaded.sem, 16)
                for dst, src in loads:
                    sp.dma_start(dst, src).then_inc(loaded.sem, 16)
            if has_back(k):
                store(k - 2)
            if front:
                for g in range(2):
                    sp.wait_ge(ht_ready.sem, ht_ready.at(k, NCH // 2 * (g + 1)))
                    sp.dma_start(u_by_token[k][g], HT[:, g, :, :]).then_inc(u_stored.sem, 16)
                sp.wait_ge(u_stored.sem, u_stored.at(k, 2))
                if later(k):
                    sp.wait_ge(in_mm.sem, in_mm.at(k - 1, 18))
                sp.dma_start(U[:, :, :], u_by_channel[k]).then_inc(u_loaded.sem, 16)

        over_images(sp, None, body, lambda k: body(k, False), first=3)
        store(B - 1)
        sp.wait_ge(stored.sem, stored.at(B - 1, 1))

    @block_ctx.gpsimd
    def _(pool):
        pool.memset(CU3[:, :], 0.0).then_inc(setup.sem, 1)
        pool.memset(GWD[:, :], 0.0).then_inc(setup.sem, 1)
        pool.memset(XBC[:, :, 0:PAD], 0.0).then_inc(setup.sem, 1)
        pool.memset(ones[:, :], 1.0).then_inc(setup.sem, 1)
        rsqrt = lambda o, x: nc.gpsimd.tensor_tensor(
            o, x, eps[0:x.shape[0], 1:2].broadcast_to(list(x.shape)), ALU.pow)
        ffn_bias = shared["w96_pair"]("ffn_b2").unsqueeze(2).broadcast_to([CH, 2, T])
        pool.wait_ge(bn_step.sem, 1)
        rsqrt(bns[:, :, 3], bns[:, :, 2]).then_inc(bn_step.sem, 1)

        def body(k, front=True):
            i = k - 1
            if has_back(k):
                pool.wait_ge(ln2["var"].sem, ln2["var"].at(k - 2, 2))
                pool.wait_ge(xx_ready.sem, xx_ready.at(k - 2, 4))
                nc.gpsimd.tensor_tensor(OUT[:, :, :], XX[:, :, :], ffn_bias, ALU.add).then_inc(xx_moved.sem, 1)
            if has_main(k):
                if has_back(k):
                    pool.wait_ge(xx_moved.sem, xx_moved.at(k - 2, 1))
                pool.wait_ge(xg_ready.sem, xg_ready.at(i, 2))
                nc.gpsimd.tensor_tensor(XX[:, :, :], X1[:, :, :], XG[:, :, :], ALU.add).then_inc(xs_added.sem, 1)
            if front:
                if has_main(k):
                    pool.wait_ge(xs_added.sem, xs_added.at(i, 1))
                pool.wait_ge(y_leaky.sem, y_leaky.at(k, 1))
                pool.wait_ge(x_loaded.sem, x_loaded.at(k, 1))
                nc.gpsimd.tensor_tensor(X1[:, :, :], Y0[:, :, :], XL, ALU.add).then_inc(x1_ready.sem, 1)
                pool.wait_ge(gn_sum.sem, gn_sum.at(k, 1))
                rsqrt(gs[:, :, 5], gs[:, :, 3]).then_inc(gn_rstd.sem, 1)
            if not has_main(k):
                pool.wait_ge(hv_ready.sem, hv_ready.at(k, 1))
                rsqrt(hmv[:, :, 3], hmv[:, :, 2]).then_inc(hr_ready.sem, 1)
                return

            def reciprocal(c):
                pool.wait_ge(ms_ready.sem, ms_ready.at(i, c + 1))
                rsqrt(RR[:, c:c + 1], SS[:, c:c + 1]).then_inc(rr_ready.sem, 1)

            def gated(c):
                if c == 0:
                    pool.wait_ge(o_used.sem, o_used.at(i, 1))
                else:
                    pool.wait_ge(y_summed.sem, y_summed.at(i, c))
                nc.gpsimd.tensor_tensor(YT[:, c, :], YT[:, c, :], ZT[:, c, :], ALU.mult).then_inc(y_gated.sem, 1)
                if c >= 1:
                    reciprocal(c - 1)

            for c in range(NCH):
                pool.wait_ge(xt_evac.sem, xt_evac.at(i, c + 1))
                if c == 0:
                    pool.wait_ge(gt_ready.sem, gt_ready.at(i, 1))
                x = heads(XT[:, c, 0:INNER])
                by_head = lambda ap: ap.unsqueeze(2).broadcast_to([128, NH1, DH1])
                if c >= 2:
                    pool.wait_ge(o_mm.sem, o_mm.at(i, c - 1))
                    pool.wait_ge(state_mm.sem, state_mm.at(i, c - 1))
                nc.gpsimd.tensor_tensor(heads(XD[:, c % 2, :]), x, by_head(GT[:, c, 12:18]), ALU.mult).then_inc(xd_ready.sem, 1)
                nc.gpsimd.tensor_tensor(heads(XW[:, c % 2, :]), x, by_head(GT[:, c, 6:12]), ALU.mult).then_inc(xw_ready.sem, 1)
                if c == 7:
                    gated(5)
                if c == 7 and front:
                    pool.wait_ge(hv_ready.sem, hv_ready.at(k, 1))
                    rsqrt(hmv[:, :, 3], hmv[:, :, 2]).then_inc(hr_ready.sem, 1)
                pool.wait_ge(xw_ready.sem, xw_ready.at(i, c + 1))
                nc.gpsimd.tensor_tensor(x, x, by_head(w128("D", 0, NH1)), ALU.mult).then_inc(xu_ready.sem, 1)
                if c in (1, 2, 3, 4, 5, 7):
                    gated(c - 1)
            reciprocal(NCH - 2)
            reciprocal(NCH - 1)

        over_images(pool, None, body, lambda k: body(k, False), first=3)
        pool.wait_ge(ln2["var"].sem, ln2["var"].at(B - 1, 2))
        pool.wait_ge(xx_ready.sem, xx_ready.at(B - 1, 4))
        nc.gpsimd.tensor_tensor(OUT[:, :, :], XX[:, :, :], ffn_bias, ALU.add).then_inc(xx_moved.sem, 1)

    @block_ctx.tensor
    def _(pe):
        mm = nc.tensor.matmul

        def average(p, kind, src, ready):
            b = 4 if kind == "mean" else 6
            for n in range(NT):
                pe.wait_ge(ready.sem, ready.at(p, n + 1))
                mm(bank[b + n][0:CH, :], mean_w[0:CH, :], src[:, span(n)], start=True, stop=True).then_inc(ln2[kind].sem, 1)

        def ffn1(p, taken):
            pe.wait_ge(ln2["h"].sem, ln2["h"].at(p, 4))
            for w in range(6):
                m, n = w // 2, w % 2
                if taken and w < 4:
                    pe.wait_ge(in_evac.sem, in_evac.at(p + 1, taken - 5 + w))
                if w >= 4:
                    pe.wait_ge(f1_evac.sem, f1_evac.at(p, w - 3))
                for c in range(2):
                    last = mm(bank[(taken + w) % 4][:, :], Wf1[:, c, m * 128:(m + 1) * 128], H2[:, c, span(n)],
                              start=(c == 0), stop=(c == 1))
                last.then_inc(f1_mm.sem, 1)

        def ffn2(p, part, taken):
            pe.wait_ge(f1_evac.sem, f1_evac.at(p, 6))
            for w in (2 * part, 2 * part + 1):
                m, n = w // 2, w % 2
                for c in range(G3):
                    last = mm(bank[(taken + 6 + w) % 4][0:CH, :], Wf2[:, c, m * CH:(m + 1) * CH], F[:, c, span(n)],
                              start=(c == 0), stop=(c == 2))
                last.then_inc(f2_mm.sem, 1)

        def group_mean(k):
            pe.wait_ge(gn_stats.sem, gn_stats.at(k, 1))
            if has_main(k):
                pe.wait_ge(in_evac.sem, in_evac.at(k - 1, 18))
            mm(bank[5][0:CH, 0:4], group[0:CH, :], gs[:, :, 0:2], start=True, stop=True).then_inc(gn_mean.sem, 1)

        def group_spread(k):
            pe.wait_ge(gn_dev.sem, gn_dev.at(k, 1))
            mm(bank[5][0:CH, 8:10], group[0:CH, :], gs[:, :, 2], start=True, stop=True).then_inc(gn_var.sem, 1)

        def by_token(k, q):
            pe.wait_ge(xg_ready.sem, xg_ready.at(k, 2))
            if has_main(k):
                pe.wait_ge(xt_evac.sem, xt_evac.at(k - 1, q + 3))
            elif q:
                pe.wait_ge(ht_evac.sem, ht_evac.at(k, q))
            for j in range(4):
                c, half = 2 * q + j // 2, j % 2
                last = nc.tensor.transpose(bank[7][:, CH * j:CH * j + CH], XG[:, half, chunk(c)], ident[0:CH, 0:CH])
            last.then_inc(ht_mm.sem, 1)

        def body(k, front=True):
            i, p = k - 1, k - 2
            if not has_main(k):
                group_mean(k)
                group_spread(k)
                for q in range(4):
                    by_token(k, q)
                return

            def project(first, last_one):
                for pos in range(first, last_one):
                    w = in_order[pos]
                    if pos in (10, 11):
                        if has_back(k):
                            pe.wait_ge(ln2["d"].sem, ln2["d"].at(p, 2))
                    elif pos >= 12:
                        pe.wait_ge(in_evac.sem, in_evac.at(i, pos - 5))
                    elif pos >= 4:
                        pe.wait_ge(in_evac.sem, in_evac.at(i, pos - 3))
                    elif later(i):
                        pe.wait_ge(xx_ready.sem, xx_ready.at(p, pos + 1))
                    b = bank[in_bank[pos]]
                    for c in range(2):
                        flags = dict(start=(c == 0), stop=(c == 1))
                        if w < 10:
                            r = tile_rows(w)
                            last = mm(b[0:r.stop - r.start, :], Win[:, c, r], U[:, c, span(w % 2)], **flags)
                        else:
                            last = mm(b[:, 0:INNER], U[:, c, chunk(w - 10)], Win[:, c, 0:INNER], **flags)
                    last.then_inc(in_mm.sem, 1)

            if not has_back(k):
                pe.wait_ge(loaded.sem, 5 * 16)
                pe.wait_ge(setup.sem, n_setup)
            pe.wait_ge(u_loaded.sem, u_loaded.at(i, 1))
            project(0, 4)
            if has_back(k):
                average(p, "mean", RS2, ln2["sum"])
            project(4, 9)
            if has_back(k):
                average(p, "var", SQ2[:, 0, :], ln2["sqsum"])
            project(9, 18)
            if has_back(k):
                ffn1(p, 18)
                ffn2(p, 0, 18)
            if front:
                group_mean(k)
            if has_back(k):
                ffn2(p, 1, 18)
            if front:
                group_spread(k)
            if has_back(k):
                pe.wait_ge(ln2["rs"].sem, ln2["rs"].at(p, 2))
            pe.wait_ge(g_ready.sem, g_ready.at(i, 2))
            pe.wait_ge(w_ready.sem, w_ready.at(i, 1))
            for c in range(NCH):
                last = mm(bank[6][:, 18 * c:18 * c + 18], GWD[:, chunk(c)], pick, start=True, stop=True)
            last.then_inc(gw_mm.sem, 1)
            pe.wait_ge(dg_ready.sem, dg_ready.at(i, 1))
            mm(bank[6][0:NS, 256:256 + NCH * NH1], ones[:, :], DG[:, :, :], start=True, stop=True).then_inc(gw_mm.sem, 1)

            def tokens(c):
                pe.wait_ge(xs_ready.sem, xs_ready.at(i, 5))
                if c:
                    pe.wait_ge(xt_evac.sem, xt_evac.at(i, c))
                if front and 3 <= c < 6:
                    pe.wait_ge(ht_evac.sem, ht_evac.at(k, c - 2))
                if c >= 6:
                    pe.wait_ge(gT_evac.sem, gT_evac.at(i, c - 5))
                for g in range(G3):
                    nc.tensor.transpose(bank[7][:, 128 * g:128 * g + 128], CV[:, g, chunk(c)], ident)
                nc.tensor.transpose(bank[7][:, INNER:KX], BS[:, chunk(c)], ident[0:NS, 0:NS]).then_inc(xt_mm.sem, 1)

            def scores(c):
                if c == 0:
                    pe.wait_ge(in_evac.sem, in_evac.at(i, 18))
                    pe.wait_ge(part_cast.sem, part_cast.at(i, 3))
                    if has_back(k):
                        pe.wait_ge(out_ready.sem, out_ready.at(p, 4))
                if c >= 2:
                    pe.wait_ge(p_ready.sem, p_ready.at(i, 2 * (c - 1)))
                mm(bank[c % 2][:, 0:L], BS[:, chunk(c)], CS[:, chunk(c)], start=True, stop=True)
                for r in range(2):
                    if c >= 1:
                        pe.wait_ge(x_exp.sem, x_exp.at(i, 2 * c - 1 + r))
                    e = bank[2 + r][:, 0:HB * L]
                    mm(e, identb[:, :], maskb[:, :, :], start=True, stop=False)
                    mm(e, CU3[:, chunk(c)], a_sel[:, r, :], start=False, stop=False)
                    for h in range(HB):
                        last = mm(bank[2 + r][:, h * L:(h + 1) * L], b_sel[:, HB * r + h, :], CU3[:, chunk(c)],
                                  start=False, stop=(h == HB - 1))
                    last.then_inc(e_mm.sem, 1)

            def state(c):
                pe.wait_ge(xw_ready.sem, xw_ready.at(i, c + 1))
                if c == 0:
                    pe.wait_ge(gt_ready.sem, gt_ready.at(i, 2))
                else:
                    pe.wait_ge(st_ready.sem, st_ready.at(i, c))
                mm(bank[6][0:NS, 0:INNER], XT[:, c, INNER:KX], XW[:, c % 2, :], start=True, stop=True).then_inc(state_mm.sem, 1)

            def outputs(c):
                pe.wait_ge(xd_ready.sem, xd_ready.at(i, c + 1))
                if c:
                    pe.wait_ge(o_used.sem, o_used.at(i, c))
                for h in range(NH1):
                    if h % HB == 0:
                        pe.wait_ge(p_ready.sem, p_ready.at(i, 2 * c + 1 + h // HB))
                    last = mm(bank[4][:, DH1 * h:DH1 * h + DH1],
                              PB[:, (2 * c + h // HB) % 4, (h % HB) * L:(h % HB + 1) * L],
                              XD[:, c % 2, DH1 * h:DH1 * h + DH1], start=True, stop=True)
                last.then_inc(o_mm.sem, 1)

            def inter(c):
                pe.wait_ge(st_ready.sem, st_ready.at(i, c))
                if c >= 2:
                    pe.wait_ge(inter_used.sem, inter_used.at(i, c - 1))
                mm(bank[5][:, 0:INNER], CS[:, chunk(c)], ST[:, :], start=True, stop=True).then_inc(inter_mm.sem, 1)

            def by_channel(c):
                pe.wait_ge(yn_ready.sem, yn_ready.at(i, c + 1))
                if front and c == 0:
                    pe.wait_ge(ht_evac.sem, ht_evac.at(k, 4))
                elif c < 3:
                    pe.wait_ge(xt_evac.sem, xt_evac.at(i, c + 6))
                else:
                    pe.wait_ge(gT_evac.sem, gT_evac.at(i, c))
                for g in range(G3):
                    last = nc.tensor.transpose(bank[7][:, g * L:(g + 1) * L], YT[:, c, 128 * g:128 * g + 128], ident)
                last.then_inc(gT_mm.sem, 1)

            def output(n):
                pe.wait_ge(gT_evac.sem, gT_evac.at(i, 4 * n + 4))
                if n == 0:
                    pe.wait_ge(p_ready.sem, p_ready.at(i, 2 * NCH))
                    pe.wait_ge(x_exp.sem, x_exp.at(i, 2 * NCH))
                for m in range(2):
                    for c in range(G3):
                        last = mm(bank[2 * n + m][0:CH, :], Wout[:, c, m * CH:(m + 1) * CH], GC[:, c, span(n)],
                                  start=(c == 0), stop=(c == 2))
                    last.then_inc(out_mm.sem, 1)

            tokens(0)
            scores(0)
            tokens(1)
            for c in range(NCH):
                if c + 1 < NCH:
                    scores(c + 1)
                if c == 1 and front:
                    pe.wait_ge(gn_sum.sem, gn_sum.at(k, 1))
                if c >= 1:
                    inter(c)
                if c < NCH - 1:
                    state(c)
                if c + 2 < NCH:
                    tokens(c + 2)
                outputs(c)
                if c < 4 and front:
                    by_token(k, c)
                if c >= 3:
                    by_channel(c - 3)
            by_channel(5)
            output(0)
            by_channel(6)
            by_channel(7)
            output(1)

        def last_back(p):
            average(p, "mean", RS2, ln2["sum"])
            average(p, "var", SQ2[:, 0, :], ln2["sqsum"])
            pe.wait_ge(xx_ready.sem, xx_ready.at(p, 4))
            ffn1(p, 0)
            ffn2(p, 0, 0)
            ffn2(p, 1, 0)

        over_images(pe, None, body, lambda k: body(k, False), first=3)
        last_back(B - 1)

    @block_ctx.scalar
    def _(act):
        A = nc.scalar.activation
        A(R[:, 0, 0:1], rows("A_log")[0:NH1, :], ACT.Exp).then_inc(own_a.sem, own_a.step())
        act.wait_ge(own_a.sem, own_a.value())
        A(rows("A_log")[0:NH1, :], R[:, 0, 0:1], ACT.Copy, scale=-1.0).then_inc(setup.sem, 1)
        act.wait_ge(bn_step.sem, 3)

        def squares(i, src, dst):
            for n in range(NT):
                act.wait_ge(ln2["d"].sem, ln2["d"].at(i, n + 1))
                if n == 0:
                    if later(i):
                        act.wait_ge(stored.sem, stored.at(i - 1, 1))
                A(dst[:, :, span(n)], src[:, :, span(n)], ACT.Square).then_inc(ln2["sq"].sem, 1)

        def deviations(i, dst):
            for n in range(NT):
                act.wait_ge(ln2["var"].sem, ln2["var"].at(i, n + 1))
                A(dst[:, span(n)], bank[6 + n][0:CH, :], ACT.Ln, bias=eps[0:CH, 0:1]).then_inc(ln2["ln"].sem, 1)
            for n in range(NT):
                act.wait_ge(ln2["ln"].sem, ln2["ln"].at(i, n + 1))
                A(dst[:, span(n)], dst[:, span(n)], ACT.Exp, scale=-0.5).then_inc(ln2["rs"].sem, 1)

        def affine(i, buf, w, b):
            for n in range(NT):
                act.wait_ge(ln2["hn"].sem, ln2["hn"].at(i, n + 1))
                for c in range(2):
                    A(buf[:, c, span(n)], buf[:, c, span(n)], ACT.Identity,
                        bias=w96(b, c), scale=w96(w, c)).then_inc(ln2["h"].sem, 1)

        def inner(p, taken):
            for w in range(6):
                m, n = w // 2, w % 2
                act.wait_ge(f1_mm.sem, f1_mm.at(p, w + 1))
                A(F[:, m, span(n)], bank[(taken + w) % 4][:, :], ACT.Gelu, bias=w128("ffn_b1", m)).then_inc(f1_evac.sem, 1)

        def by_token(k, q):
            act.wait_ge(ht_mm.sem, ht_mm.at(k, q + 1))
            A(HT[:, q // 2, 2 * (q % 2):2 * (q % 2) + 2, :], bank[7][:, 0:2 * C]
              .rearrange("p (c n) -> p c n", c=2), ACT.Copy).then_inc(ht_evac.sem, 1)

        def body(k, front=True):
            i, p = k - 1, k - 2
            if front:
                act.wait_ge(y_loaded.sem, y_loaded.at(k, 1))
                for c in range(2):
                    A(Y0[:, c, :], Y0[:, c, :], ACT.Identity, bias=bns[:, c, 5:6], scale=bns[:, c, 4:5]).then_inc(y_scaled.sem, 1)
            if not has_main(k):
                for q in range(4):
                    by_token(k, q)
                return
            own_a.start(i)
            if not has_back(k):
                act.wait_ge(setup.sem, n_setup)

            def projected(first, last_one):
                for pos in range(first, last_one):
                    w = in_order[pos]
                    act.wait_ge(in_mm.sem, in_mm.at(i, pos + 1))
                    b = bank[in_bank[pos]]
                    if w < 8:
                        A(XBC[:, w // 2, PAD + (w % 2) * 512:PAD + (w % 2 + 1) * 512], b[:, :], ACT.Copy).then_inc(in_evac.sem, 1)
                    elif w < 10:
                        A(R[:, 0, span(w % 2)], b[0:NH1, :], ACT.Identity, bias=rows("dt_bias")[0:NH1, :]).then_inc(in_evac.sem, 1)
                    else:
                        A(ZT[:, w - 10, :], b[:, 0:INNER], ACT.Silu).then_inc(in_evac.sem, 1)

            def cast(part):
                q = slice(32 * part, 32 * part + NH1)
                if part:
                    act.wait_ge(part_left.sem, part_left.at(i, part))
                else:
                    act.wait_ge(cu_ready.sem, cu_ready.at(i, 1))
                A(CU3[q, :], CU[q, :], ACT.Copy).then_inc(part_cast.sem, 1)

            if later(i):
                act.wait_ge(o_mm.sem, o_mm.at(i - 1, NCH))
            act.wait_ge(x1_ready.sem, x1_ready.at(i, 1))
            projected(0, 4)
            if has_back(k):
                squares(p, H2, SQ2)
            projected(4, 6)
            act.wait_ge(in_evac.sem, in_evac.at(i, 2))
            A(R[:, 1, :], R[:, 0, :], ACT.Abs).then_inc(own_a.sem, own_a.step())
            projected(6, 7)
            act.wait_ge(own_a.sem, own_a.value())
            A(R[:, 1, :], R[:, 1, :], ACT.Exp, scale=-1.0).then_inc(own_a.sem, own_a.step())
            projected(7, 8)
            act.wait_ge(own_a.sem, own_a.value())
            A(R[:, 1, :], R[:, 1, :], ACT.Ln, bias=1.0).then_inc(row_sp.sem, 1)
            projected(8, 10)
            cast(0)
            if has_back(k):
                deviations(p, RS2)
            projected(10, 13)
            cast(1)
            projected(13, 14)
            if has_back(k):
                affine(p, H2, "norm2_w", "norm2_b")
            projected(14, 18)
            cast(2)
            act.wait_ge(conv_done.sem, conv_done.at(i, 1))
            A(BS[:, :], CV[0:NS, 3, :], ACT.Silu).then_inc(xs_ready.sem, 1)
            A(CS[:, :], CV[NS:2 * NS, 3, :], ACT.Silu).then_inc(xs_ready.sem, 1)
            for g in range(2):
                act.wait_ge(conv_done.sem, conv_done.at(i, g + 2))
                A(CV[:, g, :], CV[:, g, :], ACT.Silu).then_inc(xs_ready.sem, 1)
            if has_back(k):
                inner(p, 18)
            act.wait_ge(conv_done.sem, conv_done.at(i, 4))
            A(CV[:, 2, :], CV[:, 2, :], ACT.Silu).then_inc(xs_ready.sem, 1)
            act.wait_ge(xg_ready.sem, xg_ready.at(i, 2))
            for c in range(2):
                A(XF[:, c, :], XG[:, c, :], ACT.Copy).then_inc(xf_copied.sem, 1)
            A(GWD[64:64 + NH1, :], R[:, 0, :], ACT.Copy).then_inc(g_ready.sem, 1)
            A(GWD[0:NH1, :], CU[0:NH1, :], ACT.Exp).then_inc(g_ready.sem, 1)
            act.wait_ge(row_w.sem, row_w.at(i, 1))
            A(R[:, 1, :], R[:, 1, :], ACT.Exp).then_inc(row_we.sem, 1)

            def tokens(c):
                act.wait_ge(xt_mm.sem, xt_mm.at(i, c + 1))
                A(XT[:, c, :], bank[7][:, 0:KX], ACT.Copy).then_inc(xt_evac.sem, 1)

            def exps(c):
                for r in range(2):
                    j = 2 * c + r
                    act.wait_ge(e_mm.sem, e_mm.at(i, j + 1))
                    if j >= 2:
                        act.wait_ge(p_ready.sem, p_ready.at(i, j - 1))
                    else:
                        act.wait_ge(w_ready.sem, w_ready.at(i, 1))
                    A(XB[:, r, :], bank[2 + r][:, 0:HB * L], ACT.Exp).then_inc(x_exp.sem, 1)

            def square_sum(c):
                act.wait_ge(y_gated.sem, y_gated.at(i, c + 1))
                if c:
                    act.wait_ge(ss_ready.sem, ss_ready.at(i, c))
                A(JK[:, :], YT[:, c, :], ACT.Square, accum_out=SS[:, c:c + 1]).then_inc(ss_ready.sem, 1)

            def channels(c):
                act.wait_ge(gT_mm.sem, gT_mm.at(i, c + 1))
                A(GC[:, :, chunk(c)], bank[7][:, 0:INNER].rearrange("p (g t) -> p g t", g=G3), ACT.Copy).then_inc(gT_evac.sem, 1)

            tokens(0)
            exps(0)
            tokens(1)
            for c in range(NCH):
                if c + 1 < NCH:
                    exps(c + 1)
                if c + 2 < NCH:
                    tokens(c + 2)
                if c >= 1:
                    square_sum(c - 1)
                if c < 4 and front:
                    by_token(k, c)
                if c >= 3:
                    channels(c - 3)
            square_sum(NCH - 1)
            for c in range(NCH - 3, NCH):
                channels(c)

        def last_back(p):
            squares(p, H2, SQ2)
            deviations(p, RS2)
            affine(p, H2, "norm2_w", "norm2_b")
            inner(p, 0)

        over_images(act, None, body, lambda k: body(k, False), first=3)
        last_back(B - 1)

    @block_ctx.vector
    def _(dve):
        V = nc.vector
        for c in range(2):
            V.bn_aggr(bns[:, c, 0:2], bn[:, c, :]).then_inc(own_v.sem, own_v.step())
        dve.wait_ge(own_v.sem, own_v.value())
        V.tensor_scalar(bns[:, :, 2], bns[:, :, 1], GN_EPS, None, ALU.add).then_inc(bn_step.sem, 1)
        dve.wait_ge(bn_step.sem, 2)
        V.tensor_tensor(bns[:, :, 4], bns[:, :, 3], shared["w96_pair"]("bn_g"), ALU.mult).then_inc(own_v.sem, own_v.step())
        dve.wait_ge(own_v.sem, own_v.value())
        V.tensor_tensor(bns[:, :, 3], bns[:, :, 0], bns[:, :, 4], ALU.mult).then_inc(own_v.sem, own_v.step())
        dve.wait_ge(own_v.sem, own_v.value())
        V.tensor_tensor(bns[:, :, 5], shared["w96_pair"]("bn_b"), bns[:, :, 3], ALU.subtract).then_inc(bn_step.sem, 1)

        def prepare():
            dve.wait_ge(loaded.sem, 5 * 16)
            for g in range(G3):
                V.tensor_scalar(Wout[:, g, :], Wout[:, g, :], w128("ssm_w", g), None, ALU.mult).then_inc(setup.sem, 1)
            V.tensor_copy(identb[:, :], ident).then_inc(setup.sem, 1)
            V.tensor_copy(maskb[:, :, :], cst("causal").unsqueeze(1).broadcast_to([128, HB, L])).then_inc(setup.sem, 1)
            V.tensor_copy(a_sel[:, :, :], sel[:, 0:NH1 * L].rearrange("p (g n) -> p g n", g=2)).then_inc(setup.sem, 1)
            V.tensor_copy(b_sel[:, :, :], sel[:, NH1 * L:].rearrange("p (g n) -> p g n", g=NH1)).then_inc(setup.sem, 1)
            dve.wait_ge(setup.sem, n_setup)

        def deviate(i, src, dst):
            for n in range(NT):
                dve.wait_ge(ln2["mean"].sem, ln2["mean"].at(i, n + 1))
                V.tensor_tensor(dst[:, :, span(n)], src[:, :, span(n)],
                                  bank[4 + n][0:CH, :].unsqueeze(1).broadcast_to([CH, 2, 512]),
                                  ALU.subtract).then_inc(ln2["d"].sem, 1)

        def sum_squares(p):
            for n in range(NT):
                dve.wait_ge(ln2["sq"].sem, ln2["sq"].at(p, n + 1))
                V.tensor_tensor(SQ2[:, 0, span(n)], SQ2[:, 0, span(n)], SQ2[:, 1, span(n)], ALU.add).then_inc(ln2["sqsum"].sem, 1)

        def scale(i, buf, rs):
            for n in range(NT):
                dve.wait_ge(ln2["rs"].sem, ln2["rs"].at(i, n + 1))
                V.tensor_tensor(buf[:, :, span(n)], buf[:, :, span(n)],
                                  rs[:, span(n)].unsqueeze(1).broadcast_to([CH, 2, 512]), ALU.mult).then_inc(ln2["hn"].sem, 1)

        def group_stats(k):
            dve.wait_ge(x1_ready.sem, x1_ready.at(k, 1))
            for c in range(2):
                for n in range(NT):
                    V.bn_stats(gst[:, c, 6 * n:6 * n + 6], X1[:, c, span(n)]).then_inc(own_f.sem, own_f.step())
            dve.wait_ge(own_f.sem, own_f.value())
            V.memset(gs[:, 0, 3:4], 0.0).then_inc(own_f.sem, own_f.step())
            V.bn_aggr(gs[:, 0, 0:2], gst[:, 0, :]).then_inc(own_f.sem, own_f.step())
            V.bn_aggr(gs[:, 1, 0:2], gst[:, 1, :]).then_inc(gn_stats.sem, 1)

        def group_deviation(k):
            dve.wait_ge(gn_mean.sem, gn_mean.at(k, 1))
            V.tensor_copy(gs[:, :, 6:8], bank[5][0:CH, 0:4].rearrange("p (c s) -> p c s", c=2)).then_inc(own_f.sem, own_f.step())
            dve.wait_ge(own_f.sem, own_f.value())
            V.tensor_tensor(gs[:, :, 2], gs[:, :, 0], gs[:, :, 6], ALU.subtract).then_inc(own_f.sem, own_f.step())
            dve.wait_ge(own_f.sem, own_f.value())
            V.tensor_tensor(gs[:, :, 2], gs[:, :, 2], gs[:, :, 2], ALU.mult).then_inc(gn_dev.sem, 1)

        def group_variance(k):
            dve.wait_ge(gn_var.sem, gn_var.at(k, 1))
            V.scalar_tensor_tensor(gs[:, :, 3], bank[5][0:CH, 8:10], GN_EPS, gs[:, :, 7],
                                   ALU.add, ALU.add).then_inc(gn_sum.sem, 1)

        def group_norm(k):
            dve.wait_ge(gn_rstd.sem, gn_rstd.at(k, 1))
            if later(k):
                dve.wait_ge(xf_copied.sem, xf_copied.at(k - 1, 2))
                dve.wait_ge(xs_added.sem, xs_added.at(k - 1, 1))
            for c in range(2):
                V.tensor_scalar(XG[:, c, :], X1[:, c, :], gs[:, c, 6:7], gs[:, c, 5:6],
                                ALU.subtract, ALU.mult).then_inc(xg_ready.sem, 1)

        def token_stats(k, q):
            dve.wait_ge(ht_evac.sem, ht_evac.at(k, q + 1))
            for c in (2 * q, 2 * q + 1):
                V.bn_stats(hst[:, c, :], ht(c)).then_inc(own_f.sem, own_f.step())

        def token_moments(k, q):
            dve.wait_ge(own_f.sem, own_f.value())
            V.memset(hmv[:, 2 * q, 3:4], 0.0).then_inc(own_f.sem, own_f.step())
            for c in (2 * q, 2 * q + 1):
                V.bn_aggr(hmv[:, c, 0:2], hst[:, c, :]).then_inc(own_f.sem, own_f.step())

        def token_center(k, q):
            if not has_main(k):
                dve.wait_ge(n1_loaded.sem, 16)
            dve.wait_ge(own_f.sem, own_f.value())
            for c in (2 * q, 2 * q + 1):
                V.scalar_tensor_tensor(ht(c), ht(c), hmv[:, c, 0:1], n1[:, 0, :],
                                       ALU.subtract, ALU.mult).then_inc(own_f.sem, own_f.step())
            if q == 3:
                V.tensor_scalar(hmv[:, :, 2], hmv[:, :, 1], GN_EPS, None, ALU.add).then_inc(hv_ready.sem, 1)

        def token_norm(k, g):
            dve.wait_ge(own_f.sem, own_f.value())
            dve.wait_ge(hr_ready.sem, hr_ready.at(k, 1))
            for c in range(4 * g, 4 * g + 4):
                V.scalar_tensor_tensor(ht(c), ht(c), hmv[:, c, 3:4], n1[:, 1, :],
                                       ALU.mult, ALU.add).then_inc(ht_ready.sem, 1)

        def finish(p, taken):
            dve.wait_ge(xx_moved.sem, xx_moved.at(p, 1))
            for w in range(4):
                m, n = w // 2, w % 2
                dve.wait_ge(f2_mm.sem, f2_mm.at(p, w + 1))
                V.tensor_tensor(OUT[:, m, span(n)], bank[(taken + 6 + w) % 4][0:CH, :], OUT[:, m, span(n)], ALU.add).then_inc(out_ready.sem, 1)

        def body(k, front=True):
            i, p = k - 1, k - 2
            if front:
                own_f.start(k)
                dve.wait_ge(y_scaled.sem, y_scaled.at(k, 2))
                V.scalar_tensor_tensor(Y0[:, :, :], Y0[:, :, :], 0.01, Y0[:, :, :], ALU.mult, ALU.max).then_inc(y_leaky.sem, 1)
            if not has_main(k):
                group_stats(k)
                group_deviation(k)
                group_variance(k)
                group_norm(k)
                for q in range(4):
                    token_stats(k, q)
                for q in range(4):
                    token_moments(k, q)
                for q in range(4):
                    token_center(k, q)
                for g in range(2):
                    token_norm(k, g)
                return
            if not has_back(k):
                prepare()
            own_v.start(i)
            if has_back(k):
                deviate(p, XF, H2)

            def convolve(g):
                at = (3, 0, 1, 2).index(g)
                dve.wait_ge(in_evac.sem, in_evac.at(i, 2 * at + 4))
                if at == 0:
                    if later(i):
                        dve.wait_ge(xt_mm.sem, xt_mm.at(i - 1, NCH))
                V.tensor_scalar(CV[:, g, :], XBC[:, g, 0:T], w128("m_conv_w", 4 * g), w128("m_conv_b", g),
                                ALU.mult, ALU.add).then_inc(own_v.sem, own_v.step())
                for t in range(1, TAPS):
                    dve.wait_ge(own_v.sem, own_v.value())
                    ins = V.scalar_tensor_tensor(
                        CV[:, g, :], XBC[:, g, t:t + T], w128("m_conv_w", 4 * g + t), CV[:, g, :], ALU.mult, ALU.add)
                    if t == TAPS - 1:
                        ins.then_inc(conv_done.sem, 1)
                    else:
                        ins.then_inc(own_v.sem, own_v.step())

            def split(part):
                a, b = slice(32 * part, 32 * part + NH1), slice(32 * part + 32, 32 * part + 32 + NH1)
                dve.wait_ge(part_cast.sem, part_cast.at(i, part + 1))
                V.tensor_tensor(CU[b, :], CU[a, :], CU3[a, :], ALU.subtract).then_inc(part_left.sem, 1)

            convolve(3)
            if has_back(k):
                sum_squares(p)
            dve.wait_ge(row_sp.sem, row_sp.at(i, 1))
            V.scalar_tensor_tensor(R[:, 0, :], R[:, 0, :], 0.0, R[:, 1, :], ALU.max, ALU.add).then_inc(own_v.sem, own_v.step())
            dve.wait_ge(own_v.sem, own_v.value())
            V.tensor_scalar(R[:, 1, :], R[:, 0, :], rows("A_log")[0:NH1, :], None, ALU.mult).then_inc(own_v.sem, own_v.step())
            dve.wait_ge(own_v.sem, own_v.value())
            V.tensor_tensor_scan(CU[0:NH1, :], reset, R[:, 1, :], 0.0, ALU.mult, ALU.add).then_inc(cu_ready.sem, 1)
            dve.wait_ge(cu_ready.sem, cu_ready.at(i, 1))
            by_chunk = lambda ap: ap.rearrange("p (c l) -> p c l", l=L)
            V.scalar_tensor_tensor(by_chunk(R[:, 1, :]), by_chunk(CU[0:NH1, :]), -1.0,
                                   CU[0:NH1, L - 1::L].unsqueeze(2).broadcast_to([NH1, NCH, L]),
                                   ALU.mult, ALU.add).then_inc(row_w.sem, 1)
            convolve(0)
            split(0)
            if has_back(k):
                scale(p, H2, RS2)
            split(1)
            convolve(1)
            convolve(2)
            if front:
                group_stats(k)
                group_deviation(k)
            dve.wait_ge(g_ready.sem, g_ready.at(i, 2))
            V.tensor_tensor(DG[:, :, :], GWD[0:NH1, L - 1::L].unsqueeze(2).broadcast_to([NH1, NCH, NH1]),
                            ident[0:NH1, 0:NH1].unsqueeze(1).broadcast_to([NH1, NCH, NH1]), ALU.mult).then_inc(dg_ready.sem, 1)
            dve.wait_ge(row_we.sem, row_we.at(i, 1))
            V.tensor_tensor(GWD[32:32 + NH1, :], R[:, 1, :], R[:, 0, :], ALU.mult).then_inc(w_ready.sem, 1)
            if has_back(k):
                finish(p, 18)
            if front:
                group_variance(k)
            dve.wait_ge(gw_mm.sem, gw_mm.at(i, 2))
            V.tensor_copy(GT[:, :, :], bank[6][:, 0:18 * NCH].rearrange("p (c n) -> p c n", c=NCH)).then_inc(gt_ready.sem, 1)
            V.tensor_copy(DEC[:, :, :], bank[6][0:NS, 256:256 + NH1 * NCH].rearrange("p (c n) -> p c n", c=NCH)).then_inc(gt_ready.sem, 1)

            def weigh(c):
                for r in range(2):
                    j = 2 * c + r
                    dve.wait_ge(x_exp.sem, x_exp.at(i, j + 1))
                    if j >= 4:
                        dve.wait_ge(o_mm.sem, o_mm.at(i, c - 1))
                    V.tensor_tensor(PB[:, j % 4, :].rearrange("p (h t) -> p h t", t=L),
                                    XB[:, r, :].rearrange("p (h t) -> p h t", t=L),
                                    bank[c % 2][:, 0:L].unsqueeze(1).broadcast_to([128, HB, L]), ALU.mult).then_inc(p_ready.sem, 1)

            def state(c):
                dve.wait_ge(state_mm.sem, state_mm.at(i, c + 1))
                if c == 0:
                    if later(i):
                        dve.wait_ge(inter_mm.sem, inter_mm.at(i - 1, NCH - 1))
                    V.tensor_copy(ST[:, :], bank[6][0:NS, 0:INNER]).then_inc(st_ready.sem, 1)
                    return
                dve.wait_ge(inter_mm.sem, inter_mm.at(i, c))
                dve.wait_ge(st_ready.sem, st_ready.at(i, c))
                V.tensor_tensor(heads(ST[:, :]), heads(ST[:, :]),
                                DEC[:, c, :].unsqueeze(2).broadcast_to([NS, NH1, DH1]), ALU.mult).then_inc(own_v.sem, own_v.step())
                dve.wait_ge(own_v.sem, own_v.value())
                V.tensor_tensor(ST[:, :], ST[:, :], bank[6][0:NS, 0:INNER], ALU.add).then_inc(st_ready.sem, 1)

            def reach(c):
                dve.wait_ge(o_used.sem, o_used.at(i, c))
                dve.wait_ge(inter_mm.sem, inter_mm.at(i, c))
                V.tensor_tensor(heads(TI[:, :]), heads(bank[5][:, 0:INNER]),
                                GT[:, c, 0:6].unsqueeze(2).broadcast_to([128, NH1, DH1]), ALU.mult).then_inc(inter_used.sem, 1)

            def total(c):
                dve.wait_ge(o_mm.sem, o_mm.at(i, c + 1))
                if c == 0:
                    dve.wait_ge(xu_ready.sem, xu_ready.at(i, 1))
                    V.tensor_tensor(YT[:, c, :], bank[4][:, 0:INNER], XT[:, c, 0:INNER], ALU.add).then_inc(o_used.sem, 1)
                    return
                dve.wait_ge(inter_used.sem, inter_used.at(i, c))
                V.tensor_tensor(YT[:, c, :], bank[4][:, 0:INNER], TI[:, :], ALU.add).then_inc(o_used.sem, 1)
                dve.wait_ge(o_used.sem, o_used.at(i, c + 1))
                dve.wait_ge(xu_ready.sem, xu_ready.at(i, c + 1))
                if c < NCH - 1:
                    V.tensor_tensor(YT[:, c, :], YT[:, c, :], XT[:, c, 0:INNER], ALU.add).then_inc(y_summed.sem, 1)
                    return
                V.tensor_tensor(YT[:, c, :], YT[:, c, :], XT[:, c, 0:INNER], ALU.add).then_inc(own_v.sem, own_v.step())
                dve.wait_ge(own_v.sem, own_v.value())
                V.tensor_tensor(YT[:, c, :], YT[:, c, :], ZT[:, c, :], ALU.mult).then_inc(y_gated.sem, 1)

            def mean_square(c):
                dve.wait_ge(ss_ready.sem, ss_ready.at(i, c + 1))
                V.tensor_scalar(SS[:, c:c + 1], SS[:, c:c + 1], 1.0 / INNER, 1e-5, ALU.mult, ALU.add).then_inc(ms_ready.sem, 1)

            def normalise(c):
                dve.wait_ge(rr_ready.sem, rr_ready.at(i, c + 1))
                V.tensor_scalar(YT[:, c, :], YT[:, c, :], RR[:, c:c + 1], None, ALU.mult).then_inc(yn_ready.sem, 1)

            weigh(0)
            if front:
                group_norm(k)
            for c in range(NCH):
                if c:
                    reach(c)
                if c < NCH - 1:
                    state(c)
                if c + 1 < NCH:
                    weigh(c + 1)
                if c >= 2:
                    normalise(c - 2)
                if front:
                    if 1 <= c <= 4:
                        token_stats(k, c - 1)
                    if 2 <= c <= 5:
                        token_moments(k, c - 2)
                    if 3 <= c <= 5:
                        token_center(k, c - 3)
                    if c == 5:
                        token_center(k, 3)
                total(c)
                if c >= 1:
                    mean_square(c - 1)
                if front and c == 7:
                    token_norm(k, 0)
                    token_norm(k, 1)
            mean_square(NCH - 1)
            normalise(NCH - 2)
            normalise(NCH - 1)
            dve.wait_ge(xf_copied.sem, xf_copied.at(i, 2))
            dve.wait_ge(xs_added.sem, xs_added.at(i, 1))
            for w in range(4):
                n, m = w // 2, w % 2
                dve.wait_ge(out_mm.sem, out_mm.at(i, w + 1))
                V.tensor_tensor(XF[:, m, span(n)], bank[w][0:CH, :], XF[:, m, span(n)], ALU.add).then_inc(xf_ready.sem, 1)
                V.tensor_tensor(XX[:, m, span(n)], bank[w][0:CH, :], XX[:, m, span(n)], ALU.add).then_inc(xx_ready.sem, 1)
                if m == 1:
                    dve.wait_ge(gT_mm.sem, gT_mm.at(i, NCH))
                    dve.wait_ge(xf_ready.sem, xf_ready.at(i, w + 1))
                    V.tensor_tensor(RS2[:, span(n)], XF[:, 0, span(n)], XF[:, 1, span(n)], ALU.add).then_inc(ln2["sum"].sem, 1)

        def last_back(p):
            deviate(p, XF, H2)
            sum_squares(p)
            scale(p, H2, RS2)
            finish(p, 0)

        over_images(dve, None, body, lambda k: body(k, False), first=3)
        last_back(B - 1)


def program(nc, d, out):
    with ExitStack() as ctx:
        def sb(name, shape, dt=F32):
            return ctx.enter_context(nc.sbuf_tensor(name, shape, dt))

        bank = [ctx.enter_context(nc.psum_tensor(f"bank{n}", [128, 512], F32)) for n in range(8)]
        w96, w128, rows, consts = (sb("col96", [CH, W96]), sb("col128", [128, W128]), sb("rows_sb", [12, 4]),
                                   sb("consts_sb", [128, WC]))
        shared = {
            "bank": bank, "consts": consts, "eps": sb("eps", [128, 2]), "bn": sb("bn", [CH, 2, B * 12]),
            "w96_sb": w96, "w128_sb": w128, "rows_sb": rows, "n_setup0": 21,
            "setup_done": Signal(ctx.enter_context(nc.semaphore("setup_done")), 0),
            "w96": lambda n, c: w96[:, AT96[n][0] + c:AT96[n][0] + c + 1],
            "w96_pair": lambda n: w96[:, AT96[n][0]:AT96[n][1]],
            "w128": lambda n, c, k=1: w128[:, AT128[n][0] + c:AT128[n][0] + c + k],
            "rows": lambda n: rows[:, ROWS.index(n):ROWS.index(n) + 1],
            "cst": lambda n: consts[:, ATC[n][0]:ATC[n][1]],
        }
        d["yc"] = nc.dram_tensor("yc", (B, CH, 2 * T), F32, kind=d.get("yc_kind", "Internal")).ap()
        d["u"] = nc.dram_tensor("u", (B, C * T), F32, kind="Internal").ap()
        with ExitStack() as ctx0:
            layer0(nc, ctx0, d, shared)
        if "yc_kind" not in d:
            with ExitStack() as ctx1:
                layer1(nc, ctx1, d, shared, out)


def constants():
    import numpy as np

    c = {n: np.zeros((128, w), np.float32) for n, w in (CONSTS | SELECT).items()}
    c["ident"][:] = np.eye(128)
    s, t = np.arange(128)[:, None], np.arange(L)[None, :]
    c["causal"][:] = np.where(s <= t, 0.0, -1e30)
    v = c["block"].reshape(128, HG, V0)
    for h in range(HG):
        v[DH0 * h:DH0 * h + DH0, h] = 1.0
    size = C // 32
    for p in range(CH):
        c["group"][p, p // size * size:p // size * size + size] = 1.0 / size
    c["mean"][:CH] = 1.0 / C
    e = c["expand"].reshape(128, G3, 128)
    a0, b0 = c["a_sel0"].reshape(128, G3, HG, L), c["b_sel0"].reshape(128, NH0, 128)
    for h in range(NH0):
        e[h, h // HG, DH0 * (h % HG):DH0 * (h % HG) + DH0] = 1.0
        for part in range(3):
            a0[32 * part + h, h // HG, h % HG] = 1.0
            b0[32 * part + h, h] = 1.0
    a1, b1 = c["a_sel1"].reshape(128, NH1, L), c["b_sel1"].reshape(128, NH1, 128)
    for h in range(NH1):
        for part in range(3):
            c["pick1"][32 * part + h, NH1 * part + h] = 1.0
            a1[32 * part + h, h] = -1.0
            b1[32 * part + h, h] = 1.0
    c["reset"][:] = 1.0
    c["reset"][:, ::L] = 0.0
    return np.concatenate([c[n] for n in CONSTS], 1), np.concatenate([c[n] for n in SELECT], 1)


def laid_out(q):
    import numpy as np

    a = {k: np.asarray(v) for k, v in q.items()}
    f = np.float32
    L0, L1 = (lambda n: a["L0_conv_" + n]), (lambda n: a["L1_conv_" + n])
    col = lambda v, p: v.reshape(-1, p).T
    src96 = {"ln_w": L0("ln_w"), "ln_b": L0("ln_b"), "b_lin": L0("b_lin"), "b_down": L0("b_down"),
             "conv2_b": L0("conv2_b"), "bn_g": L0("bn_g"), "bn_b": L0("bn_b"), "norm1_w": L1("norm1_w"),
             "norm1_b": L1("norm1_b"), "norm2_w": L1("norm2_w"), "norm2_b": L1("norm2_b"), "ffn_b2": L1("ffn_b2")}
    taps = lambda v: v.reshape(-1, 128, TAPS).transpose(1, 0, 2).reshape(128, -1)
    src128 = {"b_up": col(L0("b_up"), 128), "conv_k": taps(L0("conv_k")), "conv_b": col(L0("conv_b"), 128),
              "skip": col(L0("skip"), 128), "mh_w": col(L0("mh_w"), 128), "mh_b": col(L0("mh_b"), 128),
              "m_conv_w": taps(L1("conv_w")), "m_conv_b": col(L1("conv_b"), 128), "ssm_w": col(L1("ssm_norm_w"), 128),
              "ffn_b1": col(L1("ffn_b1"), 128), "D": np.broadcast_to(L1("D_skip")[None, :], (128, NH1))}
    rows = np.zeros((12, 4), f)
    rows[:, 0], rows[:, 1] = L0("b_i"), L0("b_f")
    rows[:NH1, 2], rows[:NH1, 3] = L1("dt_bias"), L1("A_log")
    gate = np.zeros((3 * INNER, 44), f)
    gate[:, 0:12], gate[:, 32:44] = L0("w_i"), L0("w_f")
    w3 = L0("conv2_w").transpose(1, 2, 3, 0).reshape(C, 9, C)
    conv = np.zeros((128, 15, C), f)
    conv[0:96, 0:9], conv[96:128, 0:9] = w3[0:96], w3[160:192]
    for r in range(3):
        conv[0:64, 9 + 2 * r], conv[64:128, 9 + 2 * r] = w3[96:160, 3 * r], w3[96:160, 3 * r + 1]
        conv[0:64, 10 + 2 * r] = w3[96:160, 3 * r + 2]
    return {
        "x": a["x"], "w_up": L0("w_up"), "w_q": L0("w_q"), "w_k": L0("w_k"),
        "w_qk_t": np.concatenate([L0("w_q").T, L0("w_k").T]), "w_gate": gate, "w_down": L0("w_down"),
        "w_lin": L0("w_lin"), "w_c3": conv,
        "w_in": L1("in_proj_w").T, "w_out": L1("out_proj_w").T, "w_f1": L1("ffn_w1").T, "w_f2": L1("ffn_w2").T,
        "col96": np.concatenate([col(src96[n], CH) for n in COL96], 1),
        "col128": np.concatenate([src128[n] for n in COL128], 1), "rows": rows,
        "norm1": np.broadcast_to(np.concatenate([L1("norm1_w"), L1("norm1_b")])[None, :], (128, 2 * C)),
        "consts": constants()[0], "select": constants()[1],
    }


def kernel(**inputs):
    import concourse.bacc as _bacc
    import numpy as _np
    from concourse import mybir as _mybir
    from concourse.bass_utils import run_bass_kernel_spmd as _run

    nc = _bacc.Bacc("TRN2", target_bir_lowering=False, num_devices=1)
    arrays, d = {}, {}
    for name, a in laid_out(inputs).items():
        a = _np.ascontiguousarray(a)
        arrays[f"in_{name}"] = a
        d[name] = nc.dram_tensor(f"in_{name}", a.shape, _mybir.dt.from_np(a.dtype), kind="ExternalInput").ap()
    out = nc.dram_tensor("out_0", inputs["x"].shape, _mybir.dt.float32, kind="ExternalOutput").ap()
    program(nc, d, out)
    r = _run(nc, [arrays], core_ids=[0])
    return r.results[0]["out_0"]
```
